# Optimizing a Trainium2 kernel written in Bass

```python
import numpy as np
import jax
import jax.numpy as jnp

def _softmax(x, axis=-1):
    return jax.nn.softmax(x, axis=axis)

def _gelu(x):
    return jax.nn.gelu(x, approximate=True)

def _silu(x):
    return jax.nn.silu(x)

def _sigmoid(x):
    return jax.nn.sigmoid(x)

def _layernorm(x, axis=-1, eps=1e-05):
    m = jnp.mean(x, axis=axis, keepdims=True)
    v = jnp.var(x, axis=axis, keepdims=True)
    return (x - m) / jnp.sqrt(v + eps)

def _scatter_add(tgt, idx, src, axis=0):
    return tgt.at[idx].add(src)

def _segment_sum(src, seg, n):
    return jax.ops.segment_sum(src, seg, n)
kernel_name = 'mk_flamingo_gated_d1_seqx_r4_6940cc'

def setup_inputs(seed: int=0):
    np.random.seed(seed)
    _w = jnp.asarray

    def _rec_inputs():
        import jax
        import jax.numpy as jnp
        _rk = jax.random.key(seed)
        x = -0.0002928 + 1 * jax.random.normal(jax.random.fold_in(_rk, 1), (64, 128, 256), jnp.float32)
        _lenS = 128 - jax.random.randint(jax.random.fold_in(_rk, 7), (64,), 0, max(1, 128 // 4) + 1, jnp.int32)
        _lenS2 = 128 - jax.random.randint(jax.random.fold_in(_rk, 8), (64,), 0, max(1, 128 // 4) + 1, jnp.int32)
        _ctx_1024P = jax.random.normal(jax.random.fold_in(_rk, 11), (64, 16, 256), jnp.float32)
        _ctx_1024c = jax.random.dirichlet(jax.random.fold_in(_rk, 511), 0.3 * jnp.ones((16,), jnp.float32), (64, 128))
        _ctx_1024t = jnp.einsum('bsk,bkd->bsd', _ctx_1024c, _ctx_1024P)
        _ctx_1024t = _ctx_1024t * jax.lax.rsqrt(jnp.mean(jnp.square(_ctx_1024t)) + 1e-12) * 0.953939
        ctx_1024 = -1.39393e-06 + 0.999914 * (_ctx_1024t + 0.3 * jax.random.normal(jax.random.fold_in(_rk, 611), (64, 128, 256), jnp.float32))
        _validS = jnp.arange(128)[None, :] < _lenS[:, None]
        _validS2 = jnp.arange(128)[None, :] < _lenS2[:, None]
        _causal = jnp.tril(jnp.ones((128, 128), dtype=bool))
        mask_BxS2_ik0 = jnp.where(jnp.broadcast_to(_validS2[:, :], (64, 128)), 0, 1).astype(jnp.int32)
        _g = jax.random.normal(jax.random.fold_in(_rk, 9001), (2, 1), jnp.float32)
        _g = jnp.sign(_g) * jnp.maximum(jnp.abs(_g), 1.0) + (_g == 0) * 1.0
        g_xattn = _g[0]
        g_ffn = _g[1]
        return (x, ctx_1024, mask_BxS2_ik0, g_xattn, g_ffn)
    x, ctx_1024, mask_BxS2_ik0, g_xattn, g_ffn = _rec_inputs()

    def _L0_xattn_setup():
        import jax, jax.numpy as jnp
        import numpy as np
        NUM_HEADS = 16
        key = jax.random.key(seed)
        ks = jax.random.split(key, 10)
        B, S, D = (2, 512, 256)
        q = jax.random.normal(ks[0], (B, S, D), dtype=jnp.float32)
        k = jax.random.normal(ks[1], (B, S, D), dtype=jnp.float32)
        v = jax.random.normal(ks[2], (B, S, D), dtype=jnp.float32)
        mask = jax.random.randint(ks[3], (B, S), 0, 2, dtype=jnp.int32)
        scale = 0.02
        Wq = jax.random.normal(ks[4], (D, D), dtype=jnp.float32) * scale
        bq = jax.random.normal(ks[5], (D,), dtype=jnp.float32) * scale
        Wk = jax.random.normal(ks[6], (D, D), dtype=jnp.float32) * scale
        bk = jax.random.normal(ks[7], (D,), dtype=jnp.float32) * scale
        Wv = jax.random.normal(ks[8], (D, D), dtype=jnp.float32) * scale
        bv = jax.random.normal(ks[9], (D,), dtype=jnp.float32) * scale
        return {'q': q, 'k': k, 'v': v, 'mask': mask, 'Wq': Wq, 'bq': bq, 'Wk': Wk, 'bk': bk, 'Wv': Wv, 'bv': bv}
    _L0_xattn_all = _L0_xattn_setup()
    _L0_xattn_in = {k: v for k, v in _L0_xattn_all.items() if k in ('Wq', 'bq', 'Wk', 'bk', 'Wv', 'bv')}
    del _L0_xattn_all

    def _L0_ffn_setup():
        import jax, jax.numpy as jnp
        import numpy as np
        B, T, C, H, E = (4, 512, 256, 512, 8)
        CAPACITY_FACTOR = 1.0
        key = jax.random.key(seed)
        ks = jax.random.split(key, 5)
        scale = 0.02
        return {'x': jax.random.normal(ks[0], (B, T, C), dtype=jnp.float32), 'Wg': jax.random.normal(ks[1], (E, C), dtype=jnp.float32) * scale, 'W1': jax.random.normal(ks[2], (E, H, C), dtype=jnp.float32) * scale, 'W2': jax.random.normal(ks[3], (E, C, H), dtype=jnp.float32) * scale, 'W3': jax.random.normal(ks[4], (E, H, C), dtype=jnp.float32) * scale}
    _L0_ffn_all = _L0_ffn_setup()
    _L0_ffn_in = {k: v for k, v in _L0_ffn_all.items() if k in ('Wg', 'W1', 'W2', 'W3')}
    del _L0_ffn_all
    return {'x': x, 'ctx_1024': ctx_1024, 'mask_BxS2_ik0': mask_BxS2_ik0, 'g_xattn': g_xattn, 'g_ffn': g_ffn, 'L0_xattn_Wq': _L0_xattn_in['Wq'], 'L0_xattn_bq': _L0_xattn_in['bq'], 'L0_xattn_Wk': _L0_xattn_in['Wk'], 'L0_xattn_bk': _L0_xattn_in['bk'], 'L0_xattn_Wv': _L0_xattn_in['Wv'], 'L0_xattn_bv': _L0_xattn_in['bv'], 'L0_ffn_Wg': _L0_ffn_in['Wg'], 'L0_ffn_W1': _L0_ffn_in['W1'], 'L0_ffn_W2': _L0_ffn_in['W2'], 'L0_ffn_W3': _L0_ffn_in['W3']}

def reference(x, ctx_1024, mask_BxS2_ik0, g_xattn, g_ffn, L0_xattn_Wq, L0_xattn_bq, L0_xattn_Wk, L0_xattn_bk, L0_xattn_Wv, L0_xattn_bv, L0_ffn_Wg, L0_ffn_W1, L0_ffn_W2, L0_ffn_W3):
    import jax
    import jax.numpy as jnp

    def _L0_xattn_ref(q, k, v, mask, Wq, bq, Wk, bk, Wv, bv):
        import jax, jax.numpy as jnp
        import numpy as np
        NUM_HEADS = 16
        B, S, D = q.shape
        H = NUM_HEADS
        dh = D // H
        Qh = (q @ Wq + bq).reshape(B, S, H, dh)
        Kh = (k @ Wk + bk).reshape(B, S, H, dh)
        Vh = (v @ Wv + bv).reshape(B, S, H, dh)
        scores = jnp.einsum('bqhd,bkhd->bhqk', Qh, Kh) / jnp.sqrt(jnp.float32(10.0))
        scores = jnp.where(mask[:, None, None, :] == 0, jnp.float32(-1000000000.0), scores)
        probs = jax.nn.softmax(scores, axis=-1)
        out = jnp.einsum('bhqk,bkhd->bqhd', probs, Vh).reshape(B, S, D)
        return out

    def _L0_ffn_ref(x, Wg, W1, W2, W3):
        import jax, jax.numpy as jnp
        import numpy as np
        B, T, C, H, E = (4, 512, 256, 512, 8)
        CAPACITY_FACTOR = 1.0
        b, t, c = x.shape
        e = Wg.shape[0]
        n = b * t
        capacity = max(1, int(CAPACITY_FACTOR * n / e))
        x_flat = x.reshape(n, c)
        scores = (x_flat @ Wg.T).T
        top_vals, token_idx = jax.lax.top_k(scores, capacity)
        token_w = jax.nn.softmax(top_vals, axis=-1)
        xg = x_flat[token_idx]
        h = jax.nn.silu(jnp.einsum('eic,ehc->eih', xg, W1)) * jnp.einsum('eic,ehc->eih', xg, W3)
        y = jnp.einsum('eih,ech->eic', h, W2) * token_w[..., None]
        out = jnp.zeros_like(x_flat).at[token_idx.reshape(-1)].add(y.reshape(-1, c))
        return out.reshape(b, t, c)
    x = x + jnp.tanh(g_xattn[0]) * _L0_xattn_ref(_layernorm(x, axis=-1), ctx_1024, ctx_1024, mask_BxS2_ik0, L0_xattn_Wq, L0_xattn_bq, L0_xattn_Wk, L0_xattn_bk, L0_xattn_Wv, L0_xattn_bv)
    x = x + jnp.tanh(g_ffn[0]) * _L0_ffn_ref(_layernorm(x, axis=-1), L0_ffn_Wg, L0_ffn_W1, L0_ffn_W2, L0_ffn_W3)
    return x

_drawn_inputs = setup_inputs


def setup_inputs(seed=0):
    import zlib

    import numpy as np

    out = dict(_drawn_inputs(seed))
    spreads = {}
    factors = {'L0_xattn_Wq': 6.76,
     'L0_xattn_bq': 8.0,
     'L0_xattn_Wk': 6.787,
     'L0_xattn_bk': 8.0,
     'L0_xattn_bv': 3.638,
     'L0_ffn_Wg': 8.0,
     'L0_ffn_W1': 8.0,
     'L0_ffn_W2': 8.0,
     'L0_ffn_W3': 8.0}
    for name, (base, spread) in spreads.items():
        noise = np.random.default_rng([zlib.crc32(name.encode()), seed]).standard_normal(out[name].shape)
        drawn = base * np.exp(spread * noise) if base else spread * noise
        out[name] = jnp.asarray(drawn.astype(out[name].dtype))
    for name, factor in factors.items():
        out[name] = (out[name] * factor).astype(out[name].dtype)
    return out
```

```python
from contextlib import ExitStack

import numpy as np

import concourse.bass as bass
from concourse import mybir

F32 = mybir.dt.float32
BF16 = mybir.dt.bfloat16
FP16 = mybir.dt.float16
I32 = mybir.dt.int32
U32 = mybir.dt.uint32
ALU = mybir.AluOpType
ACT = mybir.ActivationFunctionType
AX_X = mybir.AxisListType.X

P = 128
D = 256
HEADS = 16
DH = 16
GB = 4
GT = GB * P
KD = D // P
VW = 32
EPS = 1e-5
MASKED = float(2 ** 30)
SCALE = 1.0 / float(np.sqrt(np.float32(10.0)))
E = 8
F = 512
ROW = D + E
HI, MID, LO = range(3)
Q_ROWS = [HI, HI, HI, MID, MID, LO]
K_ROWS = [HI, MID, LO, HI, MID, HI]
SPLIT = len(Q_ROWS) * DH
MASK_ROW, MAX_ROW = SPLIT, SPLIT + 1
A_K, B_K = SPLIT + 1, SPLIT + 3
MAGIC = 1597463007.0
Q_SENT, K_SENT = 16 * 6, 16 * 7
LN1_OPS, LN2_OPS = 16, 9


class Batch:

    def __init__(self, k, s, total):
        self.k, self.s, self.total = k + s // 8, s % 8, total

    def back(self, n):
        return Batch(self.k, self.s - n, self.total)

    @property
    def ok(self):
        return not isinstance(self.k, int) or 0 <= 8 * self.k + self.s < self.total

    def times(self, n, more=0):
        return self.k * (8 * n) + (self.s * n + more)

    def turn(self, ring, n, more=0):
        return self.k * (8 // ring * n) + (self.s // ring * n + more)

    @property
    def tok(self):
        return self.k * (8 * P) + self.s * P

    @property
    def j(self):
        return self.s % GB

    @property
    def group(self):
        return Group(self.k, self.s // GB, self.total // GB)


class Group:

    def __init__(self, k, p, total):
        self.k, self.p, self.total = k + p // 2, p % 2, total

    def on(self, n):
        return Group(self.k, self.p + n, self.total)

    @property
    def ok(self):
        return not isinstance(self.k, int) or 0 <= 2 * self.k + self.p < self.total

    def times(self, n, more=0):
        return self.k * (2 * n) + (self.p * n + more)

    def turn(self, n, more=0):
        return self.k * n + more

    @property
    def tok(self):
        return self.k * (2 * GT) + self.p * GT


def wait(eng, sem, value):
    if not isinstance(value, int) or value > 0:
        eng.wait_ge(sem, value)


class Chain:

    def __init__(self, eng, sem, base=0, passed=None):
        self.eng, self.sem, self.base, self.n, self.passed = eng, sem, base, 0, passed

    def link(self, ins):
        ins.then_inc(self.sem, 1)
        self.n += 1
        self.eng.wait_ge(self.sem, self.base + self.n)
        if self.passed is not None and not isinstance(self.base, int):
            self.eng.sem_inc(self.passed, 1)


def attention(nc, ctx, w, x, ctx_t, mask, g_x, wq, bq, wk, bk, wv, bv, wg_t, out, rows, scores_t,
              mask_bias):
    n_tok = x.shape[0]
    NB = n_tok // P
    NG = NB // GB

    def sb(name, shape, dt=F32):
        return ctx.enter_context(nc.sbuf_tensor(name, shape, dt))

    def sem(name):
        return ctx.enter_context(nc.semaphore(name))

    def bank(name, dt=F32):
        return ctx.enter_context(nc.psum_tensor(name, [P, 512], dt))

    ident, passed = w["ident"], w["passed"]
    wq_sb, wk_sb, wv_sb = sb("wq_sb", [P, KD, D]), sb("wk_sb", [P, KD, D]), sb("wv_sb", [P, KD, D])
    wg_sb = sb("wg_sb", [P, KD, E])
    bq_sb, bk_sb = sb("bq_sb", [P, KD]), sb("bk_sb", [P, KD])
    bv_sb = sb("bv_sb", [P, D])
    gx_raw, gx = sb("gx_raw", [P, 1]), sb("gx", [P, 1])
    mask_nat = sb("mask_nat", [NB, P], I32)
    bias_nat = sb("bias_nat", [NB, P], BF16)
    x_in = [sb(f"x_in{p}", [P, GB, D]) for p in range(2)]
    c_t = [sb(f"c_t{p}", [P, KD, GT]) for p in range(2)]
    mask_b = [sb(f"mask_b{p}", [P, GT], I32) for p in range(2)]
    stats1, mv1 = sb("stats1", [P, GB, 6]), sb("mv1", [P, GB, 2])
    v1, y1, t1, nm1 = sb("v1", [P, GB]), sb("y1", [P, GB]), sb("t1", [P, GB]), sb("nm1", [P, GB])
    xn, xn_t = sb("xn", [P, GB, D]), sb("xn_t", [P, KD, GT])
    q_rest, k_val, k_rest = sb("q_rest", [P, KD, GT]), sb("k_val", [P, KD, GT]), sb("k_rest", [P, KD, GT])
    q_part, k_part = sb("q_part", [P, 3, KD, GT], BF16), sb("k_part", [P, 3, KD, GT], BF16)
    q_st = [sb(f"q_st{p}", [P, HEADS, GT], BF16) for p in range(2)]
    k_st = [sb(f"k_st{p}", [P, HEADS, GT], BF16) for p in range(2)]
    v_aug = [sb(f"v_aug{p}", [P, GB, HEADS, VW]) for p in range(2)]
    m_sb = [sb(f"m_sb{i}", [P, HEADS]) for i in range(2)]
    neg_m = [sb(f"neg_m{i}", [HEADS, 2, P], BF16) for i in range(2)]
    p_t = [sb(f"p_t{i}", [P, HEADS, P]) for i in range(2)]
    o_t = [sb(f"o_t{i}", [P, 4, P]) for i in range(2)]
    x_res = [sb(f"x_res{i}", [P, D]) for i in range(2)]
    rden, o_n = sb("rden", [P, HEADS]), sb("o_n", [P, D])
    x2 = [sb(f"x2_{i}", [P, D]) for i in range(4)]
    stats2 = sb("stats2", [P, 6])
    mv2 = [sb(f"mv2_{i}", [P, 2]) for i in range(2)]
    v2, h2, y2, t2 = sb("v2", [P, 1]), sb("h2", [P, 1]), [sb(f"y2_{i}", [P, 1]) for i in range(2)], sb("t2", [P, 1])
    row = [sb(f"row{i}", [P, ROW]) for i in range(4)]
    xn2_t = sb("xn2_t", [P, KD, P])
    s_t = [sb(f"s_t{i}", [E, P]) for i in range(2)]

    a_ps = [bank(f"a_ps{i}") for i in range(2)]
    b_ps = [bank(f"b_ps{i}") for i in range(2)]
    pv_ps = bank("pv_ps")
    f_ps = [bank(f"f_ps{i}") for i in range(2)]
    o_ps = bank("o_ps")

    s_const, s_ones, s_bias, s_bias_st, s_gx = sem("s_const"), sem("s_ones"), sem("s_bias"), sem("s_bias_st"), sem("s_gx")
    s_x = [sem(f"s_x{p}") for p in range(2)]
    s_c = [sem(f"s_c{p}") for p in range(2)]
    s_mv1, s_ln1, s_xn = sem("s_mv1"), sem("s_ln1"), sem("s_xn")
    s_st1 = sem("s_st1")
    f_done = sem("f_done")
    f_free = [sem(f"f_free{i}") for i in range(2)]
    q_hi, q_mid, q_lo = sem("q_hi"), sem("q_mid"), sem("q_lo")
    k_hi, k_r, k_mid, k_lo = sem("k_hi"), sem("k_r"), sem("k_mid"), sem("k_lo")
    s_q = [sem(f"s_q{p}") for p in range(2)]
    s_k = [sem(f"s_k{p}") for p in range(2)]
    a_done, max_done = sem("a_done"), sem("max_done")
    mt_done, nhi_done, nmid_done = sem("mt_done"), sem("nhi_done"), sem("nmid_done")
    s_m = [sem(f"s_m{i}") for i in range(2)]
    b_done, exp_done, pv_done, pv_out = sem("b_done"), sem("exp_done"), sem("pv_done"), sem("pv_out")
    ot_done, rd_done, ot_out, x2_done, st2_done, mv2_done, ln2 = (
        sem("ot_done"), sem("rd_done"), sem("ot_out"), sem("x2_done"), sem("st2_done"), sem("mv2_done"), sem("ln2"))
    xn2_done, xt2_done, xt2_out = sem("xn2_done"), sem("xt2_done"), sem("xt2_out")
    r_done, r_out, st_done, st_out = sem("r_done"), sem("r_out"), sem("st_done"), sem("st_out")
    s_res = [sem(f"s_res{i}") for i in range(2)]
    s_out = [sem(f"s_out{i}") for i in range(4)]
    s_row = [sem(f"s_row{i}") for i in range(4)]
    s_sc = [sem(f"s_sc{i}") for i in range(2)]

    def steps(eng, step):
        for g in range(2):
            for j in range(GB):
                step(eng, Batch(g // 2, 4 * (g % 2) + j, NB))
        with eng.Fori(1, NG // 2 - 1, 1) as k:
            for s in range(2 * GB):
                step(eng, Batch(k, s, NB))
        for g in range(NG - 2, NG + 2):
            for j in range(GB):
                step(eng, Batch(g // 2, 4 * (g % 2) + j, NB))

    ORDER = [("r", 7, r_out), ("st", 7, st_out), ("mt", 1, nmid_done), ("ot", 4, ot_out), ("xt", 6, xt2_out)]

    def bank_free(eng, b, what):
        i = [n for n, _, _ in ORDER].index(what)
        for back in range(1, 2 * len(ORDER)):
            n = (i - back) % len(ORDER)
            earlier = 0 if i - back >= 0 else 1 if i - back >= -len(ORDER) else 2
            _, lag, done = ORDER[n]
            use = b.back(lag + earlier)
            if use.ok:
                wait(eng, done, use.times(1, 1))
                return

    with nc.Block() as block:

        @block.sync
        def _(sp):
            n = 0
            for dst, src in ((wq_sb, wq), (wk_sb, wk), (wv_sb, wv), (wg_sb, wg_t)):
                sp.dma_start(dst[:], src.rearrange("(k p) n -> p k n", p=P)).then_inc(s_const, 16)
            for dst, src in ((bq_sb, bq), (bk_sb, bk)):
                sp.dma_start(dst[:], src).then_inc(s_const, 16)
            sp.dma_start(bv_sb[:], bv.rearrange("(a n) -> a n", a=1).to_broadcast([P, D])).then_inc(s_const, 16)
            sp.dma_start(gx_raw[:], g_x.rearrange("(a n) -> a n", a=1).to_broadcast([P, 1])).then_inc(s_const, 16)
            sp.dma_start(mask_nat[:], mask).then_inc(s_const, 16)

            def load_x(g):
                if g.ok:
                    wait(sp, s_xn, g.times(4, -4))
                    sp.sem_inc(passed, 1)
                    sp.dma_start(x_in[g.p][:], x[bass.ds(g.tok, GT), :].rearrange("(t p) d -> p t d", p=P)).then_inc(s_x[g.p], 16)

            def load_c(g):
                if g.ok:
                    wait(sp, f_done, g.times(8, -8))
                    sp.sem_inc(passed, 1)
                    wait(sp, f_free[1], g.times(4, -5))
                    sp.sem_inc(passed, 1)
                    sp.dma_start(c_t[g.p][:], ctx_t[:, bass.ds(g.tok, GT)].rearrange("(k p) t -> p k t", p=P)).then_inc(s_c[g.p], 16)
                    sp.dma_start(mask_b[g.p][:], mask.rearrange("b (a s) -> a (b s)", a=1)[:, bass.ds(g.tok, GT)].to_broadcast([P, GT])).then_inc(s_c[g.p], 16)

            def stack_q(g):
                if not g.ok:
                    return
                wait(sp, b_done, g.times(16, -16))
                for part, ready in ((HI, q_hi), (MID, q_mid), (LO, q_lo)):
                    sp.wait_ge(ready, g.times(2, 2))
                    for r, have in enumerate(Q_ROWS):
                        if have == part:
                            sp.dma_start(q_st[g.p][r * DH:(r + 1) * DH, :, :], q_part[:, part, :, :]).then_inc(s_q[g.p], 16)

            def stack_k(g):
                if not g.ok:
                    return
                wait(sp, b_done, g.times(16, -16))
                sp.sem_inc(passed, 1)
                sp.dma_start(k_st[g.p][MASK_ROW:MASK_ROW + 1, :, :],
                             mask_bias[0:1, bass.ds(g.tok, GT)].unsqueeze(1).to_broadcast([1, HEADS, GT])).then_inc(s_k[g.p], 16)
                for part, ready in ((HI, k_hi), (MID, k_mid), (LO, k_lo)):
                    sp.wait_ge(ready, g.times(2, 2))
                    for r, have in enumerate(K_ROWS):
                        if have == part:
                            sp.dma_start(k_st[g.p][r * DH:(r + 1) * DH, :, :], k_part[:, part, :, :]).then_inc(s_k[g.p], 16)

            def residual(b):
                if b.ok:
                    wait(sp, x2_done, b.times(1, -1))
                    sp.sem_inc(passed, 1)
                    sp.dma_start(x_res[b.s % 2][:], x[bass.ds(b.tok, P), :]).then_inc(s_res[b.s % 2], 16)

            def max_rows(b):
                if b.ok:
                    sp.wait_ge(nmid_done, b.times(1, 1))
                    for i in range(2):
                        r = MAX_ROW + i
                        sp.dma_start(q_st[b.group.p][r:r + 1, :, b.j * P:(b.j + 1) * P], neg_m[b.s % 2][:, i, :]).then_inc(s_m[b.s % 2], 16)

            def store_x2(b):
                if b.ok:
                    sp.wait_ge(x2_done, b.times(1, 1))
                    sp.sem_inc(passed, 1)
                    sp.dma_start(out[bass.ds(b.tok, P), :], x2[b.s % 4][:]).then_inc(s_out[b.s % 4], 16)

            def store_row(b):
                if b.ok:
                    sp.wait_ge(r_out, b.times(1, 1))
                    sp.sem_inc(passed, 1)
                    sp.dma_start(scores_t[:, bass.ds(b.tok, P)], s_t[b.s % 2][:]).then_inc(s_sc[b.s % 2], 16)
                    sp.wait_ge(st_out, b.times(1, 1))
                    sp.sem_inc(passed, 1)
                    sp.dma_start(rows[bass.ds(b.tok, P), :], row[b.s % 4][:]).then_inc(s_row[b.s % 4], 16)

            load_x(Group(0, 0, NG))
            load_x(Group(0, 1, NG))
            load_c(Group(0, 0, NG))
            load_c(Group(0, 1, NG))
            sp.wait_ge(s_bias, 1)
            sp.dma_start(mask_bias.rearrange("a (b s) -> (a b) s", s=P), bias_nat[:]).then_inc(s_bias_st, 16)
            sp.wait_ge(s_bias_st, 16)
            sp.wait_ge(s_ones, 6)
            stack_q(Group(0, 0, NG))
            stack_k(Group(0, 0, NG))

            def step(sp, b):
                g = b.group
                residual(b.back(3))
                if b.j == 0:
                    load_x(g.on(2))
                    load_c(g.on(2))
                store_x2(b.back(5))
                store_row(b.back(7))
                if b.j == 2:
                    stack_q(g.on(1))
                if b.j == 3:
                    stack_k(g.on(1))
                max_rows(b.back(1))

            steps(sp, step)
            for i in range(4):
                sp.wait_ge(s_out[i], 16 * (NB // 4))
                sp.wait_ge(s_row[i], 16 * (NB // 4))
            for i in range(2):
                sp.wait_ge(s_sc[i], 16 * (NB // 2))

        @block.gpsimd
        def _(pool):
            pool.memset(ident[:], 0.0).then_inc(w["s_id"], 1)
            pool.wait_ge(w["s_id"], 1)
            pool.affine_select(out=ident[:], in_=ident[:], compare_op=ALU.not_equal, fill=1.0, base=0,
                               pattern=[[-1, P]], channel_multiplier=1).then_inc(w["s_id"], 1)

            def ln1(g):
                if not g.ok:
                    return
                pool.wait_ge(s_mv1, g.times(4, 4))
                wait(pool, s_xn, g.times(4))
                pool.sem_inc(passed, 1)
                c = Chain(pool, s_ln1, g.times(LN1_OPS), passed)
                var, mean = mv1[:, :, 1], mv1[:, :, 0]
                c.link(pool.tensor_scalar(v1[:], var, EPS, None, ALU.add))
                c.link(pool.tensor_scalar(y1[:].bitcast(I32), v1[:].bitcast(I32), -0.5, MAGIC, ALU.mult, ALU.add))
                for _ in range(3):
                    c.link(pool.tensor_tensor(t1[:], y1[:], y1[:], ALU.mult))
                    c.link(pool.tensor_tensor(t1[:], t1[:], v1[:], ALU.mult))
                    c.link(pool.tensor_scalar(t1[:], t1[:], -0.5, 1.5, ALU.mult, ALU.add))
                    c.link(pool.tensor_tensor(y1[:], y1[:], t1[:], ALU.mult))
                c.link(pool.tensor_tensor(t1[:], mean, y1[:], ALU.mult))
                c.link(pool.tensor_scalar(nm1[:], t1[:], -1.0, None, ALU.mult))
                assert c.n == LN1_OPS

            def ln2_rstd(b):
                if not b.ok:
                    return
                pool.wait_ge(mv2_done, b.times(1, 1))
                wait(pool, xn2_done, b.times(1, -1))
                pool.sem_inc(passed, 1)
                c = Chain(pool, ln2, b.times(LN2_OPS), passed)
                y, var = y2[b.s % 2], mv2[b.s % 2][:, 1:2]
                c.link(pool.tensor_scalar(v2[:], var, EPS, None, ALU.add))
                c.link(pool.tensor_scalar(h2[:], v2[:], -0.5, None, ALU.mult))
                c.link(pool.tensor_scalar(y[:].bitcast(I32), v2[:].bitcast(I32), -0.5, MAGIC, ALU.mult, ALU.add))
                for _ in range(3):
                    c.link(pool.tensor_scalar(t2[:], y[:], y[:, 0:1], h2[:, 0:1], ALU.mult, ALU.mult))
                    c.link(pool.tensor_scalar(y[:], t2[:], 1.5, y[:, 0:1], ALU.add, ALU.mult))
                assert c.n == LN2_OPS

            def split_q(g, m):
                if g.ok:
                    pool.wait_ge(q_mid, g.times(2, m + 1))
                    pool.tensor_tensor(q_part[:, LO, m, :], q_rest[:, m, :], q_part[:, MID, m, :], ALU.subtract).then_inc(q_lo, 1)

            def rest_k(g, m):
                if g.ok:
                    pool.wait_ge(k_hi, g.times(2, m + 1))
                    pool.tensor_tensor(k_rest[:, m, :], k_val[:, m, :], k_part[:, HI, m, :], ALU.subtract).then_inc(k_r, 1)

            def split_k(g, m):
                if g.ok:
                    pool.wait_ge(k_mid, g.times(2, m + 1))
                    pool.tensor_tensor(k_part[:, LO, m, :], k_rest[:, m, :], k_part[:, MID, m, :], ALU.subtract).then_inc(k_lo, 1)

            ln1(Group(0, 0, NG))
            g = Group(0, 0, NG)
            for m in range(KD):
                split_q(g, m)
            for m in range(KD):
                rest_k(g, m)
                split_k(g, m)
            ln1(Group(0, 1, NG))

            def step(pool, b):
                g = b.group
                for m in range(KD):
                    if b.j == 1:
                        split_q(g.on(1), m)
                    if b.j == 2:
                        rest_k(g.on(1), m)
                        split_k(g.on(1), m)
                ln2_rstd(b.back(4))
                if b.j == 1:
                    ln1(g.on(2))

            steps(pool, step)

        @block.scalar
        def _(act):
            def f_wait(g, u):
                act.wait_ge(f_done, g.times(8, u + 1))

            def xn_t_out(g, k):
                if g.ok:
                    f_wait(g, k)
                    act.activation(xn_t[:, k, :], f_ps[k][:], ACT.Copy).then_inc(f_free[k], 1)

            def hi_q(g, m):
                if g.ok:
                    f_wait(g, 2 + m)
                    if m == 0:
                        last = g.on(-1)
                        wait(act, s_q[last.p], last.turn(Q_SENT, Q_SENT))
                    act.activation(q_part[:, HI, m, :], f_ps[m][:], ACT.Identity, bias=bq_sb[:, m:m + 1]).then_inc(q_hi, 1)

            def mid_q(g, m):
                if g.ok:
                    act.wait_ge(f_free[m], g.times(4, 2))
                    act.activation(q_part[:, MID, m, :], q_rest[:, m, :], ACT.Copy).then_inc(q_mid, 1)

            def hi_k(g, m):
                if g.ok:
                    act.wait_ge(f_free[m], g.times(4, 3))
                    if m == 0:
                        last = g.on(-1)
                        wait(act, s_k[last.p], last.turn(K_SENT, K_SENT))
                    act.activation(k_part[:, HI, m, :], k_val[:, m, :], ACT.Copy).then_inc(k_hi, 1)

            def mid_k(g, m):
                if g.ok:
                    act.wait_ge(k_r, g.times(2, m + 1))
                    act.activation(k_part[:, MID, m, :], k_rest[:, m, :], ACT.Copy).then_inc(k_mid, 1)

            def normalise(g, ts):
                if g.ok:
                    act.wait_ge(s_ln1, g.times(LN1_OPS, LN1_OPS))
                    wait(act, f_done, g.times(8, -6))
                    act.wait_ge(s_x[g.p], g.turn(16, 16))
                    for t in ts:
                        act.activation(xn[:, t, :], x_in[g.p][:, t, :], ACT.Identity, bias=nm1[:, t:t + 1],
                                       scale=y1[:, t:t + 1]).then_inc(s_xn, 1)

            def exp(b, q):
                if b.ok:
                    act.wait_ge(b_done, b.times(4, q + 1))
                    if q == 0:
                        wait(act, pv_done, b.times(1, -1))
                    act.activation(p_t[b.s % 2][:, 4 * q:4 * q + 4, :], b_ps[q % 2][:].rearrange("p (h s) -> p h s", s=P),
                                   ACT.Exp, scale=SCALE).then_inc(exp_done, 1)

            def neg_hi(b):
                if b.ok:
                    act.wait_ge(mt_done, b.times(1, 1))
                    wait(act, s_m[b.s % 2], b.turn(2, 32))
                    act.activation(neg_m[b.s % 2][:, 0, :], o_ps[0:HEADS, 0:P], ACT.Copy, scale=-1.0).then_inc(nhi_done, 1)

            def pv_copy(b):
                if b.ok:
                    act.wait_ge(pv_done, b.times(1, 1))
                    wait(act, ot_done, b.times(1, -1))
                    act.activation(o_t[b.s % 2][:], pv_ps[:].rearrange("p (a s) -> p a s", s=P), ACT.Copy).then_inc(pv_out, 1)

            def xt2_copy(b):
                if b.ok:
                    act.wait_ge(xt2_done, b.times(1, 1))
                    wait(act, r_done, b.times(1))
                    act.activation(xn2_t[:], o_ps[:, 0:D].rearrange("p (k s) -> p k s", s=P), ACT.Copy).then_inc(xt2_out, 1)

            act.wait_ge(s_const, 16 * 9)
            act.activation(gx[:], gx_raw[:], ACT.Tanh).then_inc(s_gx, 1)
            g = Group(0, 0, NG)
            normalise(g, range(GB))
            for k in range(KD):
                xn_t_out(g, k)
            for m in range(KD):
                hi_q(g, m)
                mid_q(g, m)
            for m in range(KD):
                hi_k(g, m)
                mid_k(g, m)
            normalise(Group(0, 1, NG), range(GB))

            def step(act, b):
                f = b.group.on(1)
                xt2_copy(b.back(7))
                exp(b.back(2), 0)
                if b.j == 0:
                    xn_t_out(f, 0)
                if b.j == 1:
                    hi_q(f, 0)
                if b.j == 2:
                    hi_k(f, 0)
                exp(b.back(2), 1)
                if b.j == 1:
                    mid_q(f, 0)
                if b.j == 2:
                    mid_k(f, 0)
                if b.j == 3:
                    normalise(b.group.on(2), (0, 1))
                exp(b.back(2), 2)
                neg_hi(b.back(1))
                if b.j == 0:
                    xn_t_out(f, 1)
                if b.j == 1:
                    hi_q(f, 1)
                if b.j == 2:
                    hi_k(f, 1)
                exp(b.back(2), 3)
                if b.j == 1:
                    mid_q(f, 1)
                if b.j == 2:
                    mid_k(f, 1)
                if b.j == 3:
                    normalise(b.group.on(2), (2, 3))
                pv_copy(b.back(3))

            steps(act, step)

        @block.vector
        def _(dve):
            for p in range(2):
                dve.memset(q_st[p][MASK_ROW:MASK_ROW + 1, :, :], 1.0).then_inc(s_ones, 1)
                dve.memset(k_st[p][MASK_ROW:MASK_ROW + 3, :, :], 1.0).then_inc(s_ones, 1)
                dve.memset(v_aug[p][:], 0.0).then_inc(s_ones, 1)
            dve.wait_ge(s_ones, 6)
            for p in range(2):
                dve.memset(v_aug[p][:, :, :, DH:DH + 1], 1.0).then_inc(s_ones, 1)
            dve.wait_ge(s_const, 16 * 9)
            dve.tensor_scalar(bias_nat[:], mask_nat[:], -1.0, MASKED, ALU.add, ALU.mult).then_inc(s_bias, 1)
            dve.wait_ge(s_gx, 1)

            def stats(g, ts):
                if not g.ok:
                    return
                dve.wait_ge(s_x[g.p], g.turn(16, 16))
                wait(dve, s_ln1, g.times(LN1_OPS))
                for t in ts:
                    dve.bn_stats(stats1[:, t, :], x_in[g.p][:, t, :]).then_inc(s_st1, 1)
                dve.wait_ge(s_st1, g.times(4, ts[-1] + 1))
                dve.sem_inc(passed, 1)
                for t in ts:
                    dve.bn_aggr(mv1[:, t, :], stats1[:, t, :]).then_inc(s_mv1, 1)

            def rest_q(g, m):
                if g.ok:
                    dve.wait_ge(q_hi, g.times(2, m + 1))
                    wait(dve, q_lo, g.times(2, m - 1))
                    dve.scalar_tensor_tensor(out=q_rest[:, m, :], in0=f_ps[m][:], scalar=bq_sb[:, m:m + 1],
                                             in1=q_part[:, HI, m, :], op0=ALU.add, op1=ALU.subtract).then_inc(f_free[m], 1)

            def make_k(g, m):
                if g.ok:
                    dve.wait_ge(f_done, g.times(8, 5 + m))
                    dve.wait_ge(s_c[g.p], g.turn(32, 32))
                    wait(dve, k_r, g.times(2, m - 1))
                    dve.scalar_tensor_tensor(out=k_val[:, m, :], in0=f_ps[m][:], scalar=bk_sb[:, m:m + 1],
                                             in1=mask_b[g.p][:], op0=ALU.add, op1=ALU.mult).then_inc(f_free[m], 1)

            def make_v(g, i):
                if g.ok:
                    dve.wait_ge(f_done, g.times(8, 7 + i))
                    if i == 0:
                        wait(dve, pv_done, g.times(4, -4))
                    for t in range(2):
                        ins = dve.tensor_tensor(v_aug[g.p][:, 2 * i + t, :, 0:DH],
                                                f_ps[i][:, t * D:(t + 1) * D].rearrange("p (h d) -> p h d", d=DH),
                                                bv_sb[:].rearrange("p (h d) -> p h d", d=DH), ALU.add)
                    ins.then_inc(f_free[i], 1)

            def maximum(b, q):
                if b.ok:
                    dve.wait_ge(a_done, b.times(4, q + 1))
                    if q == 0:
                        wait(dve, mt_done, b.times(1, -1))
                    dve.tensor_reduce(m_sb[b.s % 2][:, 4 * q:4 * q + 4], a_ps[q % 2][:].rearrange("p (h s) -> p h s", s=P),
                                      AX_X, ALU.max).then_inc(max_done, 1)

            def router_out(b):
                if b.ok:
                    dve.wait_ge(r_done, b.times(1, 1))
                    wait(dve, s_sc[b.s % 2], b.turn(2, 16))
                    wait(dve, st_done, b.times(1, -1))
                    dve.tensor_copy(s_t[b.s % 2][:], o_ps[0:E, 0:P]).then_inc(r_out, 1)

            def row_scores(b):
                if b.ok:
                    dve.wait_ge(st_done, b.times(1, 1))
                    dve.tensor_copy(row[b.s % 4][:, D:ROW], o_ps[:, 0:E]).then_inc(st_out, 1)

            def neg_mid(b):
                if b.ok:
                    dve.wait_ge(nhi_done, b.times(1, 1))
                    dve.scalar_tensor_tensor(out=neg_m[b.s % 2][:, 1, :], in0=o_ps[0:HEADS, 0:P], scalar=-1.0,
                                             in1=neg_m[b.s % 2][:, 0, :], op0=ALU.mult, op1=ALU.subtract).then_inc(nmid_done, 1)

            def finish(b):
                if not b.ok:
                    return
                dve.wait_ge(ot_done, b.times(1, 1))
                o = o_ps[:].rearrange("p (h v) -> p h v", v=VW)
                wait(dve, ot_out, b.times(1))
                dve.reciprocal(rden[:], o[:, :, DH]).then_inc(rd_done, 1)
                dve.wait_ge(rd_done, b.times(1, 1))
                wait(dve, x2_done, b.times(1))
                dve.tensor_tensor(o_n[:].rearrange("p (h d) -> p h d", d=DH), o[:, :, 0:DH],
                                  rden[:].unsqueeze(2).to_broadcast([P, HEADS, DH]), ALU.mult).then_inc(ot_out, 1)
                dve.wait_ge(ot_out, b.times(1, 1))
                dve.wait_ge(s_res[b.s % 2], b.turn(2, 16, 16))
                wait(dve, s_out[b.s % 4], b.turn(4, 16))
                wait(dve, xn2_done, b.times(1, -3))
                dve.scalar_tensor_tensor(out=x2[b.s % 4][:], in0=o_n[:], scalar=gx[:, 0:1], in1=x_res[b.s % 2][:],
                                         op0=ALU.mult, op1=ALU.add).then_inc(x2_done, 1)
                dve.wait_ge(x2_done, b.times(1, 1))
                wait(dve, mv2_done, b.times(1))
                dve.bn_stats(stats2[:], x2[b.s % 4][:]).then_inc(st2_done, 1)
                dve.wait_ge(st2_done, b.times(1, 1))
                wait(dve, xn2_done, b.times(1, -1))
                dve.sem_inc(passed, 1)
                dve.bn_aggr(mv2[b.s % 2][:], stats2[:]).then_inc(mv2_done, 1)

            def normalise2(b):
                if b.ok:
                    dve.wait_ge(ln2, b.times(LN2_OPS, LN2_OPS))
                    wait(dve, s_row[b.s % 4], b.turn(4, 16))
                    wait(dve, xt2_done, b.times(1, -3))
                    dve.tensor_scalar(row[b.s % 4][:, 0:D], x2[b.s % 4][:], mv2[b.s % 2][:, 0:1], y2[b.s % 2][:, 0:1],
                                      ALU.subtract, ALU.mult).then_inc(xn2_done, 1)

            g = Group(0, 0, NG)
            stats(g, range(GB))
            for m in range(KD):
                rest_q(g, m)
            for m in range(KD):
                make_k(g, m)
            for i in range(2):
                make_v(g, i)
            stats(Group(0, 1, NG), range(GB))

            def step(dve, b):
                f = b.group.on(1)
                maximum(b, 0)
                router_out(b.back(7))
                if b.j == 1:
                    rest_q(f, 0)
                if b.j == 2:
                    make_k(f, 0)
                if b.j == 3:
                    make_v(f, 0)
                maximum(b, 1)
                row_scores(b.back(7))
                if b.j == 1:
                    stats(b.group.on(2), range(GB))
                maximum(b, 2)
                normalise2(b.back(5))
                neg_mid(b.back(1))
                if b.j == 1:
                    rest_q(f, 1)
                if b.j == 2:
                    make_k(f, 1)
                if b.j == 3:
                    make_v(f, 1)
                maximum(b, 3)
                finish(b.back(4))

            steps(dve, step)

        @block.tensor
        def _(pe):
            pe.wait_ge(w["s_id"], 2)
            pe.wait_ge(s_const, 16 * 9)
            pe.wait_ge(s_ones, 8)

            def front(g, u):
                if not g.ok:
                    return
                i = u % 2
                ps = f_ps[i]
                wait(pe, f_free[i], g.times(4, u // 2))
                if u < 2:
                    pe.wait_ge(s_xn, g.times(4, 4))
                    for t in range(GB):
                        mm = pe.transpose(ps[:, t * P:(t + 1) * P], xn[:, t, u * P:(u + 1) * P], ident[:])
                elif u < 6:
                    wt, src = (wq_sb, xn_t) if u < 4 else (wk_sb, c_t[g.p])
                    if u < 4:
                        pe.wait_ge(f_free[0], g.times(4, 1))
                        pe.wait_ge(f_free[1], g.times(4, 1))
                    else:
                        pe.wait_ge(s_c[g.p], g.turn(32, 32))
                    for k in range(KD):
                        mm = pe.matmul(ps[:], wt[:, k, i * P:(i + 1) * P], src[:, k, :], start=(k == 0), stop=(k == KD - 1))
                else:
                    for t in range(2):
                        tok = (2 * (u - 6) + t) * P
                        for k in range(KD):
                            mm = pe.matmul(ps[:, t * D:(t + 1) * D], c_t[g.p][:, k, tok:tok + P], wv_sb[:, k, :],
                                           start=(k == 0), stop=(k == KD - 1))
                mm.then_inc(f_done, 1)

            def scores(b, q):
                if not b.ok:
                    return
                g = b.group
                if q == 0 and b.j == 0:
                    pe.wait_ge(s_q[g.p], g.turn(Q_SENT, Q_SENT))
                    pe.wait_ge(s_k[g.p], g.turn(K_SENT, K_SENT))
                wait(pe, max_done, b.times(4, q - 1))
                for i in range(4):
                    h, tok = 4 * q + i, slice(b.j * P, (b.j + 1) * P)
                    mm = pe.matmul(a_ps[q % 2][:, i * P:(i + 1) * P], q_st[g.p][0:A_K, h, tok], k_st[g.p][0:A_K, h, tok],
                                   start=True, stop=True)
                mm.then_inc(a_done, 1)

            def scores_t_(b, q):
                if not b.ok:
                    return
                g = b.group
                if q == 0:
                    pe.wait_ge(s_m[b.s % 2], b.turn(2, 32, 32))
                wait(pe, exp_done, b.times(4, q - 1))
                for i in range(4):
                    h, tok = 4 * q + i, slice(b.j * P, (b.j + 1) * P)
                    mm = pe.matmul(b_ps[q % 2][:, i * P:(i + 1) * P], k_st[g.p][0:B_K, h, tok], q_st[g.p][0:B_K, h, tok],
                                   start=True, stop=True)
                mm.then_inc(b_done, 1)

            def values(b, q):
                if not b.ok:
                    return
                if q == 0:
                    pe.wait_ge(f_free[1], b.group.times(4, 4))
                    pe.wait_ge(f_free[0], b.group.times(4, 4))
                    wait(pe, pv_out, b.times(1))
                pe.wait_ge(exp_done, b.times(4, q + 1))
                for i in range(4):
                    h = 4 * q + i
                    mm = pe.matmul(pv_ps[VW * i:VW * (i + 1), q * P:(q + 1) * P], v_aug[b.group.p][:, b.j, h, :],
                                   p_t[b.s % 2][:, h, :], start=True, stop=True)
                if q == 3:
                    mm.then_inc(pv_done, 1)

            def router(b):
                if b.back(7).ok:
                    use = b.back(7)
                    bank_free(pe, b, "r")
                    pe.wait_ge(xt2_out, use.times(1, 1))
                    for k in range(KD):
                        mm = pe.matmul(o_ps[0:E, 0:P], wg_sb[:, k, :], xn2_t[:, k, :], start=(k == 0), stop=(k == KD - 1))
                    mm.then_inc(r_done, 1)

            def scores_back(b):
                use = b.back(7)
                if use.ok:
                    bank_free(pe, b, "st")
                    pe.wait_ge(r_out, use.times(1, 1))
                    pe.sem_inc(passed, 1)
                    pe.transpose(o_ps[:, 0:E], s_t[use.s % 2][:], ident[0:E, 0:E]).then_inc(st_done, 1)

            def max_t(b):
                use = b.back(1)
                if use.ok:
                    bank_free(pe, b, "mt")
                    pe.wait_ge(max_done, use.times(4, 4))
                    pe.transpose(o_ps[0:HEADS, 0:P], m_sb[use.s % 2][:], ident[:]).then_inc(mt_done, 1)

            def out_back(b):
                use = b.back(4)
                if use.ok:
                    bank_free(pe, b, "ot")
                    pe.wait_ge(pv_out, use.times(1, 1))
                    for a in range(4):
                        mm = pe.transpose(o_ps[:, a * P:(a + 1) * P], o_t[use.s % 2][:, a, :], ident[:])
                    mm.then_inc(ot_done, 1)

            def xn2_back(b):
                use = b.back(6)
                if use.ok:
                    bank_free(pe, b, "xt")
                    pe.wait_ge(xn2_done, use.times(1, 1))
                    for k in range(KD):
                        mm = pe.transpose(o_ps[:, k * P:(k + 1) * P], row[use.s % 4][:, k * P:(k + 1) * P], ident[:])
                    mm.then_inc(xt2_done, 1)

            for u in range(8):
                front(Group(0, 0, NG), u)

            def step(pe, b):
                small = [router, scores_back, max_t, out_back]
                for q in range(4):
                    scores(b, q)
                    small[q](b)
                    scores_t_(b.back(2), q)
                    values(b.back(3), q)
                    if q % 2 == 0:
                        front(b.group.on(1), 2 * b.j + q // 2)
                xn2_back(b)

            steps(pe, step)


CHUNKS = P // E
BISECTIONS = 32
BIG = 1e30


def select(nc, ctx, w, rows, scores_t, thr, idx_all, neg_top):
    n_tok = scores_t.shape[1]
    CAP = n_tok // E
    ST = CAP // P
    T = n_tok // P
    TP = 2 * T
    EP = E // 2

    def sb(name, shape, dt=F32):
        return ctx.enter_context(nc.sbuf_tensor(name, shape, dt))

    def sem(name):
        return ctx.enter_context(nc.semaphore(name))

    def bank(name, dt=F32):
        return ctx.enter_context(nc.psum_tensor(name, [P, 512], dt))

    sc = sb("sc", [P, n_tok // CHUNKS])
    ts = sb("ts", [TP, EP, P])
    same, before, group = sb("same", [P, P]), sb("before", [TP, TP]), sb("group", [TP, TP])
    slot = sb("slot", [P, CAP])
    slot_of = sb("slot_of", [P, ST])
    ones_row, ones = sb("ones_row", [1, P]), sb("ones", [TP, P])
    part_max, bound = sb("part_max", [P, 1]), sb("bound", [P, 1])
    junk = sb("junk", [P, n_tok // CHUNKS])
    lo_hi, t, cnt, u, u2 = sb("lo_hi", [P, 2]), sb("t", [P, 1]), sb("cnt", [P, 1]), sb("u", [P, 1]), sb("u2", [P, 1])
    top = sb("top", [1, E])
    th = sb("th", [TP, EP, 2])
    above, tied, place = sb("above", [TP, EP, P]), sb("tied", [TP, EP, P]), sb("place", [TP, EP, P])
    n_above, left = sb("n_above", [TP, EP]), sb("left", [TP, EP])
    chosen, count = sb("chosen", [TP, EP, P]), sb("count", [TP, EP, P])
    start, end = sb("start", [TP, EP]), sb("end", [TP, EP])
    upto = sb("upto", [TP, EP, P + 1], FP16)
    tile_no = sb("tile_no", [TP, 1])
    under, hot = sb("under", [TP, EP, CAP], FP16), sb("hot", [TP, EP, CAP], FP16)
    cnt_junk = [sb(f"cnt_junk{i}", [P, P]) for i in range(2)]
    pos = sb("pos", [P, E * ST])

    tot_ps, small_ps = bank("tot_ps"), bank("small_ps")
    g_ps = [bank(f"g_ps{i}") for i in range(4)]

    s_sc, s_ts, s_e = sem("s_sc2"), sem("s_ts"), sem("s_e2")
    s_pm, s_bound = sem("s_pm"), sem("s_bound")
    s_top_t, s_top, s_top_b, s_init = sem("s_top_t"), sem("s_top"), sem("s_top_b"), sem("s_init")
    s_count, s_tot, s_thr = sem("s_count"), sem("s_tot"), sem("s_thr")
    s_found, s_thr_st, s_th = sem("s_found"), sem("s_thr_st"), sem("s_th")
    d = sem("d_chain")
    s_tie, s_left, s_sel, s_start, s_hot = sem("s_tie"), sem("s_left"), sem("s_sel"), sem("s_start"), sem("s_hot")
    s_pick, s_pos = sem("s_pick"), sem("s_pos")
    passed = w["passed"]

    with nc.Block() as block:

        @block.sync
        def _(sp):
            sp.dma_start(sc[:], scores_t.rearrange("e (c n) -> (e c) n", c=CHUNKS)).then_inc(s_sc, 16)
            by_tile = scores_t.rearrange("(a b) (t s) -> b t a s", b=2, s=P)
            for b in range(2):
                sp.dma_start(ts[b * T:(b + 1) * T, :, :], by_tile[b]).then_inc(s_ts, 16)
            sp.wait_ge(s_found, 1)
            sp.dma_start(thr, lo_hi[:]).then_inc(s_thr_st, 16)
            sp.wait_ge(s_thr_st, 16)
            by_expert = thr.rearrange("(a b c) n -> b c a n", b=2, c=CHUNKS)
            for b in range(2):
                sp.dma_start(th[b * T:(b + 1) * T, :, :], by_expert[b][0:1].to_broadcast([T, EP, 2])).then_inc(s_th, 16)
            sp.wait_ge(s_th, 32)

        @block.gpsimd
        def _(pool):
            c = Chain(pool, s_e)
            c.link(pool.memset(same[:], 1.0))
            v = same[:].rearrange("p (e c) -> p e c", c=CHUNKS)
            c.link(pool.affine_select(out=v, in_=v, compare_op=ALU.is_ge, fill=0.0, base=0,
                                      pattern=[[-CHUNKS, E], [0, CHUNKS]], channel_multiplier=1))
            c.link(pool.affine_select(out=v, in_=v, compare_op=ALU.is_ge, fill=0.0, base=CHUNKS - 1,
                                      pattern=[[CHUNKS, E], [0, CHUNKS]], channel_multiplier=-1))
            c.link(pool.memset(group[:], 1.0))
            c.link(pool.affine_select(out=group[:, 0:T], in_=group[:, 0:T], compare_op=ALU.is_ge, fill=0.0,
                                      base=T - 1, pattern=[[0, T]], channel_multiplier=-1))
            c.link(pool.affine_select(out=group[:, T:TP], in_=group[:, T:TP], compare_op=ALU.is_ge, fill=0.0,
                                      base=-T, pattern=[[0, T]], channel_multiplier=1))
            c.link(pool.affine_select(out=before[:], in_=group[:], compare_op=ALU.is_ge, fill=0.0, base=-1,
                                      pattern=[[1, TP]], channel_multiplier=-1))
            c.link(pool.iota(slot[:], [[1, CAP]], base=0, channel_multiplier=0, allow_small_or_imprecise_dtypes=True))
            c.link(pool.iota(slot_of[:], [[P, ST]], base=0, channel_multiplier=1, allow_small_or_imprecise_dtypes=True))
            for b in range(2):
                c.link(pool.iota(tile_no[b * T:(b + 1) * T, :], [[0, 1]], base=0, channel_multiplier=P,
                                 allow_small_or_imprecise_dtypes=True))
            c.link(pool.memset(ones_row[:], 1.0))
            c.link(pool.memset(ones[:], 1.0))
            pool.wait_ge(s_pm, 2)
            pool.partition_all_reduce(bound[:], junk[:, 0:1], P, bass.bass_isa.ReduceOp.max).then_inc(s_bound, 1)

        @block.vector
        def _(dve):
            dve.wait_ge(s_sc, 16)
            dve.tensor_reduce(part_max[:], sc[:], AX_X, ALU.max).then_inc(s_pm, 1)
            dve.tensor_reduce(junk[:, 0:1], sc[:], AX_X, ALU.max, apply_absolute_value=True).then_inc(s_pm, 1)
            dve.wait_ge(s_bound, 1)
            c = Chain(dve, s_init)
            c.link(dve.tensor_scalar(lo_hi[:, 1:2], bound[:], 2.0, 1.0 / BIG, ALU.mult, ALU.add))
            c.link(dve.tensor_scalar(lo_hi[:, 0:1], lo_hi[:, 1:2], -1.0, None, ALU.mult))
            lo, hi = lo_hi[:, 0:1], lo_hi[:, 1:2]
            with dve.Fori(0, BISECTIONS, 1) as i:
                dve.wait_ge(s_thr, i * 5)
                dve.tensor_scalar(t[:], lo, hi, 0.5, ALU.add, ALU.mult).then_inc(s_thr, 1)
                dve.wait_ge(s_thr, i * 5 + 1)
                dve.tensor_scalar(junk[:], sc[:], t[:, 0:1], 0.0, ALU.is_ge, ALU.add, accum_out=cnt[:]).then_inc(s_count, 1)
                dve.wait_ge(s_tot, i + 1)
                dve.tensor_scalar(u[:], tot_ps[:, 0:1], float(CAP), BIG, ALU.is_ge, ALU.mult).then_inc(s_thr, 1)
                dve.tensor_scalar(u2[:], tot_ps[:, 0:1], float(CAP), -BIG, ALU.is_lt, ALU.mult).then_inc(s_thr, 1)
                dve.wait_ge(s_thr, i * 5 + 3)
                dve.scalar_tensor_tensor(out=hi, in0=u[:], scalar=t[:, 0:1], in1=hi, op0=ALU.add, op1=ALU.min).then_inc(s_thr, 1)
                dve.scalar_tensor_tensor(out=lo, in0=u2[:], scalar=t[:, 0:1], in1=lo, op0=ALU.add, op1=ALU.max).then_inc(s_thr, 1)
            dve.wait_ge(s_thr, 5 * BISECTIONS)
            dve.wait_ge(s_count, BISECTIONS)
            dve.tensor_copy(u[:], lo).then_inc(s_found, 1)
            dve.wait_ge(s_top_t, 1)
            dve.tensor_reduce(top[:], small_ps[0:1, 0:P].rearrange("p (e c) -> p e c", c=CHUNKS), AX_X, ALU.max,
                              negate=True).then_inc(s_top, 1)
            dve.wait_ge(s_top_b, 1)
            dve.tensor_copy(neg_top[:], small_ps[:, 0:E]).then_inc(s_top, 1)
            c = Chain(dve, d)
            dve.wait_ge(s_ts, 32)
            dve.wait_ge(s_th, 32)
            dve.wait_ge(s_e, 13)
            wide = [TP, EP, P]
            c.link(dve.tensor_tensor(above[:], ts[:], th[:, :, 1:2].to_broadcast(wide), ALU.is_ge))
            c.link(dve.tensor_tensor(tied[:], ts[:], th[:, :, 0:1].to_broadcast(wide), ALU.is_ge))
            c.link(dve.tensor_tensor(tied[:], tied[:], above[:], ALU.subtract))
            c.link(dve.tensor_reduce(n_above[:], above[:], AX_X, ALU.add))
            for a in range(EP):
                ins = dve.tensor_tensor_scan(place[:, a, :], ones[:], tied[:, a, :], 0.0, ALU.mult, ALU.add)
                ins.then_inc(s_tie, 1)
            dve.wait_ge(s_tie, EP)
            dve.wait_ge(s_left, 1)
            c.link(dve.tensor_scalar(left[:], small_ps[0:TP, 0:EP], float(CAP), None, ALU.subtract))
            c.link(dve.tensor_tensor(place[:], place[:], left[:].unsqueeze(2).to_broadcast(wide), ALU.add))
            c.link(dve.scalar_tensor_tensor(out=chosen[:], in0=place[:], scalar=0.0, in1=tied[:], op0=ALU.is_le, op1=ALU.mult))
            c.link(dve.tensor_tensor(chosen[:], chosen[:], above[:], ALU.add))
            for a in range(EP):
                dve.tensor_tensor_scan(count[:, a, :], ones[:], chosen[:, a, :], 0.0, ALU.mult, ALU.add).then_inc(s_sel, 1)
            dve.wait_ge(s_sel, EP)
            dve.wait_ge(s_start, 1)
            c.link(dve.tensor_copy(start[:], small_ps[0:TP, 0:EP]))
            c.link(dve.tensor_tensor(end[:], start[:], count[:, :, P - 1], ALU.add))
            c.link(dve.tensor_tensor(upto[:, :, 0:P], count[:], start[:].unsqueeze(2).to_broadcast(wide), ALU.add))
            c.link(dve.tensor_copy(upto[:, :, P:P + 1], tile_no[:].unsqueeze(1).to_broadcast([TP, EP, 1])))
            for a in range(EP):
                c.link(dve.tensor_scalar(under[:, a, :], slot[0:TP, :], end[:, a:a + 1], None, ALU.is_lt))
                dve.scalar_tensor_tensor(out=hot[:, a, :], in0=slot[0:TP, :], scalar=start[:, a:a + 1], in1=under[:, a, :],
                                         op0=ALU.is_ge, op1=ALU.mult).then_inc(s_hot, 1)
            for n in range(E * ST):
                dve.wait_ge(s_pick, n + 1)
                if n >= 2:
                    dve.wait_ge(s_pos, n - 1)
                dve.tensor_scalar(cnt_junk[n % 2][:], g_ps[n % 4][:, 0:P], slot_of[:, n % ST:n % ST + 1], g_ps[n % 4][:, P:P + 1],
                                  ALU.is_le, ALU.add, accum_out=pos[:, n:n + 1]).then_inc(s_pos, 1)
            dve.wait_ge(s_pos, E * ST)
            dve.tensor_copy(idx_all[:], pos[:]).then_inc(s_pos, 1)

        @block.tensor
        def _(pe):
            pe.wait_ge(s_e, 13)
            pe.wait_ge(s_pm, 1)
            pe.transpose(small_ps[0:1, 0:P], part_max[:], w["ident"][:]).then_inc(s_top_t, 1)
            with pe.Fori(0, BISECTIONS, 1) as i:
                pe.wait_ge(s_count, i + 1)
                pe.matmul(tot_ps[:, 0:1], same[:], cnt[:], start=True, stop=True).then_inc(s_tot, 1)
            pe.wait_ge(s_top, 1)
            pe.matmul(small_ps[:, 0:E], ones_row[:], top[:], start=True, stop=True).then_inc(s_top_b, 1)
            pe.wait_ge(s_top, 2)
            pe.wait_ge(d, 4)
            pe.wait_ge(s_tie, EP)
            pe.matmul(small_ps[0:TP, 0:EP], group[:], n_above[:], start=True, stop=False)
            pe.matmul(small_ps[0:TP, 0:EP], before[:], place[:, :, P - 1], start=False, stop=True).then_inc(s_left, 1)
            pe.wait_ge(s_sel, EP)
            pe.matmul(small_ps[0:TP, 0:EP], before[:], count[:, :, P - 1], start=True, stop=True).then_inc(s_start, 1)
            for n in range(E * ST):
                e, st = n // ST, n % ST
                a, rows_ = e // 2, slice((e % 2) * T, (e % 2 + 1) * T)
                if st == 0 and e % 2 == 0:
                    pe.wait_ge(s_hot, a + 1)
                if n >= 4:
                    pe.wait_ge(s_pos, n - 3)
                pe.matmul(g_ps[n % 4][:, 0:P + 1], hot[rows_, a, st * P:(st + 1) * P], upto[rows_, a, :],
                          start=True, stop=True).then_inc(s_pick, 1)


def experts(nc, ctx, w, rows, idx_all, neg_top, g_f, w1_t, w3_t, w2_t, out):
    CAP = out.shape[0] // E
    ST = CAP // P
    HT = max(1, CAP // 512)
    SPAN = CAP // HT
    TT = SPAN // P
    FT = F // P

    def sb(name, shape, dt=F32):
        return ctx.enter_context(nc.sbuf_tensor(name, shape, dt))

    def sem(name):
        return ctx.enter_context(nc.semaphore(name))

    def bank(name, dt=F32):
        return ctx.enter_context(nc.psum_tensor(name, [P, 512], dt))

    gf_raw, gf, ones = sb("gf_raw", [P, 1]), sb("gf", [P, 1]), sb("ones3", [P, P])
    w1 = [sb(f"w1_{p}", [P, KD, F]) for p in range(2)]
    w3 = [sb(f"w3_{p}", [P, KD, F]) for p in range(2)]
    w2 = [sb(f"w2_{p}", [P, FT, D]) for p in range(2)]
    idx = [sb(f"idx{p}", [P, ST], U32) for p in range(2)]
    xg = [sb(f"xg{p}", [P, ST, ROW]) for p in range(2)]
    xg_t = [sb(f"xg_t{p}", [P, KD, CAP]) for p in range(2)]
    raw_s, top_e, e_s, sum_s, inv = sb("raw_s", [P, ST]), sb("top_e", [P, 1]), sb("e_s", [P, ST]), sb("sum_s", [P, 1]), sb("inv", [P, 1])
    weight = [sb(f"weight{p}", [P, ST]) for p in range(2)]
    act_h = [sb(f"act_h{i}", [P, SPAN]) for i in range(2)]
    hid = [sb(f"hid{i}", [P, FT, SPAN]) for i in range(HT)]
    y = [sb(f"y_{i}", [P, D]) for i in range(ST)]

    t_ps = [bank(f"t_ps{i}") for i in range(2)]
    h1_ps, h3_ps = [bank(f"h1_ps{i}") for i in range(2)], [bank("h3_ps0")]
    y_ps = [bank(f"y_ps{i}") for i in range(2)]
    z_ps = bank("z_ps")

    s_g, s_gf, s_one = sem("s_g3"), sem("s_gf"), sem("s_one3")
    s_w = [sem(f"s_w{p}") for p in range(2)]
    s_idx, s_xg = sem("s_idx"), [sem(f"s_xg{p}") for p in range(2)]
    t_done, t_out = sem("t_done"), sem("t_out")
    s_raw, s_es, z_done, s_inv, s_wt = sem("s_raw"), sem("s_es"), sem("z_done"), sem("s_inv"), sem("s_wt")
    h1_done, h3_done, silu_done, hid_done = sem("h1_done"), sem("h3_done"), sem("silu_done"), sem("hid_done")
    y_done, y_out = sem("y_done"), sem("y_out")
    s_add = [sem(f"s_add{i}") for i in range(ST)]
    passed = w["passed"]
    TRANS = KD * HT
    HID = HT * FT

    class Expert:

        def __init__(self, k, p):
            self.k, self.p = k + p // 2, p % 2

        def on(self, n):
            return Expert(self.k, self.p + n)

        @property
        def ok(self):
            return not isinstance(self.k, int) or 0 <= 2 * self.k + self.p < E

        def times(self, n, more=0):
            return self.k * (2 * n) + (self.p * n + more)

        def turn(self, n, more=0):
            return self.k * n + more

    def over(eng, step):
        for p in range(2):
            step(Expert(0, p))
        with eng.Fori(1, E // 2 - 1, 1) as k:
            for p in range(2):
                step(Expert(k, p))
        for p in range(2):
            step(Expert(E // 2 - 1, p))

    with nc.Block() as block:

        @block.sync
        def _(sp):
            sp.dma_start(gf_raw[:], g_f.rearrange("(a n) -> a n", a=1).to_broadcast([P, 1])).then_inc(s_g, 16)

            def load(e):
                if not e.ok:
                    return
                wait(sp, y_done, e.times(ST, -ST))
                sp.sem_inc(passed, 1)
                i = e.times(1)
                for dst, src, n in ((w1, w1_t, F), (w3, w3_t, F), (w2, w2_t, D)):
                    view = src.rearrange("e (k p) n -> p e k n", p=P)
                    view = view[:, i] if isinstance(i, int) else view[:, bass.ds(i, 1)].rearrange("p e k n -> p (e k) n")
                    sp.dma_start(dst[e.p][:], view).then_inc(s_w[e.p], 16)

            load(Expert(0, 0))
            load(Expert(0, 1))
            over(sp, lambda e: load(e.on(2)))
            for p in range(2):
                sp.wait_ge(s_w[p], 48 * E // 2)

        @block.gpsimd
        def _(pool):
            def gather(e):
                if not e.ok:
                    return
                wait(pool, s_idx, e.times(1, 1))
                wait(pool, t_done, e.times(TRANS, -TRANS))
                wait(pool, s_raw, e.times(1, -1))
                pool.sem_inc(passed, 1)
                for st in range(ST):
                    pool.indirect_dma_start(xg[e.p][:, st, :], None, rows[:, :],
                                            bass.IndirectOffsetOnAxis(ap=idx[e.p][:, st:st + 1], axis=0)).then_inc(s_xg[e.p], 16)

            def add(e):
                for st in range(ST):
                    wait(pool, s_add[st], e.times(16))
                for st in range(ST):
                    pool.wait_ge(y_out, e.times(ST, st + 1))
                    pool.sem_inc(passed, 1)
                    pool.indirect_dma_start(out[:, :], bass.IndirectOffsetOnAxis(ap=idx[e.p][:, st:st + 1], axis=0),
                                            y[st][:], None, compute_op=ALU.add).then_inc(s_add[st], 16)

            gather(Expert(0, 0))

            def step(e):
                gather(e.on(1))
                add(e)

            over(pool, step)
            for st in range(ST):
                pool.wait_ge(s_add[st], 16 * E)

        @block.scalar
        def _(act):
            act.wait_ge(s_g, 16)
            act.activation(gf[:], gf_raw[:], ACT.Tanh).then_inc(s_gf, 1)

            def weigh(e):
                if e.ok:
                    act.wait_ge(s_raw, e.times(1, 1))
                    wait(act, s_wt, e.times(1))
                    act.activation(e_s[:], raw_s[:], ACT.Exp, bias=top_e[:, 0:1], accum_out=sum_s[:]).then_inc(s_es, 1)

            def silu(e, n):
                act.wait_ge(h1_done, e.times(HID, n + 1))
                wait(act, hid_done, e.times(HID, n - 1))
                act.activation(act_h[n % 2][:], h1_ps[n % 2][:, 0:SPAN], ACT.Silu).then_inc(silu_done, 1)

            def y_copy(e, st):
                act.wait_ge(y_done, e.times(ST, st + 1))
                act.wait_ge(s_wt, e.times(1, 1))
                wait(act, s_add[st], e.times(16))
                act.activation(y[st][:], y_ps[st % 2][:, 0:D], ACT.Copy, scale=weight[e.p][:, st:st + 1]).then_inc(y_out, 1)

            weigh(Expert(0, 0))

            def step(e):
                for n in range(HID):
                    silu(e, n)
                for st in range(ST // 2):
                    y_copy(e, st)
                weigh(e.on(1))
                for st in range(ST // 2, ST):
                    y_copy(e, st)

            over(act, step)

        @block.vector
        def _(dve):
            dve.memset(ones[:], 1.0).then_inc(s_one, 1)
            dve.wait_ge(s_gf, 1)

            def list_of(e):
                if e.ok:
                    for st in range(ST):
                        wait(dve, s_add[st], e.times(16, -16))
                    i = e.times(ST)
                    dve.tensor_copy(idx[e.p][:], idx_all[:, i:i + ST] if isinstance(i, int) else idx_all[:, bass.ds(i, ST)]).then_inc(s_idx, 1)

            def raw(e):
                if e.ok:
                    i = e.times(1)
                    dve.wait_ge(s_xg[e.p], e.turn(16 * ST, 16 * ST))
                    wait(dve, s_es, e.times(1))
                    dve.tensor_copy(top_e[:], neg_top[:, i:i + 1] if isinstance(i, int) else neg_top[:, bass.ds(i, 1)]).then_inc(s_inv, 1)
                    col = xg[e.p][:, :, D + i:D + i + 1] if isinstance(i, int) else xg[e.p][:, :, bass.ds(i + D, 1)]
                    dve.wait_ge(s_inv, e.times(2, 1))
                    dve.tensor_copy(raw_s[:].unsqueeze(2), col).then_inc(s_raw, 1)

            def weights(e):
                if e.ok:
                    dve.wait_ge(z_done, e.times(1, 1))
                    dve.reciprocal(inv[:], z_ps[:, 0:1]).then_inc(s_inv, 1)
                    dve.wait_ge(s_inv, e.times(2, 2))
                    wait(dve, y_out, e.times(ST, -ST))
                    dve.tensor_scalar(weight[e.p][:], e_s[:], inv[:, 0:1], gf[:, 0:1], ALU.mult, ALU.mult).then_inc(s_wt, 1)

            def t_copy(e, i):
                if e.ok:
                    k, h = i % KD, i // KD
                    dve.wait_ge(t_done, e.times(TRANS, i + 1))
                    wait(dve, h3_done, e.times(HID, -HID))
                    dve.tensor_copy(xg_t[e.p][:, k, h * SPAN:(h + 1) * SPAN], t_ps[i % 2][:, 0:SPAN]).then_inc(t_out, 1)

            def gate(e, n):
                dve.wait_ge(h3_done, e.times(HID, n + 1))
                dve.wait_ge(silu_done, e.times(HID, n + 1))
                if n % FT == 0:
                    wait(dve, y_done, e.times(ST, (n // FT + 1) * TT - ST))
                dve.tensor_tensor(hid[n // FT][:, n % FT, :], act_h[n % 2][:], h3_ps[0][:, 0:SPAN], ALU.mult).then_inc(hid_done, 1)

            list_of(Expert(0, 0))
            raw(Expert(0, 0))
            weights(Expert(0, 0))
            for i in range(TRANS):
                t_copy(Expert(0, 0), i)

            def step(e):
                list_of(e.on(1))
                for n in range(HID):
                    gate(e, n)
                raw(e.on(1))
                for i in range(TRANS):
                    t_copy(e.on(1), i)
                weights(e.on(1))

            over(dve, step)

        @block.tensor
        def _(pe):
            pe.wait_ge(s_one, 1)

            def transposes(e, i):
                if e.ok:
                    k, h = i % KD, i // KD
                    if i == 0:
                        pe.wait_ge(s_xg[e.p], e.turn(16 * ST, 16 * ST))
                    wait(pe, t_out, e.times(TRANS, i - 1))
                    for t in range(TT):
                        mm = pe.transpose(t_ps[i % 2][:, t * P:(t + 1) * P], xg[e.p][:, h * TT + t, k * P:(k + 1) * P], w["ident"][:])
                    mm.then_inc(t_done, 1)

            def total(e):
                if e.ok:
                    pe.wait_ge(s_es, e.times(1, 1))
                    wait(pe, s_wt, e.times(1))
                    pe.matmul(z_ps[:, 0:1], ones[:], sum_s[:], start=True, stop=True).then_inc(z_done, 1)

            def hidden(e, n):
                h, f = n // FT, slice((n % FT) * P, (n % FT + 1) * P)
                if n == 0:
                    pe.wait_ge(s_w[e.p], e.turn(48, 48))
                    pe.wait_ge(t_out, e.times(TRANS, TRANS))
                wait(pe, silu_done, e.times(HID, n - 1))
                for k in range(KD):
                    mm = pe.matmul(h1_ps[n % 2][:, 0:SPAN], w1[e.p][:, k, f], xg_t[e.p][:, k, h * SPAN:(h + 1) * SPAN],
                                   start=(k == 0), stop=(k == KD - 1))
                mm.then_inc(h1_done, 1)
                wait(pe, hid_done, e.times(HID, n))
                for k in range(KD):
                    mm = pe.matmul(h3_ps[0][:, 0:SPAN], w3[e.p][:, k, f], xg_t[e.p][:, k, h * SPAN:(h + 1) * SPAN],
                                   start=(k == 0), stop=(k == KD - 1))
                mm.then_inc(h3_done, 1)

            def down(e, st):
                h, t = st // TT, slice((st % TT) * P, (st % TT + 1) * P)
                pe.wait_ge(hid_done, e.times(HID, (h + 1) * FT))
                wait(pe, y_out, e.times(ST, st - 1))
                for f in range(FT):
                    mm = pe.matmul(y_ps[st % 2][:, 0:D], hid[h][:, f, t], w2[e.p][:, f, :], start=(f == 0), stop=(f == FT - 1))
                mm.then_inc(y_done, 1)

            first = Expert(0, 0)
            total(first)
            for i in range(TRANS):
                transposes(first, i)

            def step(e):
                for n in range(HID):
                    hidden(e, n)
                for i in range(TRANS):
                    transposes(e.on(1), i)
                for st in range(ST // 2):
                    down(e, st)
                total(e.on(1))
                for st in range(ST // 2, ST):
                    down(e, st)

            over(pe, step)


def build(nc, x, ctx_t, mask, g_x, g_f, wq, bq, wk, bk, wv, bv, wg_t, w1_t, w3_t, w2_t, out):
    n_tok = x.shape[0]
    rows = nc.dram_tensor("rows_scratch", (n_tok, ROW), F32, kind="Internal").ap()
    scores_t = nc.dram_tensor("scores_scratch", (E, n_tok), F32, kind="Internal").ap()
    thr = nc.dram_tensor("thr_scratch", (P, 2), F32, kind="Internal").ap()
    mask_bias = nc.dram_tensor("mask_scratch", (1, n_tok), BF16, kind="Internal").ap()
    with ExitStack() as whole:
        w = {"ident": whole.enter_context(nc.sbuf_tensor("ident", [P, P], F32)),
             "s_id": whole.enter_context(nc.semaphore("s_id")),
             "passed": whole.enter_context(nc.semaphore("passed"))}
        with ExitStack() as ctx:
            attention(nc, ctx, w, x, ctx_t, mask, g_x, wq, bq, wk, bk, wv, bv, wg_t, out, rows, scores_t, mask_bias)
        idx_all = whole.enter_context(nc.sbuf_tensor("idx_all", [P, n_tok // P], U32))
        neg_top = whole.enter_context(nc.sbuf_tensor("neg_top", [P, E], F32))
        with ExitStack() as ctx:
            select(nc, ctx, w, rows, scores_t, thr, idx_all, neg_top)
        with ExitStack() as ctx:
            experts(nc, ctx, w, rows, idx_all, neg_top, g_f, w1_t, w3_t, w2_t, out)


_HEAD_MAJOR = ("L0_xattn_Wq", "L0_xattn_Wk", "L0_xattn_bq", "L0_xattn_bk")


def lay_out(inputs):
    a = {k: np.asarray(v) for k, v in inputs.items()}
    n = a["x"].shape[0] * a["x"].shape[1]

    def columns(m):
        lead = m.shape[:-1]
        m = m.reshape(*lead, P // DH, KD, DH)
        return np.moveaxis(m, (-3, -2, -1), (-1, -3, -2)).reshape(*lead, D)

    return {
        "x": a["x"].reshape(n, D),
        "ctx_t": a["ctx_1024"].reshape(n, D).T,
        "mask": a["mask_BxS2_ik0"],
        "g_x": a["g_xattn"],
        "g_f": a["g_ffn"],
        "wq": columns(a["L0_xattn_Wq"]),
        "bq": columns(a["L0_xattn_bq"]).reshape(KD, P).T,
        "wk": columns(a["L0_xattn_Wk"]),
        "bk": columns(a["L0_xattn_bk"]).reshape(KD, P).T,
        "wv": a["L0_xattn_Wv"],
        "bv": a["L0_xattn_bv"],
        "wg_t": a["L0_ffn_Wg"].T,
        "w1_t": a["L0_ffn_W1"].transpose(0, 2, 1),
        "w3_t": a["L0_ffn_W3"].transpose(0, 2, 1),
        "w2_t": a["L0_ffn_W2"].transpose(0, 2, 1),
    }


def kernel(**inputs):
    import concourse.bacc as bacc
    from concourse.bass_utils import run_bass_kernel_spmd

    shape = inputs["x"].shape
    nc = bacc.Bacc("TRN2", target_bir_lowering=False, num_devices=1)
    arrays, args = {}, []
    for name, a in lay_out(inputs).items():
        a = np.ascontiguousarray(a)
        arrays[f"in_{name}"] = a
        args.append(nc.dram_tensor(f"in_{name}", a.shape, mybir.dt.from_np(a.dtype), kind="ExternalInput").ap())
    out = nc.dram_tensor("out", (shape[0] * shape[1], D), F32, kind="ExternalOutput").ap()
    build(nc, *args, out)
    r = run_bass_kernel_spmd(nc, [arrays], core_ids=[0])
    return r.results[0]["out"].reshape(shape)
```

```python
from contextlib import ExitStack

import numpy as np

import concourse.bass as bass
from concourse import mybir

F32 = mybir.dt.float32
BF16 = mybir.dt.bfloat16
FP16 = mybir.dt.float16
I32 = mybir.dt.int32
U32 = mybir.dt.uint32
ALU = mybir.AluOpType
ACT = mybir.ActivationFunctionType
AX_X = mybir.AxisListType.X

P = 128
D = 256
HEADS = 16
DH = 16
GB = 4
GT = GB * P
KD = D // P
VW = 32
EPS = 1e-5
MASKED = float(2 ** 30)
SCALE = 1.0 / float(np.sqrt(np.float32(10.0)))
E = 8
F = 512
ROW = D + E
HI, MID, LO = range(3)
Q_ROWS = [HI, HI, HI, MID, MID, LO]
K_ROWS = [HI, MID, LO, HI, MID, HI]
SPLIT = len(Q_ROWS) * DH
MASK_ROW, MAX_ROW = SPLIT, SPLIT + 1
A_K, B_K = SPLIT + 1, SPLIT + 3
MAGIC = 1597463007.0
Q_SENT, K_SENT = 16 * 6, 16 * 7
LN_OPS = 16


class Batch:

    def __init__(self, k, s, total):
        self.k, self.s, self.total = k + s // 8, s % 8, total

    def back(self, n):
        return Batch(self.k, self.s - n, self.total)

    @property
    def ok(self):
        return not isinstance(self.k, int) or 0 <= 8 * self.k + self.s < self.total

    def times(self, n, more=0):
        return self.k * (8 * n) + (self.s * n + more)

    def turn(self, ring, n, more=0):
        return self.k * (8 // ring * n) + (self.s // ring * n + more)

    @property
    def tok(self):
        return self.k * (8 * P) + self.s * P

    @property
    def j(self):
        return self.s % GB

    @property
    def group(self):
        return Group(self.k, self.s // GB, self.total // GB)


class Group:

    def __init__(self, k, p, total):
        self.k, self.p, self.total = k + p // 2, p % 2, total

    def on(self, n):
        return Group(self.k, self.p + n, self.total)

    @property
    def ok(self):
        return not isinstance(self.k, int) or 0 <= 2 * self.k + self.p < self.total

    def times(self, n, more=0):
        return self.k * (2 * n) + (self.p * n + more)

    def turn(self, n, more=0):
        return self.k * n + more

    @property
    def tok(self):
        return self.k * (2 * GT) + self.p * GT


def wait(eng, sem, value):
    if not isinstance(value, int) or value > 0:
        eng.wait_ge(sem, value)


class Chain:

    def __init__(self, eng, sem, base=0, passed=None):
        self.eng, self.sem, self.base, self.n, self.passed = eng, sem, base, 0, passed

    def link(self, ins):
        ins.then_inc(self.sem, 1)
        self.n += 1
        self.eng.wait_ge(self.sem, self.base + self.n)
        if self.passed is not None and not isinstance(self.base, int):
            self.eng.sem_inc(self.passed, 1)


def attention(nc, ctx, w, x, ctx_t, mask, g_x, wq, bq, wk, bk, wv, bv, wg_t, out, rows, scores_t,
              mask_bias):
    n_tok = x.shape[0]
    NB = n_tok // P
    NG = NB // GB

    def sb(name, shape, dt=F32):
        return ctx.enter_context(nc.sbuf_tensor(name, shape, dt))

    def sem(name):
        return ctx.enter_context(nc.semaphore(name))

    def bank(name, dt=F32):
        return ctx.enter_context(nc.psum_tensor(name, [P, 512], dt))

    ident, passed = w["ident"], w["passed"]
    wq_sb, wk_sb, wv_sb = sb("wq_sb", [P, KD, D]), sb("wk_sb", [P, KD, D]), sb("wv_sb", [P, KD, D])
    wg_sb = sb("wg_sb", [P, KD, E])
    bq_sb, bk_sb = sb("bq_sb", [P, KD]), sb("bk_sb", [P, KD])
    bv_sb = sb("bv_sb", [P, D])
    ones_bf = sb("ones_bf", [HEADS, GT], BF16)
    gx_raw, gx = sb("gx_raw", [P, 1]), sb("gx", [P, 1])
    mask_nat = sb("mask_nat", [NB, P], I32)
    bias_nat = sb("bias_nat", [NB, P], BF16)
    x_in = [sb(f"x_in{p}", [P, GB, D]) for p in range(2)]
    c_t = [sb(f"c_t{p}", [P, KD, GT]) for p in range(2)]
    mask_b = [sb(f"mask_b{p}", [P, GT], I32) for p in range(2)]
    stats1, mv1 = sb("stats1", [P, GB, 6]), sb("mv1", [P, GB, 2])
    v1, y1, t1, nm1 = sb("v1", [P, GB]), sb("y1", [P, GB]), sb("t1", [P, GB]), sb("nm1", [P, GB])
    xn, xn_t = sb("xn", [P, GB, D]), sb("xn_t", [P, KD, GT])
    q_rest, k_val, k_rest = sb("q_rest", [P, KD, GT]), sb("k_val", [P, KD, GT]), sb("k_rest", [P, KD, GT])
    q_part, k_part = sb("q_part", [P, 3, KD, GT], BF16), sb("k_part", [P, 3, KD, GT], BF16)
    q_st = [sb(f"q_st{p}", [P, HEADS, GT], BF16) for p in range(2)]
    k_st = [sb(f"k_st{p}", [P, HEADS, GT], BF16) for p in range(2)]
    v_aug = [sb(f"v_aug{p}", [P, GB, HEADS, VW]) for p in range(2)]
    m_sb = [sb(f"m_sb{i}", [P, HEADS]) for i in range(2)]
    neg_m = [sb(f"neg_m{i}", [HEADS, 2, P], BF16) for i in range(2)]
    p_t = [sb(f"p_t{i}", [P, HEADS, P]) for i in range(2)]
    o_t = [sb(f"o_t{i}", [P, 4, P]) for i in range(2)]
    rden, o_n = sb("rden", [P, HEADS]), sb("o_n", [P, D])
    x_res = [sb(f"x_res{p}", [P, GB, D]) for p in range(2)]
    x2 = [sb(f"x2_{p}", [P, GB, D]) for p in range(2)]
    stats2 = sb("stats2", [P, 6])
    mv2 = [sb(f"mv2_{p}", [P, GB, 2]) for p in range(2)]
    v2, y2, t2 = sb("v2", [P, GB]), sb("y2", [P, GB]), sb("t2", [P, GB])
    nm2 = sb("nm2", [P, GB])
    row = [sb(f"row{p}", [P, GB, ROW]) for p in range(2)]
    xn2_t = sb("xn2_t", [P, KD, GT])
    s_t = sb("s_t", [E, GT])

    a_ps = [bank(f"a_ps{i}") for i in range(2)]
    b_ps = [bank(f"b_ps{i}") for i in range(2)]
    pv_ps = bank("pv_ps")
    f_ps = bank("f_ps")
    m_ps = bank("m_ps")
    o_ps = bank("o_ps")

    s_wq, s_wk, s_wv, s_misc = sem("s_wq"), sem("s_wk"), sem("s_wv"), sem("s_misc")
    s_ones, s_zero, s_rows1 = sem("s_ones"), sem("s_zero"), sem("s_rows1")
    s_bias, s_bias_st, s_gx = sem("s_bias"), sem("s_bias_st"), sem("s_gx")
    s_x = [sem(f"s_x{p}") for p in range(2)]
    s_c = [sem(f"s_c{p}") for p in range(2)]
    s_mv1, s_ln1, s_xn = sem("s_mv1"), sem("s_ln1"), sem("s_xn")
    s_st1 = sem("s_st1")
    f_done = sem("f_done")
    f_free = [sem(f"f_free{i}") for i in range(2)]
    q_hi, q_mid, q_lo = sem("q_hi"), sem("q_mid"), sem("q_lo")
    k_hi, k_r, k_mid, k_lo = sem("k_hi"), sem("k_r"), sem("k_mid"), sem("k_lo")
    s_q = [sem(f"s_q{p}") for p in range(2)]
    s_k = [sem(f"s_k{p}") for p in range(2)]
    a_done, max_done = sem("a_done"), sem("max_done")
    mt_done, nhi_done, nmid_done = sem("mt_done"), sem("nhi_done"), sem("nmid_done")
    s_m = [sem(f"s_m{i}") for i in range(2)]
    b_done, exp_done, pv_done, pv_out = sem("b_done"), sem("exp_done"), sem("pv_done"), sem("pv_out")
    ot_done, rd_done, ot_out, x2_done, st2_done, mv2_done, ln2 = (
        sem("ot_done"), sem("rd_done"), sem("ot_out"), sem("x2_done"), sem("st2_done"), sem("mv2_done"), sem("ln2"))
    xn2_done, xt2_done, xt2_out = sem("xn2_done"), sem("xt2_done"), sem("xt2_out")
    r_done, r_out, st_done, st_out = sem("r_done"), sem("r_out"), sem("st_done"), sem("st_out")
    s_res = [sem(f"s_res{p}") for p in range(2)]
    s_out = [sem(f"s_out{p}") for p in range(2)]
    s_row = [sem(f"s_row{p}") for p in range(2)]
    s_sc = sem("s_sc")

    def steps(eng, step):
        for g in range(4):
            for j in range(GB):
                step(eng, Batch(g // 2, 4 * (g % 2) + j, NB))
        with eng.Fori(2, NG // 2 - 1, 1) as k:
            for s in range(2 * GB):
                step(eng, Batch(k, s, NB))
        for g in range(NG - 2, NG + 4):
            for j in range(GB):
                step(eng, Batch(g // 2, 4 * (g % 2) + j, NB))

    def f_bank(g, i):
        return m_ps if i == 1 and isinstance(g.k, int) and g.k == 0 and g.p == 0 else f_ps

    O_USES = sorted([((j, 1), "ot", j) for j in range(GB)]
                    + [((3, 0), "xt", 0), ((0, 0), "xt", 1), ((1, 0), "r", 0), ((2, 0), "st", 0)])
    O_LAG = {("xt", 0): 2, ("xt", 1): 3, ("r", 0): 3, ("st", 0): 3}

    def o_free(eng, g, q, j):
        at = [x[0] for x in O_USES].index((j, q))
        for back in range(1, 4 * len(O_USES)):
            i, turn = (at - back) % len(O_USES), (at - back) // len(O_USES)
            (_, what, n) = O_USES[i]
            if what == "ot":
                use = Batch(g.k, 4 * g.p + n + 4 * turn, NB).back(4)
                if use.ok:
                    return wait(eng, ot_out, use.times(1, 1))
            else:
                use = g.on(turn - O_LAG[what, n])
                if use.ok:
                    if what == "xt":
                        return wait(eng, xt2_out, use.times(2, n + 1))
                    return wait(eng, r_out if what == "r" else st_out, use.times(1, 1))

    with nc.Block() as block:

        @block.sync
        def _(sp):
            def load_const(dst, src, ready):
                sp.dma_start(dst, src).then_inc(ready, 16)

            def square(m):
                return m.rearrange("(k p) n -> p k n", p=P)

            def over_rows(v):
                return v.rearrange("(a n) -> a n", a=1).to_broadcast([P, v.shape[0]])

            def load_x(g):
                if g.ok:
                    wait(sp, s_xn, g.times(4, -4))
                    sp.sem_inc(passed, 1)
                    sp.dma_start(x_in[g.p][:], x[bass.ds(g.tok, GT), :].rearrange("(t p) d -> p t d", p=P)).then_inc(s_x[g.p], 16)

            def load_c(g):
                if g.ok:
                    wait(sp, f_done, g.times(8, -8))
                    sp.sem_inc(passed, 1)
                    wait(sp, f_free[1], g.times(4, -5))
                    sp.sem_inc(passed, 1)
                    sp.dma_start(c_t[g.p][:], ctx_t[:, bass.ds(g.tok, GT)].rearrange("(k p) t -> p k t", p=P)).then_inc(s_c[g.p], 16)
                    sp.dma_start(mask_b[g.p][:], mask.rearrange("b (a s) -> a (b s)", a=1)[:, bass.ds(g.tok, GT)].to_broadcast([P, GT])).then_inc(s_c[g.p], 16)

            def stack_q(g):
                if not g.ok:
                    return
                wait(sp, b_done, g.times(16, -16))
                for part, ready in ((HI, q_hi), (MID, q_mid), (LO, q_lo)):
                    sp.wait_ge(ready, g.times(2, 2))
                    for r, have in enumerate(Q_ROWS):
                        if have == part:
                            sp.dma_start(q_st[g.p][r * DH:(r + 1) * DH, :, :], q_part[:, part, :, :]).then_inc(s_q[g.p], 16)

            def stack_k(g):
                if not g.ok:
                    return
                wait(sp, b_done, g.times(16, -16))
                sp.sem_inc(passed, 1)
                sp.dma_start(k_st[g.p][MASK_ROW:MASK_ROW + 1, :, :],
                             mask_bias[0:1, bass.ds(g.tok, GT)].unsqueeze(1).to_broadcast([1, HEADS, GT])).then_inc(s_k[g.p], 16)
                for part, ready in ((HI, k_hi), (MID, k_mid), (LO, k_lo)):
                    sp.wait_ge(ready, g.times(2, 2))
                    for r, have in enumerate(K_ROWS):
                        if have == part:
                            sp.dma_start(k_st[g.p][r * DH:(r + 1) * DH, :, :], k_part[:, part, :, :]).then_inc(s_k[g.p], 16)

            def residual(g):
                if g.ok:
                    wait(sp, x2_done, g.times(4, -4))
                    sp.sem_inc(passed, 1)
                    sp.dma_start(x_res[g.p][:], x[bass.ds(g.tok, GT), :].rearrange("(t p) d -> p t d", p=P)).then_inc(s_res[g.p], 16)

            def max_rows(b):
                if b.ok:
                    sp.wait_ge(nmid_done, b.times(1, 1))
                    for i in range(2):
                        r = MAX_ROW + i
                        sp.dma_start(q_st[b.group.p][r:r + 1, :, b.j * P:(b.j + 1) * P], neg_m[b.s % 2][:, i, :]).then_inc(s_m[b.s % 2], 16)

            def store_x2(g):
                if g.ok:
                    sp.wait_ge(x2_done, g.times(4, 4))
                    sp.sem_inc(passed, 1)
                    sp.dma_start(out[bass.ds(g.tok, GT), :].rearrange("(t p) d -> p t d", p=P), x2[g.p][:]).then_inc(s_out[g.p], 16)

            def store_scores(g):
                if g.ok:
                    sp.wait_ge(r_out, g.times(1, 1))
                    sp.sem_inc(passed, 1)
                    sp.dma_start(scores_t[:, bass.ds(g.tok, GT)], s_t[:]).then_inc(s_sc, 16)

            def store_rows(g):
                if g.ok:
                    sp.wait_ge(st_out, g.times(1, 1))
                    sp.sem_inc(passed, 1)
                    sp.dma_start(rows[bass.ds(g.tok, GT), :].rearrange("(t p) d -> p t d", p=P), row[g.p][:]).then_inc(s_row[g.p], 16)

            load_x(Group(0, 0, NG))
            load_const(wq_sb[:], square(wq), s_wq)
            load_const(bq_sb[:], bq, s_wq)
            load_c(Group(0, 0, NG))
            load_const(mask_nat[:], mask, s_misc)
            load_const(wk_sb[:], square(wk), s_wk)
            load_const(bk_sb[:], bk, s_wk)
            load_const(wv_sb[:], square(wv), s_wv)
            load_const(bv_sb[:], over_rows(bv), s_wv)
            load_x(Group(0, 1, NG))
            sp.wait_ge(s_ones, 1)
            for p in range(2):
                load_const(q_st[p][MASK_ROW:MASK_ROW + 1, :, :], ones_bf[:], s_rows1)
                for i in range(2):
                    load_const(k_st[p][MAX_ROW + i:MAX_ROW + i + 1, :, :], ones_bf[:], s_rows1)
            sp.wait_ge(s_bias, 1)
            sp.dma_start(mask_bias.rearrange("a (b s) -> (a b) s", s=P), bias_nat[:]).then_inc(s_bias_st, 16)
            sp.wait_ge(s_bias_st, 16)
            stack_q(Group(0, 0, NG))
            load_const(wg_sb[:], square(wg_t), s_misc)
            load_const(gx_raw[:], over_rows(g_x), s_misc)
            load_c(Group(0, 1, NG))
            stack_k(Group(0, 0, NG))

            def step(sp, b):
                g = b.group
                if b.j == 0:
                    residual(g)
                    load_x(g.on(2))
                    load_c(g.on(2))
                if b.j == 1:
                    store_x2(g.on(-2))
                if b.j == 2:
                    store_scores(g.on(-3))
                    stack_q(g.on(1))
                if b.j == 3:
                    store_rows(g.on(-3))
                    stack_k(g.on(1))
                max_rows(b.back(1))

            steps(sp, step)
            for p in range(2):
                sp.wait_ge(s_out[p], 16 * (NG // 2))
                sp.wait_ge(s_row[p], 16 * (NG // 2))
            sp.wait_ge(s_sc, 16 * NG)
            sp.wait_ge(s_rows1, 16 * 6)

        @block.gpsimd
        def _(pool):
            for p in range(2):
                pool.memset(v_aug[p][:], 0.0).then_inc(s_zero, 1)
            pool.memset(ident[:], 0.0).then_inc(w["s_id"], 1)
            pool.wait_ge(w["s_id"], 1)
            pool.affine_select(out=ident[:], in_=ident[:], compare_op=ALU.not_equal, fill=1.0, base=0,
                               pattern=[[-1, P]], channel_multiplier=1).then_inc(w["s_id"], 1)

            def rsqrt(c, var, v, y, t):
                c.link(pool.tensor_scalar(v[:], var, EPS, None, ALU.add))
                c.link(pool.tensor_scalar(y[:].bitcast(I32), v[:].bitcast(I32), -0.5, MAGIC, ALU.mult, ALU.add))
                for _ in range(3):
                    c.link(pool.tensor_tensor(t[:], y[:], y[:], ALU.mult))
                    c.link(pool.tensor_tensor(t[:], t[:], v[:], ALU.mult))
                    c.link(pool.tensor_scalar(t[:], t[:], -0.5, 1.5, ALU.mult, ALU.add))
                    c.link(pool.tensor_tensor(y[:], y[:], t[:], ALU.mult))

            def scales(c, mv, v, y, t, nm):
                rsqrt(c, mv[:, :, 1], v, y, t)
                c.link(pool.tensor_tensor(t[:], mv[:, :, 0], y[:], ALU.mult))
                c.link(pool.tensor_scalar(nm[:], t[:], -1.0, None, ALU.mult))
                assert c.n == LN_OPS

            def ln1(g):
                if g.ok:
                    pool.wait_ge(s_mv1, g.times(4, 4))
                    wait(pool, s_xn, g.times(4))
                    pool.sem_inc(passed, 1)
                    scales(Chain(pool, s_ln1, g.times(LN_OPS), passed), mv1, v1, y1, t1, nm1)

            def ln2_scales(g):
                if g.ok:
                    pool.wait_ge(mv2_done, g.times(4, 4))
                    wait(pool, xn2_done, g.times(4))
                    pool.sem_inc(passed, 1)
                    scales(Chain(pool, ln2, g.times(LN_OPS), passed), mv2[g.p], v2, y2, t2, nm2)

            def split_q(g, m):
                if g.ok:
                    pool.wait_ge(q_mid, g.times(2, m + 1))
                    pool.tensor_tensor(q_part[:, LO, m, :], q_rest[:, m, :], q_part[:, MID, m, :], ALU.subtract).then_inc(q_lo, 1)

            def rest_k(g, m):
                if g.ok:
                    pool.wait_ge(k_hi, g.times(2, m + 1))
                    pool.tensor_tensor(k_rest[:, m, :], k_val[:, m, :], k_part[:, HI, m, :], ALU.subtract).then_inc(k_r, 1)

            def split_k(g, m):
                if g.ok:
                    pool.wait_ge(k_mid, g.times(2, m + 1))
                    pool.tensor_tensor(k_part[:, LO, m, :], k_rest[:, m, :], k_part[:, MID, m, :], ALU.subtract).then_inc(k_lo, 1)

            ln1(Group(0, 0, NG))
            g = Group(0, 0, NG)
            for m in range(KD):
                split_q(g, m)
            for m in range(KD):
                rest_k(g, m)
                split_k(g, m)
            ln1(Group(0, 1, NG))

            def step(pool, b):
                g = b.group
                for m in range(KD):
                    if b.j == 1:
                        split_q(g.on(1), m)
                    if b.j == 2:
                        rest_k(g.on(1), m)
                        split_k(g.on(1), m)
                if b.j == 0:
                    ln2_scales(g.on(-2))
                if b.j == 1:
                    ln1(g.on(2))

            steps(pool, step)

        @block.scalar
        def _(act):
            def f_wait(g, u):
                act.wait_ge(f_done, g.times(8, u + 1))

            def xn_t_out(g, k):
                if g.ok:
                    f_wait(g, k)
                    act.activation(xn_t[:, k, :], f_bank(g, k)[:], ACT.Copy).then_inc(f_free[k], 1)

            def hi_q(g, m):
                if g.ok:
                    f_wait(g, 2 + m)
                    if m == 0:
                        last = g.on(-1)
                        wait(act, s_q[last.p], last.turn(Q_SENT, Q_SENT))
                    act.activation(q_part[:, HI, m, :], f_bank(g, m)[:], ACT.Identity, bias=bq_sb[:, m:m + 1]).then_inc(q_hi, 1)

            def mid_q(g, m):
                if g.ok:
                    act.wait_ge(f_free[m], g.times(4, 2))
                    act.activation(q_part[:, MID, m, :], q_rest[:, m, :], ACT.Copy).then_inc(q_mid, 1)

            def hi_k(g, m):
                if g.ok:
                    act.wait_ge(f_free[m], g.times(4, 3))
                    if m == 0:
                        last = g.on(-1)
                        wait(act, s_k[last.p], last.turn(K_SENT, K_SENT))
                    act.activation(k_part[:, HI, m, :], k_val[:, m, :], ACT.Copy).then_inc(k_hi, 1)

            def mid_k(g, m):
                if g.ok:
                    act.wait_ge(k_r, g.times(2, m + 1))
                    act.activation(k_part[:, MID, m, :], k_rest[:, m, :], ACT.Copy).then_inc(k_mid, 1)

            def normalise(g, ts):
                if g.ok:
                    act.wait_ge(s_ln1, g.times(LN_OPS, LN_OPS))
                    wait(act, f_done, g.times(8, -6))
                    act.wait_ge(s_x[g.p], g.turn(16, 16))
                    for t in ts:
                        act.activation(xn[:, t, :], x_in[g.p][:, t, :], ACT.Identity, bias=nm1[:, t:t + 1],
                                       scale=y1[:, t:t + 1]).then_inc(s_xn, 1)

            def exp(b, q):
                if b.ok:
                    act.wait_ge(b_done, b.times(4, q + 1))
                    if q == 0:
                        wait(act, pv_done, b.times(1, -1))
                    act.activation(p_t[b.s % 2][:, 4 * q:4 * q + 4, :], b_ps[q % 2][:].rearrange("p (h s) -> p h s", s=P),
                                   ACT.Exp, scale=SCALE).then_inc(exp_done, 1)

            def neg_hi(b):
                if b.ok:
                    act.wait_ge(mt_done, b.times(1, 1))
                    wait(act, s_m[b.s % 2], b.turn(2, 32))
                    act.activation(neg_m[b.s % 2][:, 0, :], m_ps[0:HEADS, 0:P], ACT.Copy, scale=-1.0).then_inc(nhi_done, 1)

            def pv_copy(b):
                if b.ok:
                    act.wait_ge(pv_done, b.times(1, 1))
                    wait(act, ot_done, b.times(1, -1))
                    act.activation(o_t[b.s % 2][:], pv_ps[:].rearrange("p (a s) -> p a s", s=P), ACT.Copy).then_inc(pv_out, 1)

            def normalise2(g, ts):
                if g.ok:
                    act.wait_ge(ln2, g.times(LN_OPS, LN_OPS))
                    wait(act, s_row[g.p], g.turn(16))
                    for t in ts:
                        act.activation(row[g.p][:, t, 0:D], x2[g.p][:, t, :], ACT.Identity, bias=nm2[:, t:t + 1],
                                       scale=y2[:, t:t + 1]).then_inc(xn2_done, 1)

            def xt2_copy(g, k):
                if g.ok:
                    act.wait_ge(xt2_done, g.times(2, k + 1))
                    wait(act, r_done, g.times(1))
                    act.activation(xn2_t[:, k, :], o_ps[:], ACT.Copy).then_inc(xt2_out, 1)

            def router_out(g):
                if g.ok:
                    act.wait_ge(r_done, g.times(1, 1))
                    wait(act, s_sc, g.times(16))
                    wait(act, st_done, g.times(1))
                    act.activation(s_t[:], o_ps[0:E, :], ACT.Copy).then_inc(r_out, 1)

            act.wait_ge(s_wq, 32)
            g = Group(0, 0, NG)
            normalise(g, range(GB))
            for k in range(KD):
                xn_t_out(g, k)
            for m in range(KD):
                hi_q(g, m)
                mid_q(g, m)
            for m in range(KD):
                hi_k(g, m)
                mid_k(g, m)
            normalise(Group(0, 1, NG), range(GB))
            act.wait_ge(s_misc, 16 * 3)
            act.activation(gx[:], gx_raw[:], ACT.Tanh).then_inc(s_gx, 1)

            def step(act, b):
                g, f = b.group, b.group.on(1)
                exp(b.back(2), 0)
                if b.j == 0:
                    xt2_copy(g.on(-3), 1)
                if b.j == 1:
                    router_out(g.on(-3))
                if b.j == 3:
                    xt2_copy(g.on(-2), 0)
                neg_hi(b.back(1))
                if b.j == 0:
                    xn_t_out(f, 0)
                if b.j == 1:
                    hi_q(f, 0)
                if b.j == 2:
                    hi_k(f, 0)
                    normalise2(g.on(-2), (0, 1))
                if b.j == 3:
                    normalise(g.on(2), (0, 1))
                exp(b.back(2), 1)
                if b.j == 1:
                    mid_q(f, 0)
                if b.j == 2:
                    mid_k(f, 0)
                exp(b.back(2), 2)
                if b.j == 0:
                    xn_t_out(f, 1)
                if b.j == 1:
                    hi_q(f, 1)
                if b.j == 2:
                    hi_k(f, 1)
                    normalise2(g.on(-2), (2, 3))
                if b.j == 3:
                    normalise(g.on(2), (2, 3))
                exp(b.back(2), 3)
                if b.j == 1:
                    mid_q(f, 1)
                if b.j == 2:
                    mid_k(f, 1)
                pv_copy(b.back(3))

            steps(act, step)

        @block.vector
        def _(dve):
            dve.memset(ones_bf[:], 1.0).then_inc(s_ones, 1)

            def stats(g, ts):
                if not g.ok:
                    return
                dve.wait_ge(s_x[g.p], g.turn(16, 16))
                wait(dve, s_ln1, g.times(LN_OPS))
                for t in ts:
                    dve.bn_stats(stats1[:, t, :], x_in[g.p][:, t, :]).then_inc(s_st1, 1)
                dve.wait_ge(s_st1, g.times(4, ts[-1] + 1))
                dve.sem_inc(passed, 1)
                for t in ts:
                    dve.bn_aggr(mv1[:, t, :], stats1[:, t, :]).then_inc(s_mv1, 1)

            def rest_q(g, m):
                if g.ok:
                    dve.wait_ge(q_hi, g.times(2, m + 1))
                    wait(dve, q_lo, g.times(2, m - 1))
                    dve.scalar_tensor_tensor(out=q_rest[:, m, :], in0=f_bank(g, m)[:], scalar=bq_sb[:, m:m + 1],
                                             in1=q_part[:, HI, m, :], op0=ALU.add, op1=ALU.subtract).then_inc(f_free[m], 1)

            def make_k(g, m):
                if g.ok:
                    dve.wait_ge(f_done, g.times(8, 5 + m))
                    dve.wait_ge(s_c[g.p], g.turn(32, 32))
                    wait(dve, k_r, g.times(2, m - 1))
                    dve.scalar_tensor_tensor(out=k_val[:, m, :], in0=f_bank(g, m)[:], scalar=bk_sb[:, m:m + 1],
                                             in1=mask_b[g.p][:], op0=ALU.add, op1=ALU.mult).then_inc(f_free[m], 1)

            def make_v(g, i):
                if g.ok:
                    dve.wait_ge(f_done, g.times(8, 7 + i))
                    if i == 0:
                        wait(dve, pv_done, g.times(4, -4))
                    for t in range(2):
                        ins = dve.tensor_tensor(v_aug[g.p][:, 2 * i + t, :, 0:DH],
                                                f_bank(g, i)[:, t * D:(t + 1) * D].rearrange("p (h d) -> p h d", d=DH),
                                                bv_sb[:].rearrange("p (h d) -> p h d", d=DH), ALU.add)
                    ins.then_inc(f_free[i], 1)

            def maximum(b, q):
                if b.ok:
                    dve.wait_ge(a_done, b.times(4, q + 1))
                    if q == 0:
                        wait(dve, mt_done, b.times(1, -1))
                    dve.tensor_reduce(m_sb[b.s % 2][:, 4 * q:4 * q + 4], a_ps[q % 2][:].rearrange("p (h s) -> p h s", s=P),
                                      AX_X, ALU.max).then_inc(max_done, 1)

            def row_scores(g):
                if g.ok:
                    dve.wait_ge(st_done, g.times(1, 1))
                    dve.tensor_copy(row[g.p][:, :, D:ROW], o_ps[:, 0:GB * E].rearrange("p (t e) -> p t e", e=E)).then_inc(st_out, 1)

            def neg_mid(b):
                if b.ok:
                    dve.wait_ge(nhi_done, b.times(1, 1))
                    dve.scalar_tensor_tensor(out=neg_m[b.s % 2][:, 1, :], in0=m_ps[0:HEADS, 0:P], scalar=-1.0,
                                             in1=neg_m[b.s % 2][:, 0, :], op0=ALU.mult, op1=ALU.subtract).then_inc(nmid_done, 1)

            def finish(b):
                if not b.ok:
                    return
                dve.wait_ge(ot_done, b.times(1, 1))
                o = o_ps[:].rearrange("p (h v) -> p h v", v=VW)
                wait(dve, ot_out, b.times(1))
                dve.reciprocal(rden[:], o[:, :, DH]).then_inc(rd_done, 1)
                dve.wait_ge(rd_done, b.times(1, 1))
                wait(dve, x2_done, b.times(1))
                dve.tensor_tensor(o_n[:].rearrange("p (h d) -> p h d", d=DH), o[:, :, 0:DH],
                                  rden[:].unsqueeze(2).to_broadcast([P, HEADS, DH]), ALU.mult).then_inc(ot_out, 1)
                dve.wait_ge(ot_out, b.times(1, 1))
                g = b.group
                dve.wait_ge(s_res[g.p], g.turn(16, 16))
                if b.j == 0:
                    wait(dve, s_out[g.p], g.turn(16))
                    wait(dve, xn2_done, g.times(4, -4))
                dve.scalar_tensor_tensor(out=x2[g.p][:, b.j, :], in0=o_n[:], scalar=gx[:, 0:1], in1=x_res[g.p][:, b.j, :],
                                         op0=ALU.mult, op1=ALU.add).then_inc(x2_done, 1)
                dve.wait_ge(x2_done, b.times(1, 1))
                wait(dve, mv2_done, b.times(1))
                dve.bn_stats(stats2[:], x2[g.p][:, b.j, :]).then_inc(st2_done, 1)
                dve.wait_ge(st2_done, b.times(1, 1))
                wait(dve, ln2, g.times(LN_OPS, -LN_OPS))
                dve.sem_inc(passed, 1)
                dve.bn_aggr(mv2[g.p][:, b.j, :], stats2[:]).then_inc(mv2_done, 1)

            g = Group(0, 0, NG)
            stats(g, range(GB))
            dve.wait_ge(s_zero, 2)
            for p in range(2):
                dve.memset(v_aug[p][:, :, :, DH:DH + 1], 1.0).then_inc(s_zero, 1)
            dve.wait_ge(s_misc, 16)
            dve.tensor_scalar(bias_nat[:], mask_nat[:], -1.0, MASKED, ALU.add, ALU.mult).then_inc(s_bias, 1)
            dve.wait_ge(s_wq, 32)
            for m in range(KD):
                rest_q(g, m)
            dve.wait_ge(s_wk, 32)
            dve.wait_ge(s_wv, 32)
            for m in range(KD):
                make_k(g, m)
            for i in range(2):
                make_v(g, i)
            stats(Group(0, 1, NG), range(GB))
            dve.wait_ge(s_gx, 1)

            def step(dve, b):
                f = b.group.on(1)
                maximum(b, 0)
                if b.j == 2:
                    row_scores(b.group.on(-3))
                neg_mid(b.back(1))
                if b.j == 1:
                    rest_q(f, 0)
                if b.j == 2:
                    make_k(f, 0)
                if b.j == 3:
                    make_v(f, 0)
                maximum(b, 1)
                if b.j == 1:
                    stats(b.group.on(2), range(GB))
                maximum(b, 2)
                finish(b.back(4))
                if b.j == 1:
                    rest_q(f, 1)
                if b.j == 2:
                    make_k(f, 1)
                if b.j == 3:
                    make_v(f, 1)
                maximum(b, 3)

            steps(dve, step)

        @block.tensor
        def _(pe):
            pe.wait_ge(w["s_id"], 2)

            def front(g, u):
                if not g.ok:
                    return
                i = u % 2
                ps = f_bank(g, i)
                if isinstance(g.k, int) and g.k + g.p == 0:
                    wait(pe, f_free[i], u // 2)
                elif u == 0:
                    wait(pe, f_free[0], g.times(4))
                    wait(pe, f_free[1], g.times(4))
                else:
                    pe.wait_ge(f_free[1 - i], g.times(4, (u - 1) // 2 + 1))
                if u < 2:
                    pe.wait_ge(s_xn, g.times(4, 4))
                    for t in range(GB):
                        mm = pe.transpose(ps[:, t * P:(t + 1) * P], xn[:, t, u * P:(u + 1) * P], ident[:])
                elif u < 6:
                    wt, src = (wq_sb, xn_t) if u < 4 else (wk_sb, c_t[g.p])
                    if isinstance(g.k, int):
                        pe.wait_ge(*((s_wq, 32) if u < 4 else (s_wk, 32)))
                    if u < 4:
                        pe.wait_ge(f_free[0], g.times(4, 1))
                        pe.wait_ge(f_free[1], g.times(4, 1))
                    else:
                        pe.wait_ge(s_c[g.p], g.turn(32, 32))
                    for k in range(KD):
                        mm = pe.matmul(ps[:], wt[:, k, i * P:(i + 1) * P], src[:, k, :], start=(k == 0), stop=(k == KD - 1))
                else:
                    if isinstance(g.k, int):
                        pe.wait_ge(s_wv, 32)
                    for t in range(2):
                        tok = (2 * (u - 6) + t) * P
                        for k in range(KD):
                            mm = pe.matmul(ps[:, t * D:(t + 1) * D], c_t[g.p][:, k, tok:tok + P], wv_sb[:, k, :],
                                           start=(k == 0), stop=(k == KD - 1))
                mm.then_inc(f_done, 1)

            def scores(b, q):
                if not b.ok:
                    return
                g = b.group
                if q == 0 and b.j == 0:
                    pe.wait_ge(s_q[g.p], g.turn(Q_SENT, Q_SENT))
                    pe.wait_ge(s_k[g.p], g.turn(K_SENT, K_SENT))
                wait(pe, max_done, b.times(4, q - 1))
                for i in range(4):
                    h, tok = 4 * q + i, slice(b.j * P, (b.j + 1) * P)
                    mm = pe.matmul(a_ps[q % 2][:, i * P:(i + 1) * P], q_st[g.p][0:A_K, h, tok], k_st[g.p][0:A_K, h, tok],
                                   start=True, stop=True)
                mm.then_inc(a_done, 1)

            def scores_t_(b, q):
                if not b.ok:
                    return
                g = b.group
                if q == 0:
                    pe.wait_ge(s_m[b.s % 2], b.turn(2, 32, 32))
                wait(pe, exp_done, b.times(4, q - 1))
                for i in range(4):
                    h, tok = 4 * q + i, slice(b.j * P, (b.j + 1) * P)
                    mm = pe.matmul(b_ps[q % 2][:, i * P:(i + 1) * P], k_st[g.p][0:B_K, h, tok], q_st[g.p][0:B_K, h, tok],
                                   start=True, stop=True)
                mm.then_inc(b_done, 1)

            def values(b, q):
                if not b.ok:
                    return
                if q == 0:
                    pe.wait_ge(f_free[1], b.group.times(4, 4))
                    pe.wait_ge(f_free[0], b.group.times(4, 4))
                    wait(pe, pv_out, b.times(1))
                pe.wait_ge(exp_done, b.times(4, q + 1))
                for i in range(4):
                    h = 4 * q + i
                    mm = pe.matmul(pv_ps[VW * i:VW * (i + 1), q * P:(q + 1) * P], v_aug[b.group.p][:, b.j, h, :],
                                   p_t[b.s % 2][:, h, :], start=True, stop=True)
                if q == 3:
                    mm.then_inc(pv_done, 1)

            def router(g, at):
                if g.ok:
                    o_free(pe, *at)
                    pe.wait_ge(xt2_out, g.times(2, 2))
                    for k in range(KD):
                        mm = pe.matmul(o_ps[0:E, :], wg_sb[:, k, :], xn2_t[:, k, :], start=(k == 0), stop=(k == KD - 1))
                    mm.then_inc(r_done, 1)

            def scores_back(g, at):
                if g.ok:
                    o_free(pe, *at)
                    pe.wait_ge(r_out, g.times(1, 1))
                    pe.sem_inc(passed, 1)
                    for t in range(GB):
                        mm = pe.transpose(o_ps[:, t * E:(t + 1) * E], s_t[:, t * P:(t + 1) * P], ident[0:E, 0:E])
                    mm.then_inc(st_done, 1)

            def max_t(b):
                use = b.back(1)
                if use.ok:
                    if isinstance(use.k, int) and use.k + use.s == 0:
                        pe.wait_ge(f_free[1], 4)
                    wait(pe, nmid_done, use.times(1))
                    pe.wait_ge(max_done, use.times(4, 4))
                    pe.transpose(m_ps[0:HEADS, 0:P], m_sb[use.s % 2][:], ident[:]).then_inc(mt_done, 1)

            def out_back(b):
                use = b.back(4)
                if use.ok:
                    o_free(pe, b.group, 1, b.j)
                    pe.wait_ge(pv_out, use.times(1, 1))
                    for a in range(4):
                        mm = pe.transpose(o_ps[:, a * P:(a + 1) * P], o_t[use.s % 2][:, a, :], ident[:])
                    mm.then_inc(ot_done, 1)

            def xn2_back(g, k, at):
                if g.ok:
                    o_free(pe, *at)
                    pe.wait_ge(xn2_done, g.times(4, 4))
                    for t in range(GB):
                        mm = pe.transpose(o_ps[:, t * P:(t + 1) * P], row[g.p][:, t, k * P:(k + 1) * P], ident[:])
                    mm.then_inc(xt2_done, 1)

            for u in range(8):
                front(Group(0, 0, NG), u)
            pe.wait_ge(s_rows1, 16 * 6)
            pe.wait_ge(s_zero, 4)
            pe.wait_ge(s_misc, 16 * 3)

            def step(pe, b):
                g = b.group
                for q in range(4):
                    scores(b, q)
                    if (b.j, q) == (3, 0):
                        xn2_back(g.on(-2), 0, (g, q, b.j))
                    if (b.j, q) == (0, 0):
                        xn2_back(g.on(-3), 1, (g, q, b.j))
                    if (b.j, q) == (1, 0):
                        router(g.on(-3), (g, q, b.j))
                    if (b.j, q) == (2, 0):
                        scores_back(g.on(-3), (g, q, b.j))
                    if q == 1:
                        out_back(b)
                    scores_t_(b.back(2), q)
                    if q == 1:
                        values(b.back(3), 0)
                    if q >= 1:
                        values(b.back(3), q)
                    if q % 2 == 0:
                        front(g.on(1), 2 * b.j + q // 2)
                    if q == 0:
                        max_t(b)

            steps(pe, step)


CHUNKS = P // E
BISECTIONS = 32
BIG = 1e30


def select(nc, ctx, w, rows, scores_t, thr, idx_all, neg_top):
    n_tok = scores_t.shape[1]
    CAP = n_tok // E
    ST = CAP // P
    T = n_tok // P
    TP = 2 * T
    EP = E // 2

    def sb(name, shape, dt=F32):
        return ctx.enter_context(nc.sbuf_tensor(name, shape, dt))

    def sem(name):
        return ctx.enter_context(nc.semaphore(name))

    def bank(name, dt=F32):
        return ctx.enter_context(nc.psum_tensor(name, [P, 512], dt))

    sc = sb("sc", [P, n_tok // CHUNKS])
    ts = sb("ts", [TP, EP, P])
    same, before, group = sb("same", [P, P]), sb("before", [TP, TP]), sb("group", [TP, TP])
    slot = sb("slot", [P, CAP])
    slot_of = sb("slot_of", [P, ST])
    ones_row, ones = sb("ones_row", [1, P]), sb("ones", [TP, P])
    part_max, bound = sb("part_max", [P, 1]), sb("bound", [P, 1])
    junk = sb("junk", [P, n_tok // CHUNKS])
    lo_hi, t, cnt, u, u2 = sb("lo_hi", [P, 2]), sb("t", [P, 1]), sb("cnt", [P, 1]), sb("u", [P, 1]), sb("u2", [P, 1])
    top = sb("top", [1, E])
    th = sb("th", [TP, EP, 2])
    above, tied, place = sb("above", [TP, EP, P]), sb("tied", [TP, EP, P]), sb("place", [TP, EP, P])
    n_above, left = sb("n_above", [TP, EP]), sb("left", [TP, EP])
    chosen, count = sb("chosen", [TP, EP, P]), sb("count", [TP, EP, P])
    start, end = sb("start", [TP, EP]), sb("end", [TP, EP])
    upto = sb("upto", [TP, EP, P + 1], FP16)
    tile_no = sb("tile_no", [TP, 1])
    under, hot = sb("under", [TP, EP, CAP], FP16), sb("hot", [TP, EP, CAP], FP16)
    cnt_junk = [sb(f"cnt_junk{i}", [P, P]) for i in range(2)]
    pos = sb("pos", [P, E * ST])

    tot_ps, small_ps = bank("tot_ps"), bank("small_ps")
    g_ps = [bank(f"g_ps{i}") for i in range(4)]

    s_sc, s_ts, s_e = sem("s_sc2"), sem("s_ts"), sem("s_e2")
    s_pm, s_bound = sem("s_pm"), sem("s_bound")
    s_top_t, s_top, s_top_b = sem("s_top_t"), sem("s_top"), sem("s_top_b")
    s_count, s_tot, s_thr = sem("s_count"), sem("s_tot"), sem("s_thr")
    s_found, s_thr_st, s_th = sem("s_found"), sem("s_thr_st"), sem("s_th")
    d = sem("d_chain")
    s_tie, s_left, s_sel, s_start, s_hot = sem("s_tie"), sem("s_left"), sem("s_sel"), sem("s_start"), sem("s_hot")
    s_pick, s_pos = sem("s_pick"), sem("s_pos")
    passed = w["passed"]

    with nc.Block() as block:

        @block.sync
        def _(sp):
            sp.dma_start(sc[:], scores_t.rearrange("e (c n) -> (e c) n", c=CHUNKS)).then_inc(s_sc, 16)
            by_tile = scores_t.rearrange("(a b) (t s) -> b t a s", b=2, s=P)
            for b in range(2):
                sp.dma_start(ts[b * T:(b + 1) * T, :, :], by_tile[b]).then_inc(s_ts, 16)
            sp.wait_ge(s_found, 1)
            sp.dma_start(thr, lo_hi[:]).then_inc(s_thr_st, 16)
            sp.wait_ge(s_thr_st, 16)
            by_expert = thr.rearrange("(a b c) n -> b c a n", b=2, c=CHUNKS)
            for b in range(2):
                sp.dma_start(th[b * T:(b + 1) * T, :, :], by_expert[b][0:1].to_broadcast([T, EP, 2])).then_inc(s_th, 16)
            sp.wait_ge(s_th, 32)

        @block.gpsimd
        def _(pool):
            c = Chain(pool, s_e)
            c.link(pool.memset(same[:], 1.0))
            v = same[:].rearrange("p (e c) -> p e c", c=CHUNKS)
            c.link(pool.affine_select(out=v, in_=v, compare_op=ALU.is_ge, fill=0.0, base=0,
                                      pattern=[[-CHUNKS, E], [0, CHUNKS]], channel_multiplier=1))
            c.link(pool.affine_select(out=v, in_=v, compare_op=ALU.is_ge, fill=0.0, base=CHUNKS - 1,
                                      pattern=[[CHUNKS, E], [0, CHUNKS]], channel_multiplier=-1))
            c.link(pool.memset(group[:], 1.0))
            c.link(pool.affine_select(out=group[:, 0:T], in_=group[:, 0:T], compare_op=ALU.is_ge, fill=0.0,
                                      base=T - 1, pattern=[[0, T]], channel_multiplier=-1))
            c.link(pool.affine_select(out=group[:, T:TP], in_=group[:, T:TP], compare_op=ALU.is_ge, fill=0.0,
                                      base=-T, pattern=[[0, T]], channel_multiplier=1))
            c.link(pool.affine_select(out=before[:], in_=group[:], compare_op=ALU.is_ge, fill=0.0, base=-1,
                                      pattern=[[1, TP]], channel_multiplier=-1))
            c.link(pool.iota(slot[:], [[1, CAP]], base=0, channel_multiplier=0, allow_small_or_imprecise_dtypes=True))
            c.link(pool.iota(slot_of[:], [[P, ST]], base=0, channel_multiplier=1, allow_small_or_imprecise_dtypes=True))
            for b in range(2):
                c.link(pool.iota(tile_no[b * T:(b + 1) * T, :], [[0, 1]], base=0, channel_multiplier=P,
                                 allow_small_or_imprecise_dtypes=True))
            c.link(pool.memset(ones_row[:], 1.0))
            c.link(pool.memset(ones[:], 1.0))
            pool.wait_ge(s_pm, 2)
            pool.partition_all_reduce(bound[:], junk[:, 0:1], P, bass.bass_isa.ReduceOp.max).then_inc(s_bound, 1)

        @block.vector
        def _(dve):
            dve.wait_ge(s_sc, 16)
            dve.tensor_reduce(part_max[:], sc[:], AX_X, ALU.max).then_inc(s_pm, 1)
            dve.tensor_reduce(junk[:, 0:1], sc[:], AX_X, ALU.max, apply_absolute_value=True).then_inc(s_pm, 1)
            dve.wait_ge(s_bound, 1)
            c = Chain(dve, s_thr)
            c.link(dve.tensor_scalar(lo_hi[:, 1:2], bound[:], 2.0, 1.0 / BIG, ALU.mult, ALU.add))
            c.link(dve.tensor_scalar(lo_hi[:, 0:1], lo_hi[:, 1:2], -1.0, None, ALU.mult))
            lo, hi = lo_hi[:, 0:1], lo_hi[:, 1:2]
            with dve.Fori(0, BISECTIONS, 1) as i:
                dve.wait_ge(s_thr, i * 5 + 2)
                dve.tensor_scalar(t[:], lo, hi, 0.5, ALU.add, ALU.mult).then_inc(s_thr, 1)
                dve.wait_ge(s_thr, i * 5 + 3)
                dve.tensor_scalar(junk[:], sc[:], t[:, 0:1], 0.0, ALU.is_ge, ALU.add, accum_out=cnt[:]).then_inc(s_count, 1)
                dve.wait_ge(s_tot, i + 1)
                dve.tensor_scalar(u[:], tot_ps[:, 0:1], float(CAP), BIG, ALU.is_ge, ALU.mult).then_inc(s_thr, 1)
                dve.tensor_scalar(u2[:], tot_ps[:, 0:1], float(CAP), -BIG, ALU.is_lt, ALU.mult).then_inc(s_thr, 1)
                dve.wait_ge(s_thr, i * 5 + 5)
                dve.scalar_tensor_tensor(out=hi, in0=u[:], scalar=t[:, 0:1], in1=hi, op0=ALU.add, op1=ALU.min).then_inc(s_thr, 1)
                dve.scalar_tensor_tensor(out=lo, in0=u2[:], scalar=t[:, 0:1], in1=lo, op0=ALU.add, op1=ALU.max).then_inc(s_thr, 1)
            dve.wait_ge(s_thr, 5 * BISECTIONS + 2)
            dve.wait_ge(s_count, BISECTIONS)
            dve.tensor_copy(u[:], lo).then_inc(s_found, 1)
            dve.wait_ge(s_top_t, 1)
            dve.tensor_reduce(top[:], small_ps[0:1, 0:P].rearrange("p (e c) -> p e c", c=CHUNKS), AX_X, ALU.max,
                              negate=True).then_inc(s_top, 1)
            dve.wait_ge(s_top_b, 1)
            dve.tensor_copy(neg_top[:], small_ps[:, 0:E]).then_inc(s_top, 1)
            c = Chain(dve, d)
            dve.wait_ge(s_ts, 32)
            dve.wait_ge(s_th, 32)
            dve.wait_ge(s_e, 13)
            wide = [TP, EP, P]
            c.link(dve.tensor_tensor(above[:], ts[:], th[:, :, 1:2].to_broadcast(wide), ALU.is_ge))
            c.link(dve.tensor_tensor(tied[:], ts[:], th[:, :, 0:1].to_broadcast(wide), ALU.is_ge))
            c.link(dve.tensor_tensor(tied[:], tied[:], above[:], ALU.subtract))
            c.link(dve.tensor_reduce(n_above[:], above[:], AX_X, ALU.add))
            for a in range(EP):
                ins = dve.tensor_tensor_scan(place[:, a, :], ones[:], tied[:, a, :], 0.0, ALU.mult, ALU.add)
                ins.then_inc(s_tie, 1)
            dve.wait_ge(s_tie, EP)
            dve.wait_ge(s_left, 1)
            c.link(dve.tensor_scalar(left[:], small_ps[0:TP, 0:EP], float(CAP), None, ALU.subtract))
            c.link(dve.tensor_tensor(place[:], place[:], left[:].unsqueeze(2).to_broadcast(wide), ALU.add))
            c.link(dve.scalar_tensor_tensor(out=chosen[:], in0=place[:], scalar=0.0, in1=tied[:], op0=ALU.is_le, op1=ALU.mult))
            c.link(dve.tensor_tensor(chosen[:], chosen[:], above[:], ALU.add))
            for a in range(EP):
                dve.tensor_tensor_scan(count[:, a, :], ones[:], chosen[:, a, :], 0.0, ALU.mult, ALU.add).then_inc(s_sel, 1)
            dve.wait_ge(s_sel, EP)
            dve.wait_ge(s_start, 1)
            c.link(dve.tensor_copy(start[:], small_ps[0:TP, 0:EP]))
            c.link(dve.tensor_tensor(end[:], start[:], count[:, :, P - 1], ALU.add))
            c.link(dve.tensor_tensor(upto[:, :, 0:P], count[:], start[:].unsqueeze(2).to_broadcast(wide), ALU.add))
            c.link(dve.tensor_copy(upto[:, :, P:P + 1], tile_no[:].unsqueeze(1).to_broadcast([TP, EP, 1])))
            for a in range(EP):
                c.link(dve.tensor_scalar(under[:, a, :], slot[0:TP, :], end[:, a:a + 1], None, ALU.is_lt))
                dve.scalar_tensor_tensor(out=hot[:, a, :], in0=slot[0:TP, :], scalar=start[:, a:a + 1], in1=under[:, a, :],
                                         op0=ALU.is_ge, op1=ALU.mult).then_inc(s_hot, 1)
            for n in range(E * ST):
                dve.wait_ge(s_pick, n + 1)
                if n >= 2:
                    dve.wait_ge(s_pos, n - 1)
                dve.tensor_scalar(cnt_junk[n % 2][:], g_ps[n % 4][:, 0:P], slot_of[:, n % ST:n % ST + 1], g_ps[n % 4][:, P:P + 1],
                                  ALU.is_le, ALU.add, accum_out=pos[:, n:n + 1]).then_inc(s_pos, 1)
            dve.wait_ge(s_pos, E * ST)
            dve.tensor_copy(idx_all[:], pos[:]).then_inc(s_pos, 1)

        @block.tensor
        def _(pe):
            pe.wait_ge(s_e, 13)
            pe.wait_ge(s_pm, 1)
            pe.transpose(small_ps[0:1, 0:P], part_max[:], w["ident"][:]).then_inc(s_top_t, 1)
            with pe.Fori(0, BISECTIONS, 1) as i:
                pe.wait_ge(s_count, i + 1)
                pe.matmul(tot_ps[:, 0:1], same[:], cnt[:], start=True, stop=True).then_inc(s_tot, 1)
            pe.wait_ge(s_top, 1)
            pe.matmul(small_ps[:, 0:E], ones_row[:], top[:], start=True, stop=True).then_inc(s_top_b, 1)
            pe.wait_ge(s_top, 2)
            pe.wait_ge(d, 4)
            pe.wait_ge(s_tie, EP)
            pe.matmul(small_ps[0:TP, 0:EP], group[:], n_above[:], start=True, stop=False)
            pe.matmul(small_ps[0:TP, 0:EP], before[:], place[:, :, P - 1], start=False, stop=True).then_inc(s_left, 1)
            pe.wait_ge(s_sel, EP)
            pe.matmul(small_ps[0:TP, 0:EP], before[:], count[:, :, P - 1], start=True, stop=True).then_inc(s_start, 1)
            for n in range(E * ST):
                e, st = n // ST, n % ST
                a, rows_ = e // 2, slice((e % 2) * T, (e % 2 + 1) * T)
                if st == 0 and e % 2 == 0:
                    pe.wait_ge(s_hot, a + 1)
                if n >= 4:
                    pe.wait_ge(s_pos, n - 3)
                pe.matmul(g_ps[n % 4][:, 0:P + 1], hot[rows_, a, st * P:(st + 1) * P], upto[rows_, a, :],
                          start=True, stop=True).then_inc(s_pick, 1)


def experts(nc, ctx, w, rows, idx_all, neg_top, g_f, w1_t, w3_t, w2_t, out):
    CAP = out.shape[0] // E
    ST = CAP // P
    HT = max(1, CAP // 512)
    SPAN = CAP // HT
    TT = SPAN // P
    FT = F // P

    def sb(name, shape, dt=F32):
        return ctx.enter_context(nc.sbuf_tensor(name, shape, dt))

    def sem(name):
        return ctx.enter_context(nc.semaphore(name))

    def bank(name, dt=F32):
        return ctx.enter_context(nc.psum_tensor(name, [P, 512], dt))

    gf_raw, gf, ones = sb("gf_raw", [P, 1]), sb("gf", [P, 1]), sb("ones3", [P, P])
    w1 = [sb(f"w1_{p}", [P, KD, F]) for p in range(2)]
    w3 = [sb(f"w3_{p}", [P, KD, F]) for p in range(2)]
    w2 = [sb(f"w2_{p}", [P, FT, D]) for p in range(2)]
    idx = [sb(f"idx{p}", [P, ST], U32) for p in range(2)]
    xg = [sb(f"xg{p}", [P, ST, ROW]) for p in range(2)]
    xg_t = [sb(f"xg_t{p}", [P, KD, CAP]) for p in range(2)]
    raw_s, top_e, e_s, sum_s, inv = sb("raw_s", [P, ST]), sb("top_e", [P, 1]), sb("e_s", [P, ST]), sb("sum_s", [P, 1]), sb("inv", [P, 1])
    weight = [sb(f"weight{p}", [P, ST]) for p in range(2)]
    act_h = [sb(f"act_h{i}", [P, SPAN]) for i in range(2)]
    hid = [sb(f"hid{i}", [P, FT, SPAN]) for i in range(HT)]
    y = [sb(f"y_{i}", [P, D]) for i in range(ST)]

    t_ps = [bank(f"t_ps{i}") for i in range(2)]
    h1_ps, h3_ps = [bank(f"h1_ps{i}") for i in range(2)], [bank("h3_ps0")]
    y_ps = [bank(f"y_ps{i}") for i in range(2)]
    z_ps = bank("z_ps")

    s_g, s_gf, s_one = sem("s_g3"), sem("s_gf"), sem("s_one3")
    s_w = [sem(f"s_w{p}") for p in range(2)]
    s_idx, s_xg = sem("s_idx"), [sem(f"s_xg{p}") for p in range(2)]
    t_done, t_out = sem("t_done"), sem("t_out")
    s_raw, s_es, z_done, s_inv, s_wt = sem("s_raw"), sem("s_es"), sem("z_done"), sem("s_inv"), sem("s_wt")
    h1_done, h3_done, silu_done, hid_done = sem("h1_done"), sem("h3_done"), sem("silu_done"), sem("hid_done")
    y_done, y_out = sem("y_done"), sem("y_out")
    s_add = [sem(f"s_add{i}") for i in range(ST)]
    passed = w["passed"]
    TRANS = KD * HT
    HID = HT * FT

    class Expert:

        def __init__(self, k, p):
            self.k, self.p = k + p // 2, p % 2

        def on(self, n):
            return Expert(self.k, self.p + n)

        @property
        def ok(self):
            return not isinstance(self.k, int) or 0 <= 2 * self.k + self.p < E

        def times(self, n, more=0):
            return self.k * (2 * n) + (self.p * n + more)

        def turn(self, n, more=0):
            return self.k * n + more

    def over(eng, step):
        for p in range(2):
            step(Expert(0, p))
        with eng.Fori(1, E // 2 - 1, 1) as k:
            for p in range(2):
                step(Expert(k, p))
        for p in range(2):
            step(Expert(E // 2 - 1, p))

    with nc.Block() as block:

        @block.sync
        def _(sp):
            sp.dma_start(gf_raw[:], g_f.rearrange("(a n) -> a n", a=1).to_broadcast([P, 1])).then_inc(s_g, 16)

            def load(e):
                if not e.ok:
                    return
                wait(sp, y_done, e.times(ST, -ST))
                sp.sem_inc(passed, 1)
                i = e.times(1)
                for dst, src, n in ((w1, w1_t, F), (w3, w3_t, F), (w2, w2_t, D)):
                    view = src.rearrange("e (k p) n -> p e k n", p=P)
                    view = view[:, i] if isinstance(i, int) else view[:, bass.ds(i, 1)].rearrange("p e k n -> p (e k) n")
                    sp.dma_start(dst[e.p][:], view).then_inc(s_w[e.p], 16)

            load(Expert(0, 0))
            load(Expert(0, 1))
            over(sp, lambda e: load(e.on(2)))
            for p in range(2):
                sp.wait_ge(s_w[p], 48 * E // 2)

        @block.gpsimd
        def _(pool):
            def gather(e):
                if not e.ok:
                    return
                wait(pool, s_idx, e.times(1, 1))
                wait(pool, t_done, e.times(TRANS, -TRANS))
                wait(pool, s_raw, e.times(1, -1))
                pool.sem_inc(passed, 1)
                for st in range(ST):
                    pool.indirect_dma_start(xg[e.p][:, st, :], None, rows[:, :],
                                            bass.IndirectOffsetOnAxis(ap=idx[e.p][:, st:st + 1], axis=0)).then_inc(s_xg[e.p], 16)

            def add(e):
                for st in range(ST):
                    wait(pool, s_add[st], e.times(16))
                for st in range(ST):
                    pool.wait_ge(y_out, e.times(ST, st + 1))
                    pool.sem_inc(passed, 1)
                    pool.indirect_dma_start(out[:, :], bass.IndirectOffsetOnAxis(ap=idx[e.p][:, st:st + 1], axis=0),
                                            y[st][:], None, compute_op=ALU.add).then_inc(s_add[st], 16)

            gather(Expert(0, 0))

            def step(e):
                gather(e.on(1))
                add(e)

            over(pool, step)
            for st in range(ST):
                pool.wait_ge(s_add[st], 16 * E)

        @block.scalar
        def _(act):
            act.wait_ge(s_g, 16)
            act.activation(gf[:], gf_raw[:], ACT.Tanh).then_inc(s_gf, 1)

            def weigh(e):
                if e.ok:
                    act.wait_ge(s_raw, e.times(1, 1))
                    wait(act, s_wt, e.times(1))
                    act.activation(e_s[:], raw_s[:], ACT.Exp, bias=top_e[:, 0:1], accum_out=sum_s[:]).then_inc(s_es, 1)

            def silu(e, n):
                act.wait_ge(h1_done, e.times(HID, n + 1))
                wait(act, hid_done, e.times(HID, n - 1))
                act.activation(act_h[n % 2][:], h1_ps[n % 2][:, 0:SPAN], ACT.Silu).then_inc(silu_done, 1)

            def y_copy(e, st):
                act.wait_ge(y_done, e.times(ST, st + 1))
                act.wait_ge(s_wt, e.times(1, 1))
                wait(act, s_add[st], e.times(16))
                act.activation(y[st][:], y_ps[st % 2][:, 0:D], ACT.Copy, scale=weight[e.p][:, st:st + 1]).then_inc(y_out, 1)

            weigh(Expert(0, 0))

            def step(e):
                for n in range(HID):
                    silu(e, n)
                for st in range(ST // 2):
                    y_copy(e, st)
                weigh(e.on(1))
                for st in range(ST // 2, ST):
                    y_copy(e, st)

            over(act, step)

        @block.vector
        def _(dve):
            dve.memset(ones[:], 1.0).then_inc(s_one, 1)
            dve.wait_ge(s_gf, 1)

            def list_of(e):
                if e.ok:
                    for st in range(ST):
                        wait(dve, s_add[st], e.times(16, -16))
                    i = e.times(ST)
                    dve.tensor_copy(idx[e.p][:], idx_all[:, i:i + ST] if isinstance(i, int) else idx_all[:, bass.ds(i, ST)]).then_inc(s_idx, 1)

            def raw(e):
                if e.ok:
                    i = e.times(1)
                    dve.wait_ge(s_xg[e.p], e.turn(16 * ST, 16 * ST))
                    wait(dve, s_es, e.times(1))
                    dve.tensor_copy(top_e[:], neg_top[:, i:i + 1] if isinstance(i, int) else neg_top[:, bass.ds(i, 1)]).then_inc(s_inv, 1)
                    col = xg[e.p][:, :, D + i:D + i + 1] if isinstance(i, int) else xg[e.p][:, :, bass.ds(i + D, 1)]
                    dve.wait_ge(s_inv, e.times(2, 1))
                    dve.tensor_copy(raw_s[:].unsqueeze(2), col).then_inc(s_raw, 1)

            def weights(e):
                if e.ok:
                    dve.wait_ge(z_done, e.times(1, 1))
                    dve.reciprocal(inv[:], z_ps[:, 0:1]).then_inc(s_inv, 1)
                    dve.wait_ge(s_inv, e.times(2, 2))
                    wait(dve, y_out, e.times(ST, -ST))
                    dve.tensor_scalar(weight[e.p][:], e_s[:], inv[:, 0:1], gf[:, 0:1], ALU.mult, ALU.mult).then_inc(s_wt, 1)

            def t_copy(e, i):
                if e.ok:
                    k, h = i % KD, i // KD
                    dve.wait_ge(t_done, e.times(TRANS, i + 1))
                    wait(dve, h3_done, e.times(HID, -HID))
                    dve.tensor_copy(xg_t[e.p][:, k, h * SPAN:(h + 1) * SPAN], t_ps[i % 2][:, 0:SPAN]).then_inc(t_out, 1)

            def gate(e, n):
                dve.wait_ge(h3_done, e.times(HID, n + 1))
                dve.wait_ge(silu_done, e.times(HID, n + 1))
                if n % FT == 0:
                    wait(dve, y_done, e.times(ST, (n // FT + 1) * TT - ST))
                dve.tensor_tensor(hid[n // FT][:, n % FT, :], act_h[n % 2][:], h3_ps[0][:, 0:SPAN], ALU.mult).then_inc(hid_done, 1)

            list_of(Expert(0, 0))
            raw(Expert(0, 0))
            weights(Expert(0, 0))
            for i in range(TRANS):
                t_copy(Expert(0, 0), i)

            def step(e):
                list_of(e.on(1))
                for n in range(HID):
                    gate(e, n)
                raw(e.on(1))
                for i in range(TRANS):
                    t_copy(e.on(1), i)
                weights(e.on(1))

            over(dve, step)

        @block.tensor
        def _(pe):
            pe.wait_ge(s_one, 1)

            def transposes(e, i):
                if e.ok:
                    k, h = i % KD, i // KD
                    if i == 0:
                        pe.wait_ge(s_xg[e.p], e.turn(16 * ST, 16 * ST))
                    wait(pe, t_out, e.times(TRANS, i - 1))
                    for t in range(TT):
                        mm = pe.transpose(t_ps[i % 2][:, t * P:(t + 1) * P], xg[e.p][:, h * TT + t, k * P:(k + 1) * P], w["ident"][:])
                    mm.then_inc(t_done, 1)

            def total(e):
                if e.ok:
                    pe.wait_ge(s_es, e.times(1, 1))
                    wait(pe, s_wt, e.times(1))
                    pe.matmul(z_ps[:, 0:1], ones[:], sum_s[:], start=True, stop=True).then_inc(z_done, 1)

            def hidden(e, n):
                h, f = n // FT, slice((n % FT) * P, (n % FT + 1) * P)
                if n == 0:
                    pe.wait_ge(s_w[e.p], e.turn(48, 48))
                    pe.wait_ge(t_out, e.times(TRANS, TRANS))
                wait(pe, silu_done, e.times(HID, n - 1))
                for k in range(KD):
                    mm = pe.matmul(h1_ps[n % 2][:, 0:SPAN], w1[e.p][:, k, f], xg_t[e.p][:, k, h * SPAN:(h + 1) * SPAN],
                                   start=(k == 0), stop=(k == KD - 1))
                mm.then_inc(h1_done, 1)
                wait(pe, hid_done, e.times(HID, n))
                for k in range(KD):
                    mm = pe.matmul(h3_ps[0][:, 0:SPAN], w3[e.p][:, k, f], xg_t[e.p][:, k, h * SPAN:(h + 1) * SPAN],
                                   start=(k == 0), stop=(k == KD - 1))
                mm.then_inc(h3_done, 1)

            def down(e, st):
                h, t = st // TT, slice((st % TT) * P, (st % TT + 1) * P)
                pe.wait_ge(hid_done, e.times(HID, (h + 1) * FT))
                wait(pe, y_out, e.times(ST, st - 1))
                for f in range(FT):
                    mm = pe.matmul(y_ps[st % 2][:, 0:D], hid[h][:, f, t], w2[e.p][:, f, :], start=(f == 0), stop=(f == FT - 1))
                mm.then_inc(y_done, 1)

            first = Expert(0, 0)
            total(first)
            for i in range(TRANS):
                transposes(first, i)

            def step(e):
                for n in range(HID):
                    hidden(e, n)
                for i in range(TRANS):
                    transposes(e.on(1), i)
                for st in range(ST // 2):
                    down(e, st)
                total(e.on(1))
                for st in range(ST // 2, ST):
                    down(e, st)

            over(pe, step)


def build(nc, x, ctx_t, mask, g_x, g_f, wq, bq, wk, bk, wv, bv, wg_t, w1_t, w3_t, w2_t, out):
    n_tok = x.shape[0]
    rows = nc.dram_tensor("rows_scratch", (n_tok, ROW), F32, kind="Internal").ap()
    scores_t = nc.dram_tensor("scores_scratch", (E, n_tok), F32, kind="Internal").ap()
    thr = nc.dram_tensor("thr_scratch", (P, 2), F32, kind="Internal").ap()
    mask_bias = nc.dram_tensor("mask_scratch", (1, n_tok), BF16, kind="Internal").ap()
    with ExitStack() as whole:
        w = {"ident": whole.enter_context(nc.sbuf_tensor("ident", [P, P], F32)),
             "s_id": whole.enter_context(nc.semaphore("s_id")),
             "passed": whole.enter_context(nc.semaphore("passed"))}
        with ExitStack() as ctx:
            attention(nc, ctx, w, x, ctx_t, mask, g_x, wq, bq, wk, bk, wv, bv, wg_t, out, rows, scores_t, mask_bias)
        idx_all = whole.enter_context(nc.sbuf_tensor("idx_all", [P, n_tok // P], U32))
        neg_top = whole.enter_context(nc.sbuf_tensor("neg_top", [P, E], F32))
        with ExitStack() as ctx:
            select(nc, ctx, w, rows, scores_t, thr, idx_all, neg_top)
        with ExitStack() as ctx:
            experts(nc, ctx, w, rows, idx_all, neg_top, g_f, w1_t, w3_t, w2_t, out)


_HEAD_MAJOR = ("L0_xattn_Wq", "L0_xattn_Wk", "L0_xattn_bq", "L0_xattn_bk")


def lay_out(inputs):
    a = {k: np.asarray(v) for k, v in inputs.items()}
    n = a["x"].shape[0] * a["x"].shape[1]

    def columns(m):
        lead = m.shape[:-1]
        m = m.reshape(*lead, P // DH, KD, DH)
        return np.moveaxis(m, (-3, -2, -1), (-1, -3, -2)).reshape(*lead, D)

    return {
        "x": a["x"].reshape(n, D),
        "ctx_t": a["ctx_1024"].reshape(n, D).T,
        "mask": a["mask_BxS2_ik0"],
        "g_x": a["g_xattn"],
        "g_f": a["g_ffn"],
        "wq": columns(a["L0_xattn_Wq"]),
        "bq": columns(a["L0_xattn_bq"]).reshape(KD, P).T,
        "wk": columns(a["L0_xattn_Wk"]),
        "bk": columns(a["L0_xattn_bk"]).reshape(KD, P).T,
        "wv": a["L0_xattn_Wv"],
        "bv": a["L0_xattn_bv"],
        "wg_t": a["L0_ffn_Wg"].T,
        "w1_t": a["L0_ffn_W1"].transpose(0, 2, 1),
        "w3_t": a["L0_ffn_W3"].transpose(0, 2, 1),
        "w2_t": a["L0_ffn_W2"].transpose(0, 2, 1),
    }


def kernel(**inputs):
    import concourse.bacc as bacc
    from concourse.bass_utils import run_bass_kernel_spmd

    shape = inputs["x"].shape
    nc = bacc.Bacc("TRN2", target_bir_lowering=False, num_devices=1)
    arrays, args = {}, []
    for name, a in lay_out(inputs).items():
        a = np.ascontiguousarray(a)
        arrays[f"in_{name}"] = a
        args.append(nc.dram_tensor(f"in_{name}", a.shape, mybir.dt.from_np(a.dtype), kind="ExternalInput").ap())
    out = nc.dram_tensor("out", (shape[0] * shape[1], D), F32, kind="ExternalOutput").ap()
    build(nc, *args, out)
    r = run_bass_kernel_spmd(nc, [arrays], core_ids=[0])
    return r.results[0]["out"].reshape(shape)
```

```python
from contextlib import ExitStack

import numpy as np

import concourse.bass as bass
from concourse import mybir

F32 = mybir.dt.float32
BF16 = mybir.dt.bfloat16
FP16 = mybir.dt.float16
F32R = mybir.dt.float32r
I32 = mybir.dt.int32
U32 = mybir.dt.uint32
ALU = mybir.AluOpType
ACT = mybir.ActivationFunctionType
AX_X = mybir.AxisListType.X

P = 128
D = 256
HEADS = 16
DH = 16
GB = 4
GT = GB * P
KD = D // P
VW = 32
EPS = 1e-5
MASKED = float(2 ** 30)
SCALE = 1.0 / float(np.sqrt(np.float32(10.0)))
E = 8
F = 512
ROW = D + E
HI, MID, LO = range(3)
Q_ROWS = [HI, HI, HI, MID, MID, LO]
K_ROWS = [HI, MID, LO, HI, MID, HI]
SPLIT = len(Q_ROWS) * DH
MASK_ROW, MAX_ROW = SPLIT, SPLIT + 1
A_K, B_K = SPLIT + 1, SPLIT + 3
MAGIC = 1597463007.0
Q_SENT, K_SENT = 16 * 6, 16 * 7
LN_OPS = 16


OT_AT = 2


class Batch:

    def __init__(self, k, s, total):
        self.k, self.s, self.total = k + s // 8, s % 8, total

    def back(self, n):
        return Batch(self.k, self.s - n, self.total)

    @property
    def ok(self):
        return not isinstance(self.k, int) or 0 <= 8 * self.k + self.s < self.total

    def times(self, n, more=0):
        return self.k * (8 * n) + (self.s * n + more)

    def turn(self, ring, n, more=0):
        return self.k * (8 // ring * n) + (self.s // ring * n + more)

    @property
    def tok(self):
        return self.k * (8 * P) + self.s * P

    @property
    def j(self):
        return self.s % GB

    @property
    def group(self):
        return Group(self.k, self.s // GB, self.total // GB)


class Group:

    def __init__(self, k, p, total):
        self.k, self.p, self.total = k + p // 2, p % 2, total

    def on(self, n):
        return Group(self.k, self.p + n, self.total)

    @property
    def ok(self):
        return not isinstance(self.k, int) or 0 <= 2 * self.k + self.p < self.total

    def times(self, n, more=0):
        return self.k * (2 * n) + (self.p * n + more)

    def turn(self, n, more=0):
        return self.k * n + more

    @property
    def tok(self):
        return self.k * (2 * GT) + self.p * GT


def wait(eng, sem, value):
    if not isinstance(value, int) or value > 0:
        eng.wait_ge(sem, value)


class Chain:

    def __init__(self, eng, sem, base=0, passed=None):
        self.eng, self.sem, self.base, self.n, self.passed = eng, sem, base, 0, passed

    def link(self, ins):
        ins.then_inc(self.sem, 1)
        self.n += 1
        self.eng.wait_ge(self.sem, self.base + self.n)
        if self.passed is not None and not isinstance(self.base, int):
            self.eng.sem_inc(self.passed, 1)


def attention(nc, ctx, w, x, ctx_t, mask, g_x, wq, bq, wk, bk, wv, bv, wg_t, out, rows, scores_t,
              mask_bias):
    n_tok = x.shape[0]
    NB = n_tok // P
    NG = NB // GB

    def sb(name, shape, dt=F32):
        return ctx.enter_context(nc.sbuf_tensor(name, shape, dt))

    def sem(name):
        return ctx.enter_context(nc.semaphore(name))

    def bank(name, dt=F32):
        return ctx.enter_context(nc.psum_tensor(name, [P, 512], dt))

    ident, passed = w["ident"], w["passed"]
    wq_sb, wk_sb, wv_sb = sb("wq_sb", [P, KD, D]), sb("wk_sb", [P, KD, D]), sb("wv_sb", [P, KD, D])
    wg_sb = sb("wg_sb", [P, KD, E])
    bq_sb, bk_sb = sb("bq_sb", [P, KD]), sb("bk_sb", [P, KD])
    bv_sb = sb("bv_sb", [P, D])
    ones_bf = sb("ones_bf", [HEADS, GT], BF16)
    gx_raw, gx = sb("gx_raw", [P, 1]), sb("gx", [P, 1])
    mask_nat = sb("mask_nat", [NB, P], I32)
    bias_nat = sb("bias_nat", [NB, P], BF16)
    x_in = [sb(f"x_in{p}", [P, GB, D]) for p in range(2)]
    c_t = [sb(f"c_t{p}", [P, KD, GT]) for p in range(2)]
    mask_b = [sb(f"mask_b{p}", [P, GT], I32) for p in range(2)]
    stats1, mv1 = sb("stats1", [P, GB, 6]), sb("mv1", [P, GB, 2])
    v1, y1, t1, nm1 = sb("v1", [P, GB]), sb("y1", [P, GB]), sb("t1", [P, GB]), sb("nm1", [P, GB])
    xn, xn_t = sb("xn", [P, GB, D]), sb("xn_t", [P, KD, GT])
    q_rest, k_val, k_rest = sb("q_rest", [P, KD, GT]), sb("k_val", [P, KD, GT]), sb("k_rest", [P, KD, GT])
    q_part, k_part = sb("q_part", [P, 3, KD, GT], BF16), sb("k_part", [P, 3, KD, GT], BF16)
    q_st = [sb(f"q_st{p}", [P, HEADS, GT], BF16) for p in range(2)]
    k_st = [sb(f"k_st{p}", [P, HEADS, GT], BF16) for p in range(2)]
    v_aug = [sb(f"v_aug{p}", [P, GB, HEADS, VW]) for p in range(2)]
    m_sb = [sb(f"m_sb{i}", [P, HEADS]) for i in range(2)]
    neg_m = [sb(f"neg_m{i}", [HEADS, 2, P], BF16) for i in range(2)]
    p_t = [sb(f"p_t{i}", [P, HEADS, P]) for i in range(2)]
    o_t = [sb(f"o_t{i}", [P, 4, P]) for i in range(2)]
    rden, o_n = sb("rden", [P, HEADS]), sb("o_n", [P, D])
    x_res = [sb(f"x_res{p}", [P, GB, D]) for p in range(2)]
    x2 = [sb(f"x2_{p}", [P, GB, D]) for p in range(2)]
    stats2 = sb("stats2", [P, 6])
    mv2 = [sb(f"mv2_{p}", [P, GB, 2]) for p in range(2)]
    v2, y2, t2 = sb("v2", [P, GB]), sb("y2", [P, GB]), sb("t2", [P, GB])
    nm2 = sb("nm2", [P, GB])
    row = [sb(f"row{p}", [P, GB, ROW]) for p in range(2)]
    xn2_t = sb("xn2_t", [P, KD, GT])
    s_t = sb("s_t", [E, GT])

    a_ps = [bank(f"a_ps{i}") for i in range(2)]
    b_ps = [bank(f"b_ps{i}") for i in range(2)]
    pv_ps = bank("pv_ps")
    f_ps = bank("f_ps")
    m_ps = bank("m_ps")
    o_ps = bank("o_ps")

    s_wq, s_wk, s_wv, s_misc = sem("s_wq"), sem("s_wk"), sem("s_wv"), sem("s_misc")
    s_ones, s_zero, s_rows1 = sem("s_ones"), sem("s_zero"), sem("s_rows1")
    s_bias, s_bias_st, s_gx = sem("s_bias"), sem("s_bias_st"), sem("s_gx")
    s_x = [sem(f"s_x{p}") for p in range(2)]
    s_c = [sem(f"s_c{p}") for p in range(2)]
    s_mv1, s_ln1, s_xn = sem("s_mv1"), sem("s_ln1"), sem("s_xn")
    s_st1 = sem("s_st1")
    f_done = sem("f_done")
    f_free = [sem(f"f_free{i}") for i in range(2)]
    q_hi, q_mid, q_lo = sem("q_hi"), sem("q_mid"), sem("q_lo")
    k_hi, k_r, k_mid, k_lo = sem("k_hi"), sem("k_r"), sem("k_mid"), sem("k_lo")
    s_q = [sem(f"s_q{p}") for p in range(2)]
    s_k = [sem(f"s_k{p}") for p in range(2)]
    a_done, max_done = sem("a_done"), sem("max_done")
    mt_done, nhi_done, nmid_done = sem("mt_done"), sem("nhi_done"), sem("nmid_done")
    s_m = [sem(f"s_m{i}") for i in range(2)]
    b_done, exp_done, pv_done, pv_out = sem("b_done"), sem("exp_done"), sem("pv_done"), sem("pv_out")
    ot_done, rd_done, ot_out, x2_done, st2_done, mv2_done, ln2 = (
        sem("ot_done"), sem("rd_done"), sem("ot_out"), sem("x2_done"), sem("st2_done"), sem("mv2_done"), sem("ln2"))
    xn2_done, xt2_done, xt2_out = sem("xn2_done"), sem("xt2_done"), sem("xt2_out")
    r_done, r_out, st_done, st_out = sem("r_done"), sem("r_out"), sem("st_done"), sem("st_out")
    s_res = [sem(f"s_res{p}") for p in range(2)]
    s_out = [sem(f"s_out{p}") for p in range(2)]
    s_row = [sem(f"s_row{p}") for p in range(2)]
    s_sc = sem("s_sc")

    def steps(eng, step):
        for g in range(4):
            for j in range(GB):
                step(eng, Batch(g // 2, 4 * (g % 2) + j, NB))
        with eng.Fori(2, NG // 2 - 1, 1) as k:
            for s in range(2 * GB):
                step(eng, Batch(k, s, NB))
        for g in range(NG - 2, NG + 4):
            for j in range(GB):
                step(eng, Batch(g // 2, 4 * (g % 2) + j, NB))

    def f_bank(g, i):
        return m_ps if i == 1 and isinstance(g.k, int) and g.k == 0 and g.p == 0 else f_ps

    O_USES = sorted([((j, OT_AT), "ot", j) for j in range(GB)]
                    + [((3, 0), "xt", 0), ((0, 0), "xt", 1), ((1, 0), "r", 0), ((2, 0), "st", 0)])
    O_LAG = {("xt", 0): 2, ("xt", 1): 3, ("r", 0): 3, ("st", 0): 3}

    def o_free(eng, g, q, j):
        at = [x[0] for x in O_USES].index((j, q))
        for back in range(1, 4 * len(O_USES)):
            i, turn = (at - back) % len(O_USES), (at - back) // len(O_USES)
            (_, what, n) = O_USES[i]
            if what == "ot":
                use = Batch(g.k, 4 * g.p + n + 4 * turn, NB).back(4)
                if use.ok:
                    return wait(eng, ot_out, use.times(1, 1))
            else:
                use = g.on(turn - O_LAG[what, n])
                if use.ok:
                    if what == "xt":
                        return wait(eng, xt2_out, use.times(2, n + 1))
                    return wait(eng, r_out if what == "r" else st_out, use.times(1, 1))

    with nc.Block() as block:

        @block.sync
        def _(sp):
            def load_const(dst, src, ready):
                sp.dma_start(dst, src).then_inc(ready, 16)

            def square(m):
                return m.rearrange("(k p) n -> p k n", p=P)

            def over_rows(v):
                return v.rearrange("(a n) -> a n", a=1).to_broadcast([P, v.shape[0]])

            def load_x(g):
                if g.ok:
                    wait(sp, s_xn, g.times(4, -4))
                    sp.sem_inc(passed, 1)
                    sp.dma_start(x_in[g.p][:], x[bass.ds(g.tok, GT), :].rearrange("(t p) d -> p t d", p=P)).then_inc(s_x[g.p], 16)

            def load_c(g):
                if g.ok:
                    wait(sp, f_done, g.times(8, -8))
                    sp.sem_inc(passed, 1)
                    wait(sp, f_free[1], g.times(4, -5))
                    sp.sem_inc(passed, 1)
                    sp.dma_start(c_t[g.p][:], ctx_t[:, bass.ds(g.tok, GT)].rearrange("(k p) t -> p k t", p=P)).then_inc(s_c[g.p], 16)
                    sp.dma_start(mask_b[g.p][:], mask.rearrange("b (a s) -> a (b s)", a=1)[:, bass.ds(g.tok, GT)].to_broadcast([P, GT])).then_inc(s_c[g.p], 16)

            def stack_q(g):
                if not g.ok:
                    return
                wait(sp, b_done, g.times(16, -16))
                for part, ready in ((HI, q_hi), (MID, q_mid), (LO, q_lo)):
                    sp.wait_ge(ready, g.times(2, 2))
                    for r, have in enumerate(Q_ROWS):
                        if have == part:
                            sp.dma_start(q_st[g.p][r * DH:(r + 1) * DH, :, :], q_part[:, part, :, :]).then_inc(s_q[g.p], 16)

            def stack_k(g):
                if not g.ok:
                    return
                wait(sp, b_done, g.times(16, -16))
                sp.sem_inc(passed, 1)
                sp.dma_start(k_st[g.p][MASK_ROW:MASK_ROW + 1, :, :],
                             mask_bias[0:1, bass.ds(g.tok, GT)].unsqueeze(1).to_broadcast([1, HEADS, GT])).then_inc(s_k[g.p], 16)
                for part, ready in ((HI, k_hi), (MID, k_mid), (LO, k_lo)):
                    sp.wait_ge(ready, g.times(2, 2))
                    for r, have in enumerate(K_ROWS):
                        if have == part:
                            sp.dma_start(k_st[g.p][r * DH:(r + 1) * DH, :, :], k_part[:, part, :, :]).then_inc(s_k[g.p], 16)

            def residual(g):
                if g.ok:
                    wait(sp, x2_done, g.times(4, -4))
                    sp.sem_inc(passed, 1)
                    sp.dma_start(x_res[g.p][:], x[bass.ds(g.tok, GT), :].rearrange("(t p) d -> p t d", p=P)).then_inc(s_res[g.p], 16)

            def max_rows(b):
                if b.ok:
                    sp.wait_ge(nmid_done, b.times(1, 1))
                    for i in range(2):
                        r = MAX_ROW + i
                        sp.dma_start(q_st[b.group.p][r:r + 1, :, b.j * P:(b.j + 1) * P], neg_m[b.s % 2][:, i, :]).then_inc(s_m[b.s % 2], 16)

            def store_x2(g):
                if g.ok:
                    sp.wait_ge(x2_done, g.times(4, 4))
                    sp.sem_inc(passed, 1)
                    sp.dma_start(out[bass.ds(g.tok, GT), :].rearrange("(t p) d -> p t d", p=P), x2[g.p][:]).then_inc(s_out[g.p], 16)

            def store_scores(g):
                if g.ok:
                    sp.wait_ge(r_out, g.times(1, 1))
                    sp.sem_inc(passed, 1)
                    sp.dma_start(scores_t[:, bass.ds(g.tok, GT)], s_t[:]).then_inc(s_sc, 16)

            def store_rows(g):
                if g.ok:
                    sp.wait_ge(st_out, g.times(1, 1))
                    sp.sem_inc(passed, 1)
                    sp.dma_start(rows[bass.ds(g.tok, GT), :].rearrange("(t p) d -> p t d", p=P), row[g.p][:]).then_inc(s_row[g.p], 16)

            load_x(Group(0, 0, NG))
            load_const(wq_sb[:], square(wq), s_wq)
            load_const(bq_sb[:], bq, s_wq)
            load_c(Group(0, 0, NG))
            load_const(mask_nat[:], mask, s_misc)
            load_const(wk_sb[:], square(wk), s_wk)
            load_const(bk_sb[:], bk, s_wk)
            load_const(wv_sb[:], square(wv), s_wv)
            load_const(bv_sb[:], over_rows(bv), s_wv)
            load_x(Group(0, 1, NG))
            sp.wait_ge(s_ones, 1)
            for p in range(2):
                load_const(q_st[p][MASK_ROW:MASK_ROW + 1, :, :], ones_bf[:], s_rows1)
                for i in range(2):
                    load_const(k_st[p][MAX_ROW + i:MAX_ROW + i + 1, :, :], ones_bf[:], s_rows1)
            sp.wait_ge(s_bias, 1)
            sp.dma_start(mask_bias.rearrange("a (b s) -> (a b) s", s=P), bias_nat[:]).then_inc(s_bias_st, 16)
            sp.wait_ge(s_bias_st, 16)
            stack_q(Group(0, 0, NG))
            load_const(wg_sb[:], square(wg_t), s_misc)
            load_const(gx_raw[:], over_rows(g_x), s_misc)
            load_c(Group(0, 1, NG))
            stack_k(Group(0, 0, NG))

            def step(sp, b):
                g = b.group
                if b.j == 0:
                    residual(g)
                    load_x(g.on(2))
                    load_c(g.on(2))
                if b.j == 1:
                    store_x2(g.on(-2))
                if b.j == 2:
                    store_scores(g.on(-3))
                    stack_q(g.on(1))
                if b.j == 3:
                    store_rows(g.on(-3))
                    stack_k(g.on(1))
                max_rows(b.back(1))

            steps(sp, step)
            for p in range(2):
                sp.wait_ge(s_out[p], 16 * (NG // 2))
                sp.wait_ge(s_row[p], 16 * (NG // 2))
            sp.wait_ge(s_sc, 16 * NG)
            sp.wait_ge(s_rows1, 16 * 6)

        @block.gpsimd
        def _(pool):
            for p in range(2):
                pool.memset(v_aug[p][:], 0.0).then_inc(s_zero, 1)
            pool.memset(ident[:], 0.0).then_inc(w["s_id"], 1)
            pool.wait_ge(w["s_id"], 1)
            pool.affine_select(out=ident[:], in_=ident[:], compare_op=ALU.not_equal, fill=1.0, base=0,
                               pattern=[[-1, P]], channel_multiplier=1).then_inc(w["s_id"], 1)

            def rsqrt(c, var, v, y, t):
                c.link(pool.tensor_scalar(v[:], var, EPS, None, ALU.add))
                c.link(pool.tensor_scalar(y[:].bitcast(I32), v[:].bitcast(I32), -0.5, MAGIC, ALU.mult, ALU.add))
                for _ in range(3):
                    c.link(pool.tensor_tensor(t[:], y[:], y[:], ALU.mult))
                    c.link(pool.tensor_tensor(t[:], t[:], v[:], ALU.mult))
                    c.link(pool.tensor_scalar(t[:], t[:], -0.5, 1.5, ALU.mult, ALU.add))
                    c.link(pool.tensor_tensor(y[:], y[:], t[:], ALU.mult))

            def scales(c, mv, v, y, t, nm):
                rsqrt(c, mv[:, :, 1], v, y, t)
                c.link(pool.tensor_tensor(t[:], mv[:, :, 0], y[:], ALU.mult))
                c.link(pool.tensor_scalar(nm[:], t[:], -1.0, None, ALU.mult))
                assert c.n == LN_OPS

            def ln1(g):
                if g.ok:
                    pool.wait_ge(s_mv1, g.times(4, 4))
                    wait(pool, s_xn, g.times(4))
                    pool.sem_inc(passed, 1)
                    scales(Chain(pool, s_ln1, g.times(LN_OPS), passed), mv1, v1, y1, t1, nm1)

            def ln2_scales(g):
                if g.ok:
                    pool.wait_ge(mv2_done, g.times(4, 4))
                    wait(pool, xn2_done, g.times(4))
                    pool.sem_inc(passed, 1)
                    scales(Chain(pool, ln2, g.times(LN_OPS), passed), mv2[g.p], v2, y2, t2, nm2)

            def split_q(g, m):
                if g.ok:
                    pool.wait_ge(q_mid, g.times(2, m + 1))
                    pool.tensor_tensor(q_part[:, LO, m, :], q_rest[:, m, :], q_part[:, MID, m, :], ALU.subtract).then_inc(q_lo, 1)

            def rest_k(g, m):
                if g.ok:
                    pool.wait_ge(k_hi, g.times(2, m + 1))
                    pool.tensor_tensor(k_rest[:, m, :], k_val[:, m, :], k_part[:, HI, m, :], ALU.subtract).then_inc(k_r, 1)

            def split_k(g, m):
                if g.ok:
                    pool.wait_ge(k_mid, g.times(2, m + 1))
                    pool.tensor_tensor(k_part[:, LO, m, :], k_rest[:, m, :], k_part[:, MID, m, :], ALU.subtract).then_inc(k_lo, 1)

            ln1(Group(0, 0, NG))
            g = Group(0, 0, NG)
            for m in range(KD):
                split_q(g, m)
            for m in range(KD):
                rest_k(g, m)
                split_k(g, m)
            ln1(Group(0, 1, NG))

            def step(pool, b):
                g = b.group
                for m in range(KD):
                    if b.j == 1:
                        split_q(g.on(1), m)
                    if b.j == 2:
                        rest_k(g.on(1), m)
                        split_k(g.on(1), m)
                if b.j == 0:
                    ln2_scales(g.on(-2))
                if b.j == 1:
                    ln1(g.on(2))

            steps(pool, step)

        @block.scalar
        def _(act):
            def f_wait(g, u):
                act.wait_ge(f_done, g.times(8, u + 1))

            def xn_t_out(g, k):
                if g.ok:
                    f_wait(g, k)
                    act.activation(xn_t[:, k, :], f_bank(g, k)[:], ACT.Copy).then_inc(f_free[k], 1)

            def hi_q(g, m):
                if g.ok:
                    f_wait(g, 2 + m)
                    if m == 0:
                        last = g.on(-1)
                        wait(act, s_q[last.p], last.turn(Q_SENT, Q_SENT))
                    act.activation(q_part[:, HI, m, :], f_bank(g, m)[:], ACT.Identity, bias=bq_sb[:, m:m + 1]).then_inc(q_hi, 1)

            def mid_q(g, m):
                if g.ok:
                    act.wait_ge(f_free[m], g.times(4, 2))
                    act.activation(q_part[:, MID, m, :], q_rest[:, m, :], ACT.Copy).then_inc(q_mid, 1)

            def hi_k(g, m):
                if g.ok:
                    act.wait_ge(f_free[m], g.times(4, 3))
                    if m == 0:
                        last = g.on(-1)
                        wait(act, s_k[last.p], last.turn(K_SENT, K_SENT))
                    act.activation(k_part[:, HI, m, :], k_val[:, m, :], ACT.Copy).then_inc(k_hi, 1)

            def mid_k(g, m):
                if g.ok:
                    act.wait_ge(k_r, g.times(2, m + 1))
                    act.activation(k_part[:, MID, m, :], k_rest[:, m, :], ACT.Copy).then_inc(k_mid, 1)

            def normalise(g, ts):
                if g.ok:
                    act.wait_ge(s_ln1, g.times(LN_OPS, LN_OPS))
                    wait(act, f_done, g.times(8, -6))
                    act.wait_ge(s_x[g.p], g.turn(16, 16))
                    for t in ts:
                        act.activation(xn[:, t, :], x_in[g.p][:, t, :], ACT.Identity, bias=nm1[:, t:t + 1],
                                       scale=y1[:, t:t + 1]).then_inc(s_xn, 1)

            def exp(b, q):
                if b.ok:
                    act.wait_ge(b_done, b.times(4, q + 1))
                    if q == 0:
                        wait(act, pv_done, b.times(1, -1))
                    act.activation(p_t[b.s % 2][:, 4 * q:4 * q + 4, :], b_ps[q % 2][:].rearrange("p (h s) -> p h s", s=P),
                                   ACT.Exp, scale=SCALE).then_inc(exp_done, 1)

            def neg_hi(b):
                if b.ok:
                    act.wait_ge(mt_done, b.times(1, 1))
                    wait(act, s_m[b.s % 2], b.turn(2, 32))
                    act.activation(neg_m[b.s % 2][:, 0, :], m_ps[0:HEADS, 0:P], ACT.Copy, scale=-1.0).then_inc(nhi_done, 1)

            def pv_copy(b):
                if b.ok:
                    act.wait_ge(pv_done, b.times(1, 1))
                    wait(act, ot_done, b.times(1, -1))
                    act.activation(o_t[b.s % 2][:], pv_ps[:].rearrange("p (a s) -> p a s", s=P), ACT.Copy).then_inc(pv_out, 1)

            def normalise2(g, ts):
                if g.ok:
                    act.wait_ge(ln2, g.times(LN_OPS, LN_OPS))
                    wait(act, s_row[g.p], g.turn(16))
                    for t in ts:
                        act.activation(row[g.p][:, t, 0:D], x2[g.p][:, t, :], ACT.Identity, bias=nm2[:, t:t + 1],
                                       scale=y2[:, t:t + 1]).then_inc(xn2_done, 1)

            def xt2_copy(g, k):
                if g.ok:
                    act.wait_ge(xt2_done, g.times(2, k + 1))
                    wait(act, r_done, g.times(1))
                    act.activation(xn2_t[:, k, :], o_ps[:], ACT.Copy).then_inc(xt2_out, 1)

            def router_out(g):
                if g.ok:
                    act.wait_ge(r_done, g.times(1, 1))
                    wait(act, s_sc, g.times(16))
                    wait(act, st_done, g.times(1))
                    act.activation(s_t[:], o_ps[0:E, :], ACT.Copy).then_inc(r_out, 1)

            act.wait_ge(s_wq, 32)
            g = Group(0, 0, NG)
            normalise(g, range(GB))
            for k in range(KD):
                xn_t_out(g, k)
            for m in range(KD):
                hi_q(g, m)
                mid_q(g, m)
            for m in range(KD):
                hi_k(g, m)
                mid_k(g, m)
            normalise(Group(0, 1, NG), range(GB))
            act.wait_ge(s_misc, 16 * 3)
            act.activation(gx[:], gx_raw[:], ACT.Tanh).then_inc(s_gx, 1)

            def step(act, b):
                g, f = b.group, b.group.on(1)
                exp(b.back(3), 3)
                if b.j == 0:
                    xn_t_out(f, 0)
                if b.j == 1:
                    hi_q(f, 0)
                if b.j == 2:
                    hi_k(f, 0)
                neg_hi(b.back(1))
                if b.j == 0:
                    xt2_copy(g.on(-3), 1)
                if b.j == 1:
                    router_out(g.on(-3))
                if b.j == 3:
                    xt2_copy(g.on(-2), 0)
                if b.j == 2:
                    normalise2(g.on(-2), (0, 1))
                if b.j == 3:
                    normalise(g.on(2), (0, 1))
                exp(b.back(2), 0)
                exp(b.back(2), 1)
                if b.j == 1:
                    mid_q(f, 0)
                if b.j == 2:
                    mid_k(f, 0)
                if b.j == 0:
                    xn_t_out(f, 1)
                if b.j == 1:
                    hi_q(f, 1)
                if b.j == 2:
                    hi_k(f, 1)
                if b.j == 2:
                    normalise2(g.on(-2), (2, 3))
                if b.j == 3:
                    normalise(g.on(2), (2, 3))
                exp(b.back(2), 2)
                pv_copy(b.back(3))
                if b.j == 1:
                    mid_q(f, 1)
                if b.j == 2:
                    mid_k(f, 1)

            steps(act, step)

        @block.vector
        def _(dve):
            dve.memset(ones_bf[:], 1.0).then_inc(s_ones, 1)

            def stats(g, ts):
                if not g.ok:
                    return
                dve.wait_ge(s_x[g.p], g.turn(16, 16))
                wait(dve, s_ln1, g.times(LN_OPS))
                for t in ts:
                    dve.bn_stats(stats1[:, t, :], x_in[g.p][:, t, :]).then_inc(s_st1, 1)
                dve.wait_ge(s_st1, g.times(4, ts[-1] + 1))
                dve.sem_inc(passed, 1)
                for t in ts:
                    dve.bn_aggr(mv1[:, t, :], stats1[:, t, :]).then_inc(s_mv1, 1)

            def rest_q(g, m):
                if g.ok:
                    dve.wait_ge(q_hi, g.times(2, m + 1))
                    wait(dve, q_lo, g.times(2, m - 1))
                    dve.scalar_tensor_tensor(out=q_rest[:, m, :], in0=f_bank(g, m)[:], scalar=bq_sb[:, m:m + 1],
                                             in1=q_part[:, HI, m, :], op0=ALU.add, op1=ALU.subtract).then_inc(f_free[m], 1)

            def make_k(g, m):
                if g.ok:
                    dve.wait_ge(f_done, g.times(8, 5 + m))
                    dve.wait_ge(s_c[g.p], g.turn(32, 32))
                    wait(dve, k_r, g.times(2, m - 1))
                    dve.scalar_tensor_tensor(out=k_val[:, m, :], in0=f_bank(g, m)[:], scalar=bk_sb[:, m:m + 1],
                                             in1=mask_b[g.p][:], op0=ALU.add, op1=ALU.mult).then_inc(f_free[m], 1)

            def make_v(g, i):
                if g.ok:
                    dve.wait_ge(f_done, g.times(8, 7 + i))
                    if i == 0:
                        wait(dve, pv_done, g.times(4, -4))
                    for t in range(2):
                        ins = dve.tensor_tensor(v_aug[g.p][:, 2 * i + t, :, 0:DH],
                                                f_bank(g, i)[:, t * D:(t + 1) * D].rearrange("p (h d) -> p h d", d=DH),
                                                bv_sb[:].rearrange("p (h d) -> p h d", d=DH), ALU.add)
                    ins.then_inc(f_free[i], 1)

            def maximum(b, q):
                if b.ok:
                    dve.wait_ge(a_done, b.times(4, q + 1))
                    if q == 0:
                        wait(dve, mt_done, b.times(1, -1))
                    dve.tensor_reduce(m_sb[b.s % 2][:, 4 * q:4 * q + 4], a_ps[q % 2][:].rearrange("p (h s) -> p h s", s=P),
                                      AX_X, ALU.max).then_inc(max_done, 1)

            def row_scores(g):
                if g.ok:
                    dve.wait_ge(st_done, g.times(1, 1))
                    dve.tensor_copy(row[g.p][:, :, D:ROW], o_ps[:, 0:GB * E].rearrange("p (t e) -> p t e", e=E)).then_inc(st_out, 1)

            def neg_mid(b):
                if b.ok:
                    dve.wait_ge(nhi_done, b.times(1, 1))
                    dve.scalar_tensor_tensor(out=neg_m[b.s % 2][:, 1, :], in0=m_ps[0:HEADS, 0:P], scalar=-1.0,
                                             in1=neg_m[b.s % 2][:, 0, :], op0=ALU.mult, op1=ALU.subtract).then_inc(nmid_done, 1)

            def finish(b):
                if not b.ok:
                    return
                dve.wait_ge(ot_done, b.times(1, 1))
                o = o_ps[:].rearrange("p (h v) -> p h v", v=VW)
                wait(dve, ot_out, b.times(1))
                dve.reciprocal(rden[:], o[:, :, DH]).then_inc(rd_done, 1)
                dve.wait_ge(rd_done, b.times(1, 1))
                wait(dve, x2_done, b.times(1))
                dve.tensor_tensor(o_n[:].rearrange("p (h d) -> p h d", d=DH), o[:, :, 0:DH],
                                  rden[:].unsqueeze(2).to_broadcast([P, HEADS, DH]), ALU.mult).then_inc(ot_out, 1)
                dve.wait_ge(ot_out, b.times(1, 1))
                g = b.group
                dve.wait_ge(s_res[g.p], g.turn(16, 16))
                if b.j == 0:
                    wait(dve, s_out[g.p], g.turn(16))
                    wait(dve, xn2_done, g.times(4, -4))
                dve.scalar_tensor_tensor(out=x2[g.p][:, b.j, :], in0=o_n[:], scalar=gx[:, 0:1], in1=x_res[g.p][:, b.j, :],
                                         op0=ALU.mult, op1=ALU.add).then_inc(x2_done, 1)
                dve.wait_ge(x2_done, b.times(1, 1))
                wait(dve, mv2_done, b.times(1))
                dve.bn_stats(stats2[:], x2[g.p][:, b.j, :]).then_inc(st2_done, 1)
                dve.wait_ge(st2_done, b.times(1, 1))
                wait(dve, ln2, g.times(LN_OPS, -LN_OPS))
                dve.sem_inc(passed, 1)
                dve.bn_aggr(mv2[g.p][:, b.j, :], stats2[:]).then_inc(mv2_done, 1)

            g = Group(0, 0, NG)
            stats(g, range(GB))
            dve.wait_ge(s_zero, 2)
            for p in range(2):
                dve.memset(v_aug[p][:, :, :, DH:DH + 1], 1.0).then_inc(s_zero, 1)
            dve.wait_ge(s_misc, 16)
            dve.tensor_scalar(bias_nat[:], mask_nat[:], -1.0, MASKED, ALU.add, ALU.mult).then_inc(s_bias, 1)
            dve.wait_ge(s_wq, 32)
            for m in range(KD):
                rest_q(g, m)
            dve.wait_ge(s_wk, 32)
            dve.wait_ge(s_wv, 32)
            for m in range(KD):
                make_k(g, m)
            for i in range(2):
                make_v(g, i)
            stats(Group(0, 1, NG), range(GB))
            dve.wait_ge(s_gx, 1)

            def step(dve, b):
                f = b.group.on(1)
                maximum(b, 0)
                if b.j == 1:
                    stats(b.group.on(2), range(GB))
                if b.j == 1:
                    rest_q(f, 0)
                if b.j == 2:
                    make_k(f, 0)
                if b.j == 3:
                    make_v(f, 0)
                neg_mid(b.back(1))
                if b.j == 2:
                    row_scores(b.group.on(-3))
                maximum(b, 1)
                maximum(b, 2)
                finish(b.back(4))
                if b.j == 1:
                    rest_q(f, 1)
                if b.j == 2:
                    make_k(f, 1)
                if b.j == 3:
                    make_v(f, 1)
                maximum(b, 3)

            steps(dve, step)

        @block.tensor
        def _(pe):
            pe.wait_ge(w["s_id"], 2)

            def front(g, u):
                if not g.ok:
                    return
                i = u % 2
                ps = f_bank(g, i)
                if isinstance(g.k, int) and g.k + g.p == 0:
                    wait(pe, f_free[i], u // 2)
                elif u == 0:
                    wait(pe, f_free[0], g.times(4))
                    wait(pe, f_free[1], g.times(4))
                else:
                    pe.wait_ge(f_free[1 - i], g.times(4, (u - 1) // 2 + 1))
                if u < 2:
                    pe.wait_ge(s_xn, g.times(4, 4))
                    for t in range(GB):
                        mm = pe.transpose(ps[:, t * P:(t + 1) * P], xn[:, t, u * P:(u + 1) * P], ident[:])
                elif u < 6:
                    wt, src = (wq_sb, xn_t) if u < 4 else (wk_sb, c_t[g.p])
                    if isinstance(g.k, int):
                        pe.wait_ge(*((s_wq, 32) if u < 4 else (s_wk, 32)))
                    if u < 4:
                        pe.wait_ge(f_free[0], g.times(4, 1))
                        pe.wait_ge(f_free[1], g.times(4, 1))
                    else:
                        pe.wait_ge(s_c[g.p], g.turn(32, 32))
                    for k in range(KD):
                        mm = pe.matmul(ps[:], wt[:, k, i * P:(i + 1) * P], src[:, k, :], start=(k == 0), stop=(k == KD - 1))
                else:
                    if isinstance(g.k, int):
                        pe.wait_ge(s_wv, 32)
                    for t in range(2):
                        tok = (2 * (u - 6) + t) * P
                        for k in range(KD):
                            mm = pe.matmul(ps[:, t * D:(t + 1) * D], c_t[g.p][:, k, tok:tok + P], wv_sb[:, k, :],
                                           start=(k == 0), stop=(k == KD - 1))
                mm.then_inc(f_done, 1)

            def scores(b, q):
                if not b.ok:
                    return
                g = b.group
                if q == 0 and b.j == 0:
                    pe.wait_ge(s_q[g.p], g.turn(Q_SENT, Q_SENT))
                    pe.wait_ge(s_k[g.p], g.turn(K_SENT, K_SENT))
                wait(pe, max_done, b.times(4, q - 1))
                for i in range(4):
                    h, tok = 4 * q + i, slice(b.j * P, (b.j + 1) * P)
                    mm = pe.matmul(a_ps[q % 2][:, i * P:(i + 1) * P], q_st[g.p][0:A_K, h, tok], k_st[g.p][0:A_K, h, tok],
                                   start=True, stop=True)
                mm.then_inc(a_done, 1)

            def scores_t_(b, q):
                if not b.ok:
                    return
                g = b.group
                if q == 0:
                    pe.wait_ge(s_m[b.s % 2], b.turn(2, 32, 32))
                wait(pe, exp_done, b.times(4, q - 1))
                for i in range(4):
                    h, tok = 4 * q + i, slice(b.j * P, (b.j + 1) * P)
                    mm = pe.matmul(b_ps[q % 2][:, i * P:(i + 1) * P], k_st[g.p][0:B_K, h, tok], q_st[g.p][0:B_K, h, tok],
                                   start=True, stop=True)
                mm.then_inc(b_done, 1)

            def values(b, q):
                if not b.ok:
                    return
                if q == 0:
                    pe.wait_ge(f_free[1], b.group.times(4, 4))
                    pe.wait_ge(f_free[0], b.group.times(4, 4))
                    wait(pe, pv_out, b.times(1))
                pe.wait_ge(exp_done, b.times(4, q + 1))
                for i in range(4):
                    h = 4 * q + i
                    mm = pe.matmul(pv_ps[VW * i:VW * (i + 1), q * P:(q + 1) * P], v_aug[b.group.p][:, b.j, h, :],
                                   p_t[b.s % 2][:, h, :], start=True, stop=True)
                if q == 3:
                    mm.then_inc(pv_done, 1)

            def router(g, at):
                if g.ok:
                    o_free(pe, *at)
                    pe.wait_ge(xt2_out, g.times(2, 2))
                    for k in range(KD):
                        mm = pe.matmul(o_ps[0:E, :], wg_sb[:, k, :], xn2_t[:, k, :], start=(k == 0), stop=(k == KD - 1))
                    mm.then_inc(r_done, 1)

            def scores_back(g, at):
                if g.ok:
                    o_free(pe, *at)
                    pe.wait_ge(r_out, g.times(1, 1))
                    pe.sem_inc(passed, 1)
                    for t in range(GB):
                        mm = pe.transpose(o_ps[:, t * E:(t + 1) * E], s_t[:, t * P:(t + 1) * P], ident[0:E, 0:E])
                    mm.then_inc(st_done, 1)

            def max_t(b):
                use = b.back(1)
                if use.ok:
                    if isinstance(use.k, int) and use.k + use.s == 0:
                        pe.wait_ge(f_free[1], 4)
                    wait(pe, nmid_done, use.times(1))
                    pe.wait_ge(max_done, use.times(4, 4))
                    pe.transpose(m_ps[0:HEADS, 0:P], m_sb[use.s % 2][:], ident[:]).then_inc(mt_done, 1)

            def out_back(b):
                use = b.back(4)
                if use.ok:
                    o_free(pe, b.group, OT_AT, b.j)
                    pe.wait_ge(pv_out, use.times(1, 1))
                    for a in range(4):
                        mm = pe.transpose(o_ps[:, a * P:(a + 1) * P], o_t[use.s % 2][:, a, :], ident[:])
                    mm.then_inc(ot_done, 1)

            def xn2_back(g, k, at):
                if g.ok:
                    o_free(pe, *at)
                    pe.wait_ge(xn2_done, g.times(4, 4))
                    for t in range(GB):
                        mm = pe.transpose(o_ps[:, t * P:(t + 1) * P], row[g.p][:, t, k * P:(k + 1) * P], ident[:])
                    mm.then_inc(xt2_done, 1)

            for u in range(8):
                front(Group(0, 0, NG), u)
            pe.wait_ge(s_rows1, 16 * 6)
            pe.wait_ge(s_zero, 4)
            pe.wait_ge(s_misc, 16 * 3)

            def step(pe, b):
                g = b.group
                for q in range(4):
                    scores(b, q)
                    if q == OT_AT:
                        out_back(b)
                    scores_t_(*((b.back(2), q - 1) if q else (b.back(3), 3)))
                    if q == 1:
                        values(b.back(3), 0)
                    if q >= 1:
                        values(b.back(3), q)
                    if q in (0, 2):
                        front(g.on(1), 2 * b.j + q // 2)
                    if q == 0:
                        max_t(b)
                    if (b.j, q) == (3, 0):
                        xn2_back(g.on(-2), 0, (g, q, b.j))
                    if (b.j, q) == (0, 0):
                        xn2_back(g.on(-3), 1, (g, q, b.j))
                    if (b.j, q) == (1, 0):
                        router(g.on(-3), (g, q, b.j))
                    if (b.j, q) == (2, 0):
                        scores_back(g.on(-3), (g, q, b.j))

            steps(pe, step)


CHUNKS = P // E
ROUNDS = 14
CUTS = 3
BIG = 1e30
SEARCH_CONSTS = 4 + CUTS + 4
SEL_CONSTS = SEARCH_CONSTS + 17


def select(nc, ctx, w, scores_t, sh):
    n_tok = scores_t.shape[1]
    CAP = n_tok // E
    ST = CAP // P
    T = n_tok // P
    TP = 2 * T
    EP = E // 2

    def sb(name, shape, dt=F32):
        return ctx.enter_context(nc.sbuf_tensor(name, shape, dt))

    def sem(name):
        return ctx.enter_context(nc.semaphore(name))

    sc = sb("sc", [P, n_tok // CHUNKS])
    ts = sb("ts", [TP, EP, P])
    same, before, group = sb("same", [P, P]), sb("before", [TP, TP]), sb("group", [TP, TP])
    slot = sb("slot", [P, CAP])
    slot_of = sb("slot_of", [P, ST])
    ones_row, ones = sb("ones_row", [1, P]), sb("ones", [TP, P])
    part_max, part_min = sb("part_max", [P, 1]), sb("part_min", [P, 1])
    ends, spread = sb("ends", [1, 2, E]), sb("spread", [1, 2, P])
    junk = sb("junk", [P, CUTS, n_tok // CHUNKS], BF16)
    cut = [sb(f"cut{p}", [P, CUTS + 1]) for p in range(2)]
    ge = [sb(f"ge{p}", [P, CUTS + 1]) for p in range(2)]
    step = [sb(f"step{p}", [P, 1]) for p in range(2)]
    nth, cnt, passes = sb("nth", [P, CUTS]), sb("cnt", [P, CUTS]), sb("passes", [P, 1])
    high, lo_hi = sb("high", [P, CUTS + 1]), sb("lo_hi", [P, 2])
    parity, pair, by_pair = sb("parity", [P, 2, T]), sb("pair", [P, EP]), sb("by_pair", [P, EP, 2])
    top = sb("top", [1, E])
    th = sb("th", [TP, EP, 2])
    above, tied, place = sb("above", [TP, EP, P]), sb("tied", [TP, EP, P]), sb("place", [TP, EP, P])
    n_above, left = sb("n_above", [TP, EP]), sb("left", [TP, EP])
    chosen, count = sb("chosen", [TP, EP, P]), sb("count", [TP, EP, P])
    start, end = sb("start", [TP, EP]), sb("end", [TP, EP])
    upto = sb("upto", [TP, EP, P + 1], FP16)
    tile_no = sb("tile_no", [TP, 1])
    under, hot = sb("under", [TP, EP, CAP], FP16), sb("hot", [TP, EP, CAP], FP16)
    cnt_junk = [sb(f"cnt_junk{i}", [P, P]) for i in range(2)]
    pos = sb("pos", [P, E * ST])

    tot_ps, small_ps, g_ps = sh["banks"][0], sh["banks"][1], sh["banks"][2:6]
    idx_all, neg_top, s_pos = sh["idx_all"], sh["neg_top"], sh["s_pos"]

    s_sc, s_ts, s_e = sem("s_sc2"), sem("s_ts"), sem("s_e2")
    s_pm, s_bound = sem("s_pm"), sem("s_bound")
    s_top_t, s_top, s_top_b = sem("s_top_t"), sem("s_top"), sem("s_top_b")
    s_count, s_tot, s_thr = sem("s_count"), sem("s_tot"), sem("s_thr")
    s_found, s_side, s_th = sem("s_found"), sem("s_side"), sem("s_th")
    d = sem("d_chain")
    s_tie, s_left, s_sel, s_start, s_hot = sem("s_tie"), sem("s_left"), sem("s_sel"), sem("s_start"), sem("s_hot")
    s_pick = sem("s_pick")

    def sync(sp):
        sp.dma_start(sc[:], scores_t.rearrange("e (c n) -> (e c) n", c=CHUNKS)).then_inc(s_sc, 16)
        by_tile = scores_t.rearrange("(a b) (t s) -> b t a s", b=2, s=P)
        for b in range(2):
            sp.dma_start(ts[b * T:(b + 1) * T, :, :], by_tile[b]).then_inc(s_ts, 16)

    def gpsimd(pool):
        c = Chain(pool, s_e)
        c.link(pool.memset(same[:], 1.0))
        v = same[:].rearrange("p (e c) -> p e c", c=CHUNKS)
        c.link(pool.affine_select(out=v, in_=v, compare_op=ALU.is_ge, fill=0.0, base=0,
                                  pattern=[[-CHUNKS, E], [0, CHUNKS]], channel_multiplier=1))
        c.link(pool.affine_select(out=v, in_=v, compare_op=ALU.is_ge, fill=0.0, base=CHUNKS - 1,
                                  pattern=[[CHUNKS, E], [0, CHUNKS]], channel_multiplier=-1))
        c.link(pool.memset(ones_row[:], 1.0))
        for i in range(CUTS):
            c.link(pool.memset(nth[:, i:i + 1], i + 1.0))
        c.link(pool.memset(cut[1][:], 0.0))
        c.link(pool.memset(ge[1][:], 1.0))
        for p in range(2):
            c.link(pool.memset(ge[p][:, CUTS:CUTS + 1], 0.0))
        assert c.n == SEARCH_CONSTS
        c.link(pool.memset(group[:], 1.0))
        c.link(pool.affine_select(out=group[:, 0:T], in_=group[:, 0:T], compare_op=ALU.is_ge, fill=0.0,
                                  base=T - 1, pattern=[[0, T]], channel_multiplier=-1))
        c.link(pool.affine_select(out=group[:, T:TP], in_=group[:, T:TP], compare_op=ALU.is_ge, fill=0.0,
                                  base=-T, pattern=[[0, T]], channel_multiplier=1))
        c.link(pool.affine_select(out=before[:], in_=group[:], compare_op=ALU.is_ge, fill=0.0, base=-1,
                                  pattern=[[1, TP]], channel_multiplier=-1))
        c.link(pool.iota(slot[:], [[1, CAP]], base=0, channel_multiplier=0, allow_small_or_imprecise_dtypes=True))
        c.link(pool.iota(slot_of[:], [[P, ST]], base=0, channel_multiplier=1, allow_small_or_imprecise_dtypes=True))
        for b in range(2):
            c.link(pool.iota(tile_no[b * T:(b + 1) * T, :], [[0, 1]], base=0, channel_multiplier=P,
                             allow_small_or_imprecise_dtypes=True))
        c.link(pool.memset(ones[:], 1.0))
        c.link(pool.memset(pair[:], 0.0))
        c.link(pool.memset(parity[:], 0.0))
        for b in range(2):
            c.link(pool.affine_select(out=pair[:], in_=pair[:], compare_op=ALU.not_equal, fill=1.0, base=-CHUNKS * b,
                                      pattern=[[-2 * CHUNKS, EP]], channel_multiplier=1))
        for a in range(EP):
            c.link(pool.affine_select(out=parity[:], in_=parity[:], compare_op=ALU.not_equal, fill=1.0,
                                      base=-2 * CHUNKS * a, pattern=[[-CHUNKS, 2], [0, T]], channel_multiplier=1))
        assert c.n == SEL_CONSTS

    def vector(dve):
        dve.wait_ge(s_sc, 16)
        dve.tensor_reduce(part_max[:], sc[:], AX_X, ALU.max).then_inc(s_pm, 1)
        dve.tensor_reduce(part_min[:], sc[:], AX_X, ALU.min).then_inc(s_pm, 1)
        dve.wait_ge(s_top_t, 1)
        by_part = small_ps[0:1, 0:2 * P].rearrange("p (i e c) -> p i e c", i=2, c=CHUNKS)
        c = Chain(dve, s_top)
        dve.tensor_reduce(ends[:, 0, :], by_part[:, 0], AX_X, ALU.max).then_inc(s_bound, 1)
        dve.tensor_reduce(ends[:, 1, :], by_part[:, 1], AX_X, ALU.min).then_inc(s_bound, 1)
        dve.wait_ge(s_bound, 2)
        c.link(dve.tensor_scalar(top[:], ends[:, 0, :], -1.0, None, ALU.mult))
        c.link(dve.tensor_copy(spread[:].rearrange("p i (e c) -> p i e c", c=CHUNKS),
                               ends[:].unsqueeze(3).to_broadcast([1, 2, E, CHUNKS])))
        dve.wait_ge(s_top_b, 1)
        dve.sem_inc(s_thr, 1)
        c.link(dve.tensor_copy(neg_top[:], small_ps[:, 0:E]))
        dve.wait_ge(s_e, SEARCH_CONSTS)
        lo, hi = lo_hi[:, 0:1], lo_hi[:, 1:2]
        c = Chain(dve, s_side)
        c.link(dve.tensor_scalar(hi, small_ps[:, E:E + 1], 1.0 + 2.0 ** -22, None, ALU.mult))
        c.link(dve.scalar_tensor_tensor(out=hi, in0=small_ps[:, E:E + 1], scalar=1.0 - 2.0 ** -22, in1=hi,
                                        op0=ALU.mult, op1=ALU.max))
        c.link(dve.tensor_scalar(cut[1][:, CUTS:CUTS + 1], hi, 1.0 / BIG, None, ALU.add))
        c.link(dve.tensor_copy(lo, small_ps[:, E + 1:E + 2]))
        c.link(dve.tensor_tensor(step[1][:], cut[1][:, CUTS:CUTS + 1], lo, ALU.subtract))
        c.link(dve.tensor_scalar(step[0][:], step[1][:], 1.0 / (CUTS + 1), None, ALU.mult))
        SIDE = c.n

        def settle(p, out_):
            return (lambda: dve.scalar_tensor_tensor(out=high[:], in0=ge[p][:], scalar=BIG, in1=cut[p][:],
                                                     op0=ALU.mult, op1=ALU.add),
                    lambda: dve.tensor_reduce(out_, high[:], AX_X, ALU.min))

        with dve.Fori(0, ROUNDS // 2, 1) as i:
            for p in range(2):
                if p == 0:
                    dve.wait_ge(s_thr, i * 6 + 1)
                else:
                    dve.wait_ge(s_thr, i * 6 + 4)
                dve.wait_ge(s_side, i * 6 + (SIDE + 3 * p))
                dve.tensor_scalar(cut[p][:, 0:CUTS], nth[:], step[p][:, 0:1], lo, ALU.mult, ALU.add).then_inc(s_thr, 1)
                dve.wait_ge(s_thr, i * 6 + (3 * p + 2))
                for n in range(CUTS):
                    dve.tensor_scalar(junk[:, n, :], sc[:], cut[p][:, n:n + 1], 0.0, ALU.is_ge, ALU.add,
                                      accum_out=cnt[:, n:n + 1]).then_inc(s_count, 1)
                add, least = settle(1 - p, cut[p][:, CUTS:CUTS + 1])
                add().then_inc(s_side, 1)
                dve.tensor_scalar(step[1 - p][:], step[p][:], 1.0 / (CUTS + 1), None, ALU.mult).then_inc(s_side, 1)
                dve.wait_ge(s_side, i * 6 + (SIDE + 3 * p + 1))
                least().then_inc(s_side, 1)
                dve.wait_ge(s_tot, i * 2 + (p + 1))
                dve.tensor_scalar(ge[p][:, 0:CUTS], tot_ps[:, 0:CUTS], float(CAP), 0.0, ALU.is_ge, ALU.add,
                                  accum_out=passes[:]).then_inc(s_thr, 1)
                dve.wait_ge(s_thr, i * 6 + (3 * p + 3))
                dve.scalar_tensor_tensor(out=lo, in0=passes[:], scalar=step[p][:, 0:1], in1=lo,
                                         op0=ALU.mult, op1=ALU.add).then_inc(s_thr, 1)
        dve.wait_ge(s_thr, 3 * ROUNDS + 1)
        dve.wait_ge(s_side, 3 * ROUNDS + SIDE)
        dve.wait_ge(s_count, CUTS * ROUNDS)
        c = Chain(dve, s_found)
        add, least = settle(1, hi)
        dve.wait_ge(s_e, SEL_CONSTS)
        c.link(add())
        c.link(least())
        c.link(dve.tensor_tensor(by_pair[:], pair[:].unsqueeze(2).to_broadcast([P, EP, 2]),
                                 lo_hi[:].unsqueeze(1).to_broadcast([P, EP, 2]), ALU.mult))
        dve.wait_ge(s_th, 1)
        dve.tensor_copy(th[:], tot_ps[0:TP, 0:2 * EP].rearrange("p (a i) -> p a i", i=2)).then_inc(s_th, 1)
        c = Chain(dve, d)
        dve.wait_ge(s_ts, 32)
        dve.wait_ge(s_th, 2)
        wide = [TP, EP, P]
        c.link(dve.tensor_tensor(above[:], ts[:], th[:, :, 1:2].to_broadcast(wide), ALU.is_ge))
        c.link(dve.tensor_tensor(tied[:], ts[:], th[:, :, 0:1].to_broadcast(wide), ALU.is_ge))
        c.link(dve.tensor_tensor(tied[:], tied[:], above[:], ALU.subtract))
        c.link(dve.tensor_reduce(n_above[:], above[:], AX_X, ALU.add))
        for a in range(EP):
            ins = dve.tensor_tensor_scan(place[:, a, :], ones[:], tied[:, a, :], 0.0, ALU.mult, ALU.add)
            ins.then_inc(s_tie, 1)
        dve.wait_ge(s_tie, EP)
        dve.wait_ge(s_left, 1)
        c.link(dve.tensor_scalar(left[:], small_ps[0:TP, 0:EP], float(CAP), None, ALU.subtract))
        c.link(dve.tensor_tensor(place[:], place[:], left[:].unsqueeze(2).to_broadcast(wide), ALU.add))
        c.link(dve.scalar_tensor_tensor(out=chosen[:], in0=place[:], scalar=0.0, in1=tied[:], op0=ALU.is_le, op1=ALU.mult))
        c.link(dve.tensor_tensor(chosen[:], chosen[:], above[:], ALU.add))
        for a in range(EP):
            dve.tensor_tensor_scan(count[:, a, :], ones[:], chosen[:, a, :], 0.0, ALU.mult, ALU.add).then_inc(s_sel, 1)
        dve.wait_ge(s_sel, EP)
        dve.wait_ge(s_start, 1)
        c.link(dve.tensor_copy(start[:], small_ps[0:TP, 0:EP]))
        c.link(dve.tensor_tensor(end[:], start[:], count[:, :, P - 1], ALU.add))
        c.link(dve.tensor_tensor(upto[:, :, 0:P], count[:], start[:].unsqueeze(2).to_broadcast(wide), ALU.add))
        c.link(dve.tensor_copy(upto[:, :, P:P + 1], tile_no[:].unsqueeze(1).to_broadcast([TP, EP, 1])))
        for a in range(EP):
            c.link(dve.tensor_scalar(under[:, a, :], slot[0:TP, :], end[:, a:a + 1], None, ALU.is_lt))
            dve.scalar_tensor_tensor(out=hot[:, a, :], in0=slot[0:TP, :], scalar=start[:, a:a + 1], in1=under[:, a, :],
                                     op0=ALU.is_ge, op1=ALU.mult).then_inc(s_hot, 1)
        for n in range(E * ST):
            dve.wait_ge(s_pick, n + 1)
            if n >= 2:
                dve.wait_ge(s_pos, n - 1)
            dve.tensor_scalar(cnt_junk[n % 2][:], g_ps[n % 4][:, 0:P], slot_of[:, n % ST:n % ST + 1], g_ps[n % 4][:, P:P + 1],
                              ALU.is_le, ALU.add, accum_out=pos[:, n:n + 1]).then_inc(s_pos, 1)
            if n == ST - 1:
                dve.wait_ge(s_pos, ST)
                dve.tensor_copy(sh["idx"][0][:], pos[:, 0:ST]).then_inc(sh["s_idx"], 1)
        dve.wait_ge(s_pos, E * ST)
        dve.tensor_copy(idx_all[:], pos[:]).then_inc(s_pos, 1)

    def tensor(pe):
        pe.wait_ge(s_e, SEARCH_CONSTS)
        pe.wait_ge(s_pm, 2)
        for i, part in enumerate((part_max, part_min)):
            mm = pe.transpose(small_ps[0:1, i * P:(i + 1) * P], part[:], w["ident"][:])
        mm.then_inc(s_top_t, 1)
        pe.wait_ge(s_top, 2)
        pe.matmul(small_ps[:, 0:E], ones_row[:], top[:], start=True, stop=True)
        for i in range(2):
            mm = pe.matmul(small_ps[:, E + i:E + i + 1], spread[:, i, :], ones_row[:, 0:1], start=True, stop=True)
        mm.then_inc(s_top_b, 1)
        with pe.Fori(0, ROUNDS, 1) as i:
            pe.wait_ge(s_count, i * CUTS + CUTS)
            pe.matmul(tot_ps[:, 0:CUTS], same[:], cnt[:], start=True, stop=True).then_inc(s_tot, 1)
        pe.wait_ge(s_found, 3)
        pe.matmul(tot_ps[0:TP, 0:2 * EP], parity[:].rearrange("p b t -> p (b t)"), by_pair[:].rearrange("p a i -> p (a i)"),
                  start=True, stop=True).then_inc(s_th, 1)
        pe.wait_ge(d, 4)
        pe.wait_ge(s_tie, EP)
        pe.matmul(small_ps[0:TP, 0:EP], group[:], n_above[:], start=True, stop=False)
        pe.matmul(small_ps[0:TP, 0:EP], before[:], place[:, :, P - 1], start=False, stop=True).then_inc(s_left, 1)
        pe.wait_ge(s_sel, EP)
        pe.matmul(small_ps[0:TP, 0:EP], before[:], count[:, :, P - 1], start=True, stop=True).then_inc(s_start, 1)
        for n in range(E * ST):
            e, st = n // ST, n % ST
            a, rows_ = e // 2, slice((e % 2) * T, (e % 2 + 1) * T)
            if st == 0 and e % 2 == 0:
                pe.wait_ge(s_hot, a + 1)
            if n >= 4:
                pe.wait_ge(s_pos, n - 3)
            pe.matmul(g_ps[n % 4][:, 0:P + 1], hot[rows_, a, st * P:(st + 1) * P], upto[rows_, a, :],
                      start=True, stop=True).then_inc(s_pick, 1)

    return {"sync": sync, "gpsimd": gpsimd, "vector": vector, "tensor": tensor}


def experts(nc, ctx, w, rows, g_f, w1_t, w3_t, w2_t, out, sh):
    CAP = out.shape[0] // E
    ST = CAP // P
    HT = max(1, CAP // 512)
    SPAN = CAP // HT
    TT = SPAN // P
    FT = F // P

    def sb(name, shape, dt=F32):
        return ctx.enter_context(nc.sbuf_tensor(name, shape, dt))

    def sem(name):
        return ctx.enter_context(nc.semaphore(name))

    gf_raw, gf, ones = sb("gf_raw", [P, 1]), sb("gf", [P, 1]), sb("ones3", [P, P])
    w1 = [sb(f"w1_{p}", [P, KD, F]) for p in range(2)]
    w3 = [sb(f"w3_{p}", [P, KD, F]) for p in range(2)]
    w2 = [sb(f"w2_{p}", [P, FT, D]) for p in range(2)]
    idx_add = [sb(f"idx_add{p}", [P, ST], U32) for p in range(2)]
    xg = [sb(f"xg{p}", [P, ST, ROW]) for p in range(2)]
    x_hi = [sb(f"x_hi{p}", [P, KD, CAP], F32R) for p in range(2)]
    x_lo = [sb(f"x_lo{p}", [P, KD, CAP], F32R) for p in range(2)]
    w_hi = [[sb(f"w{i}_hi{p}", [P, KD, F], F32R) for i in (1, 3)] for p in range(2)]
    w_lo = [[sb(f"w{i}_lo{p}", [P, KD, F], F32R) for i in (1, 3)] for p in range(2)]
    raw_s, top_e, e_s, sum_s, inv = sb("raw_s", [P, ST]), sb("top_e", [P, 1]), sb("e_s", [P, ST]), sb("sum_s", [P, 1]), sb("inv", [P, 1])
    weight = [sb(f"weight{p}", [P, ST]) for p in range(2)]
    act_h = [sb(f"act_h{i}", [P, SPAN]) for i in range(2)]
    hid = [sb(f"hid{i}", [P, FT, SPAN]) for i in range(HT)]
    y = [sb(f"y_{i}", [P, D]) for i in range(ST)]

    banks = sh["banks"]
    z_ps, t_ps, h1_ps, y_ps, h3_ps = banks[0], banks[1:3], banks[3:5], banks[5:7], banks[7]
    idx_all, neg_top, s_pos, idx, s_idx = sh["idx_all"], sh["neg_top"], sh["s_pos"], sh["idx"], sh["s_idx"]

    s_g, s_gf, s_one = sem("s_g3"), sem("s_gf"), sem("s_one3")
    s_w = [sem(f"s_w{p}") for p in range(2)]
    s_xg = [sem(f"s_xg{p}") for p in range(2)]
    w_hi_done, w_lo_done, x_hi_done = sem("w_hi_done"), sem("w_lo_done"), sem("x_hi_done")
    s_idx_add = sem("s_idx_add")
    t_done, t_out = sem("t_done"), sem("t_out")
    s_raw, s_es, z_done, s_inv, s_wt = sem("s_raw"), sem("s_es"), sem("z_done"), sem("s_inv"), sem("s_wt")
    h1_done, h3_done, silu_done, hid_done = sem("h1_done"), sem("h3_done"), sem("silu_done"), sem("hid_done")
    y_done, y_out = sem("y_done"), sem("y_out")
    s_add = [sem(f"s_add{i}") for i in range(ST)]
    passed = w["passed"]
    TRANS = KD * HT
    HID = HT * FT

    class Expert:

        def __init__(self, k, p):
            self.k, self.p = k + p // 2, p % 2

        def on(self, n):
            return Expert(self.k, self.p + n)

        @property
        def ok(self):
            return not isinstance(self.k, int) or 0 <= 2 * self.k + self.p < E

        def times(self, n, more=0):
            return self.k * (2 * n) + (self.p * n + more)

        def turn(self, n, more=0):
            return self.k * n + more

    def over(eng, step):
        for p in range(2):
            step(Expert(0, p))
        with eng.Fori(1, E // 2 - 1, 1) as k:
            for p in range(2):
                step(Expert(k, p))
        for p in range(2):
            step(Expert(E // 2 - 1, p))

    def sync(sp):
        sp.dma_start(gf_raw[:], g_f.rearrange("(a n) -> a n", a=1).to_broadcast([P, 1])).then_inc(s_g, 16)

        def load(e):
            if not e.ok:
                return
            wait(sp, y_done, e.times(ST, -ST))
            wait(sp, w_lo_done, e.times(2, -2))
            sp.sem_inc(passed, 1)
            i = e.times(1)
            for dst, src, n in ((w1, w1_t, F), (w3, w3_t, F), (w2, w2_t, D)):
                view = src.rearrange("e (k p) n -> p e k n", p=P)
                view = view[:, i] if isinstance(i, int) else view[:, bass.ds(i, 1)].rearrange("p e k n -> p (e k) n")
                sp.dma_start(dst[e.p][:], view).then_inc(s_w[e.p], 16)

        load(Expert(0, 0))
        load(Expert(0, 1))
        over(sp, lambda e: load(e.on(2)))
        for p in range(2):
            sp.wait_ge(s_w[p], 48 * E // 2)

    def gpsimd(pool):
        def gather(e):
            if not e.ok:
                return
            wait(pool, s_idx, e.times(1, 1))
            wait(pool, t_done, e.times(TRANS, -TRANS))
            wait(pool, s_raw, e.times(1, -1))
            pool.sem_inc(passed, 1)
            for st in range(ST):
                pool.indirect_dma_start(xg[e.p][:, st, :], None, rows[:, :],
                                        bass.IndirectOffsetOnAxis(ap=idx[e.p][:, st:st + 1], axis=0)).then_inc(s_xg[e.p], 16)

        def add(e):
            for st in range(ST):
                wait(pool, s_add[st], e.times(16))
            pool.wait_ge(s_idx_add, e.times(1, 1))
            for st in range(ST):
                pool.wait_ge(y_out, e.times(ST, st + 1))
                pool.sem_inc(passed, 1)
                pool.indirect_dma_start(out[:, :], bass.IndirectOffsetOnAxis(ap=idx_add[e.p][:, st:st + 1], axis=0),
                                        y[st][:], None, compute_op=ALU.add).then_inc(s_add[st], 16)

        def weights_lo(e):
            if e.ok:
                for i, w_raw in enumerate((w1, w3)):
                    pool.wait_ge(w_hi_done, e.times(2, i + 1))
                    wait(pool, h3_done, e.times(HID, -HID))
                    pool.tensor_tensor(w_lo[e.p][i][:], w_raw[e.p][:], w_hi[e.p][i][:].bitcast(F32), ALU.subtract).then_inc(w_lo_done, 1)

        pool.memset(ones[:], 1.0).then_inc(s_one, 1)
        weights_lo(Expert(0, 0))
        gather(Expert(0, 0))

        def step(e):
            gather(e.on(1))
            weights_lo(e.on(1))
            add(e)

        over(pool, step)
        for st in range(ST):
            pool.wait_ge(s_add[st], 16 * E)

    def scalar(act):
        act.wait_ge(s_g, 16)
        act.activation(gf[:], gf_raw[:], ACT.Tanh).then_inc(s_gf, 1)

        def weigh(e):
            if e.ok:
                act.wait_ge(s_raw, e.times(1, 1))
                wait(act, s_wt, e.times(1))
                act.activation(e_s[:], raw_s[:], ACT.Exp, bias=top_e[:, 0:1], accum_out=sum_s[:]).then_inc(s_es, 1)

        def silu(e, n):
            act.wait_ge(h1_done, e.times(HID, n + 1))
            wait(act, hid_done, e.times(HID, n - 1))
            act.activation(act_h[n % 2][:], h1_ps[n % 2][:, 0:SPAN], ACT.Silu).then_inc(silu_done, 1)

        def y_copy(e, st):
            act.wait_ge(y_done, e.times(ST, st + 1))
            act.wait_ge(s_wt, e.times(1, 1))
            wait(act, s_add[st], e.times(16))
            act.activation(y[st][:], y_ps[st % 2][:, 0:D], ACT.Copy, scale=weight[e.p][:, st:st + 1]).then_inc(y_out, 1)

        def weights_hi(e):
            if e.ok:
                act.wait_ge(s_w[e.p], e.turn(48, 48))
                wait(act, h3_done, e.times(HID, -HID))
                for i, w_raw in enumerate((w1, w3)):
                    act.activation(w_hi[e.p][i][:], w_raw[e.p][:], ACT.Copy).then_inc(w_hi_done, 1)

        def tokens_hi(e, i):
            if e.ok:
                k, h = i % KD, i // KD
                act.wait_ge(t_done, e.times(TRANS, i + 1))
                wait(act, h3_done, e.times(HID, -HID))
                act.activation(x_hi[e.p][:, k, h * SPAN:(h + 1) * SPAN], t_ps[i % 2][:, 0:SPAN], ACT.Copy).then_inc(x_hi_done, 1)

        weights_hi(Expert(0, 0))
        for i in range(TRANS):
            tokens_hi(Expert(0, 0), i)
        weigh(Expert(0, 0))

        def step(e):
            for n in range(HID):
                silu(e, n)
                if n == HID // 2:
                    weights_hi(e.on(1))
            for st in range(ST):
                y_copy(e, st)
                if st % 2 == 0:
                    tokens_hi(e.on(1), st // 2)
            weigh(e.on(1))

        over(act, step)

    def vector(dve):
        dve.wait_ge(s_gf, 1)

        def tiles_of(e):
            i = e.times(ST)
            return idx_all[:, i:i + ST] if isinstance(i, int) else idx_all[:, bass.ds(i, ST)]

        def list_of(e):
            if e.ok:
                wait(dve, s_xg[e.p], e.turn(16 * ST))
                dve.sem_inc(passed, 1)
                dve.tensor_copy(idx[e.p][:], tiles_of(e)).then_inc(s_idx, 1)

        def list_to_add(e):
            for st in range(ST):
                wait(dve, s_add[st], e.times(16, -16))
            dve.sem_inc(passed, 1)
            dve.tensor_copy(idx_add[e.p][:], tiles_of(e)).then_inc(s_idx_add, 1)

        def raw(e):
            if e.ok:
                i = e.times(1)
                dve.wait_ge(s_xg[e.p], e.turn(16 * ST, 16 * ST))
                wait(dve, s_es, e.times(1))
                dve.tensor_copy(top_e[:], neg_top[:, i:i + 1] if isinstance(i, int) else neg_top[:, bass.ds(i, 1)]).then_inc(s_inv, 1)
                col = xg[e.p][:, :, D + i:D + i + 1] if isinstance(i, int) else xg[e.p][:, :, bass.ds(i + D, 1)]
                dve.wait_ge(s_inv, e.times(2, 1))
                dve.tensor_copy(raw_s[:].unsqueeze(2), col).then_inc(s_raw, 1)

        def weights(e):
            if e.ok:
                dve.wait_ge(z_done, e.times(1, 1))
                dve.reciprocal(inv[:], z_ps[:, 0:1]).then_inc(s_inv, 1)
                dve.wait_ge(s_inv, e.times(2, 2))
                wait(dve, y_out, e.times(ST, -ST))
                dve.tensor_scalar(weight[e.p][:], e_s[:], inv[:, 0:1], gf[:, 0:1], ALU.mult, ALU.mult).then_inc(s_wt, 1)

        def tokens_lo(e, i):
            if e.ok:
                k, h = i % KD, i // KD
                dve.wait_ge(x_hi_done, e.times(TRANS, i + 1))
                wait(dve, h3_done, e.times(HID, -HID))
                cols = slice(h * SPAN, (h + 1) * SPAN)
                dve.tensor_tensor(x_lo[e.p][:, k, cols], t_ps[i % 2][:, 0:SPAN], x_hi[e.p][:, k, cols].bitcast(F32),
                                  ALU.subtract).then_inc(t_out, 1)

        def gate(e, n):
            dve.wait_ge(h3_done, e.times(HID, n + 1))
            dve.wait_ge(silu_done, e.times(HID, n + 1))
            if n % FT == 0:
                wait(dve, y_done, e.times(ST, (n // FT + 1) * TT - ST))
            dve.tensor_tensor(hid[n // FT][:, n % FT, :], act_h[n % 2][:], h3_ps[:, 0:SPAN], ALU.mult).then_inc(hid_done, 1)

        dve.wait_ge(s_pos, E * ST + 1)
        raw(Expert(0, 0))
        for i in range(TRANS):
            tokens_lo(Expert(0, 0), i)

        def step(e):
            list_of(e.on(1))
            for n in range(HID):
                gate(e, n)
                if n == 1:
                    weights(e)
            list_to_add(e)
            raw(e.on(1))
            for i in range(TRANS):
                tokens_lo(e.on(1), i)

        over(dve, step)

    def tensor(pe):
        pe.wait_ge(s_one, 1)
        pe.wait_ge(s_pos, E * ST)

        def transposes(e, i):
            if e.ok:
                k, h = i % KD, i // KD
                if i == 0:
                    pe.wait_ge(s_xg[e.p], e.turn(16 * ST, 16 * ST))
                wait(pe, t_out, e.times(TRANS, i - 1))
                for t in range(TT):
                    mm = pe.transpose(t_ps[i % 2][:, t * P:(t + 1) * P], xg[e.p][:, h * TT + t, k * P:(k + 1) * P], w["ident"][:])
                mm.then_inc(t_done, 1)

        def total(e):
            if e.ok:
                pe.wait_ge(s_es, e.times(1, 1))
                wait(pe, s_wt, e.times(1))
                pe.matmul(z_ps[:, 0:1], ones[:], sum_s[:], start=True, stop=True).then_inc(z_done, 1)

        def products(ps, e, i, f, h):
            passes = [(w_, x_, k) for k in range(KD) for w_, x_ in ((w_hi, x_hi), (w_hi, x_lo), (w_lo, x_hi))]
            for n, (w_, x_, k) in enumerate(passes):
                mm = pe.matmul(ps[:, 0:SPAN], w_[e.p][i][:, k, f], x_[e.p][:, k, h * SPAN:(h + 1) * SPAN],
                               start=(n == 0), stop=(n == len(passes) - 1))
            return mm

        def hidden(e, n):
            h, f = n // FT, slice((n % FT) * P, (n % FT + 1) * P)
            if n == 0:
                pe.wait_ge(w_lo_done, e.times(2, 2))
                pe.wait_ge(t_out, e.times(TRANS, TRANS))
            wait(pe, silu_done, e.times(HID, n - 1))
            products(h1_ps[n % 2], e, 0, f, h).then_inc(h1_done, 1)
            wait(pe, hid_done, e.times(HID, n))
            products(h3_ps, e, 1, f, h).then_inc(h3_done, 1)

        def down(e, st):
            h, t = st // TT, slice((st % TT) * P, (st % TT + 1) * P)
            pe.wait_ge(hid_done, e.times(HID, (h + 1) * FT))
            pe.wait_ge(s_w[e.p], e.turn(48, 48))
            wait(pe, y_out, e.times(ST, st - 1))
            for f in range(FT):
                mm = pe.matmul(y_ps[st % 2][:, 0:D], hid[h][:, f, t], w2[e.p][:, f, :], start=(f == 0), stop=(f == FT - 1))
            mm.then_inc(y_done, 1)

        first = Expert(0, 0)
        for i in range(TRANS):
            transposes(first, i)

        def step(e):
            for n in range(HID):
                hidden(e, n)
                if n == 1:
                    total(e)
            for st in range(ST):
                down(e, st)
                if st % 2 == 0:
                    transposes(e.on(1), st // 2)

        over(pe, step)

    return {"sync": sync, "gpsimd": gpsimd, "scalar": scalar, "vector": vector, "tensor": tensor}


def build(nc, x, ctx_t, mask, g_x, g_f, wq, bq, wk, bk, wv, bv, wg_t, w1_t, w3_t, w2_t, out):
    n_tok = x.shape[0]
    rows = nc.dram_tensor("rows_scratch", (n_tok, ROW), F32, kind="Internal").ap()
    scores_t = nc.dram_tensor("scores_scratch", (E, n_tok), F32, kind="Internal").ap()
    mask_bias = nc.dram_tensor("mask_scratch", (1, n_tok), BF16, kind="Internal").ap()
    with ExitStack() as whole:
        w = {"ident": whole.enter_context(nc.sbuf_tensor("ident", [P, P], F32)),
             "s_id": whole.enter_context(nc.semaphore("s_id")),
             "passed": whole.enter_context(nc.semaphore("passed"))}
        with ExitStack() as ctx:
            attention(nc, ctx, w, x, ctx_t, mask, g_x, wq, bq, wk, bk, wv, bv, wg_t, out, rows, scores_t, mask_bias)
        with ExitStack() as ctx:
            choose_and_run(nc, ctx, w, rows, scores_t, g_f, w1_t, w3_t, w2_t, out)


def choose_and_run(nc, ctx, w, rows, scores_t, g_f, w1_t, w3_t, w2_t, out):
    tiles = out.shape[0] // P
    share = {
        "banks": [ctx.enter_context(nc.psum_tensor(f"bank{i}", [P, 512], F32)) for i in range(8)],
        "idx_all": ctx.enter_context(nc.sbuf_tensor("idx_all", [P, tiles], U32)),
        "idx": [ctx.enter_context(nc.sbuf_tensor(f"idx{p}", [P, tiles // E], U32)) for p in range(2)],
        "neg_top": ctx.enter_context(nc.sbuf_tensor("neg_top", [P, E], F32)),
        "s_idx": ctx.enter_context(nc.semaphore("s_idx")),
        "s_pos": ctx.enter_context(nc.semaphore("s_pos")),
    }
    sel = select(nc, ctx, w, scores_t, share)
    run = experts(nc, ctx, w, rows, g_f, w1_t, w3_t, w2_t, out, share)
    with nc.Block() as block:

        @block.sync
        def _(sp):
            sel["sync"](sp)
            run["sync"](sp)

        @block.gpsimd
        def _(pool):
            sel["gpsimd"](pool)
            run["gpsimd"](pool)

        @block.scalar
        def _(act):
            run["scalar"](act)

        @block.vector
        def _(dve):
            sel["vector"](dve)
            run["vector"](dve)

        @block.tensor
        def _(pe):
            sel["tensor"](pe)
            run["tensor"](pe)


_HEAD_MAJOR = ("L0_xattn_Wq", "L0_xattn_Wk", "L0_xattn_bq", "L0_xattn_bk")


def lay_out(inputs):
    a = {k: np.asarray(v) for k, v in inputs.items()}
    n = a["x"].shape[0] * a["x"].shape[1]

    def columns(m):
        lead = m.shape[:-1]
        m = m.reshape(*lead, P // DH, KD, DH)
        return np.moveaxis(m, (-3, -2, -1), (-1, -3, -2)).reshape(*lead, D)

    return {
        "x": a["x"].reshape(n, D),
        "ctx_t": a["ctx_1024"].reshape(n, D).T,
        "mask": a["mask_BxS2_ik0"],
        "g_x": a["g_xattn"],
        "g_f": a["g_ffn"],
        "wq": columns(a["L0_xattn_Wq"]),
        "bq": columns(a["L0_xattn_bq"]).reshape(KD, P).T,
        "wk": columns(a["L0_xattn_Wk"]),
        "bk": columns(a["L0_xattn_bk"]).reshape(KD, P).T,
        "wv": a["L0_xattn_Wv"],
        "bv": a["L0_xattn_bv"],
        "wg_t": a["L0_ffn_Wg"].T,
        "w1_t": a["L0_ffn_W1"].transpose(0, 2, 1),
        "w3_t": a["L0_ffn_W3"].transpose(0, 2, 1),
        "w2_t": a["L0_ffn_W2"].transpose(0, 2, 1),
    }


def kernel(**inputs):
    import concourse.bacc as bacc
    from concourse.bass_utils import run_bass_kernel_spmd

    shape = inputs["x"].shape
    nc = bacc.Bacc("TRN2", target_bir_lowering=False, num_devices=1)
    arrays, args = {}, []
    for name, a in lay_out(inputs).items():
        a = np.ascontiguousarray(a)
        arrays[f"in_{name}"] = a
        args.append(nc.dram_tensor(f"in_{name}", a.shape, mybir.dt.from_np(a.dtype), kind="ExternalInput").ap())
    out = nc.dram_tensor("out", (shape[0] * shape[1], D), F32, kind="ExternalOutput").ap()
    build(nc, *args, out)
    r = run_bass_kernel_spmd(nc, [arrays], core_ids=[0])
    return r.results[0]["out"].reshape(shape)
```
